# Optimizing a Trainium2 kernel written in Bass

```python
import numpy as np
import jax
import jax.numpy as jnp

def _softmax(x, axis=-1):
    return jax.nn.softmax(x, axis=axis)

def _gelu(x):
    return jax.nn.gelu(x, approximate=True)

def _silu(x):
    return jax.nn.silu(x)

def _sigmoid(x):
    return jax.nn.sigmoid(x)

def _layernorm(x, axis=-1, eps=1e-05):
    m = jnp.mean(x, axis=axis, keepdims=True)
    v = jnp.var(x, axis=axis, keepdims=True)
    return (x - m) / jnp.sqrt(v + eps)

def _scatter_add(tgt, idx, src, axis=0):
    return tgt.at[idx].add(src)

def _segment_sum(src, seg, n):
    return jax.ops.segment_sum(src, seg, n)
kernel_name = 'mk_vit_tower_d2_tok_img1024_r4_8de3d7'

def setup_inputs(seed: int=0):
    np.random.seed(seed)
    _w = jnp.asarray

    def _rec_inputs():
        import jax
        import jax.numpy as jnp
        _rk = jax.random.key(seed)
        x = -0.000169711 + 1.00022 * jax.random.normal(jax.random.fold_in(_rk, 1), (128, 3, 128, 128), jnp.float32)
        return x
    x = _rec_inputs()

    def _L0_tok_setup():
        import jax, jax.numpy as jnp
        import numpy as np
        C = 256
        H8 = 8
        DH = C // H8
        PS = 14
        CS = 3
        IMG = 168
        B = 4

        def _ln(x, g, b):
            mu = jnp.mean(x, axis=-1, keepdims=True)
            xc = x - mu
            var = jnp.mean(xc * xc, axis=-1, keepdims=True)
            return xc * jax.lax.rsqrt(var + 1e-05) * g + b

        def _forward(pixel_values, conv_w, class_emb, la_ln_q_g, la_ln_q_b, la_wq, la_ln_kv_g, la_ln_kv_b, la_wkv, la_proj_w, la_proj_b, ga_ln_q_g, ga_ln_q_b, ga_wq, ga_ln_kv_g, ga_ln_kv_b, ga_wkv, ga_proj_w, ga_proj_b, mod_w, mod_b):
            b = pixel_values.shape[0]
            pe = jax.lax.conv_general_dilated(pixel_values, conv_w, (PS, PS), 'VALID', dimension_numbers=('NCHW', 'OIHW', 'NCHW'))
            HP = pe.shape[2]
            h = HP // CS
            hw, N = (h * h, CS * CS)
            scale = C ** (-0.5)
            grid = pe.reshape(b, C, h, CS, h, CS)
            red = grid.mean(axis=(3, 5)).reshape(b, C, hw).transpose(0, 2, 1)
            win = grid.transpose(0, 2, 4, 3, 5, 1).reshape(b, hw, N, C)
            q = _ln(red, la_ln_q_g, la_ln_q_b) @ la_wq
            q = q.reshape(b, hw, H8, DH).transpose(0, 2, 1, 3)
            kv = _ln(win, la_ln_kv_g, la_ln_kv_b) @ la_wkv
            kv = kv.reshape(b, hw, N, 2, H8, DH).transpose(3, 0, 4, 1, 2, 5)
            k_, v_ = (kv[0], kv[1])
            attn = jax.nn.softmax(jnp.einsum('bhnd,bhnkd->bhnk', q * scale, k_), axis=-1)
            agg = jnp.einsum('bhnk,bhnkd->bhnd', attn, v_)
            agg = agg.transpose(0, 2, 1, 3).reshape(b, hw, C)
            local_out = red + agg @ la_proj_w + la_proj_b
            cls = jnp.broadcast_to(class_emb, (b, 1, C))
            gq = (_ln(cls, ga_ln_q_g, ga_ln_q_b) @ ga_wq).reshape(b, H8, DH)
            gkv = _ln(local_out, ga_ln_kv_g, ga_ln_kv_b) @ ga_wkv
            gkv = gkv.reshape(b, hw, 2, H8, DH).transpose(2, 0, 3, 1, 4)
            gk, gv = (gkv[0], gkv[1])
            gattn = jax.nn.softmax(jnp.einsum('bhd,bhnd->bhn', gq * scale, gk), axis=-1)
            gagg = jnp.einsum('bhn,bhnd->bhd', gattn, gv).reshape(b, 1, C)
            cls_out = cls + gagg @ ga_proj_w + ga_proj_b
            patch_out = local_out @ mod_w + mod_b
            return jnp.concatenate([patch_out, cls_out], axis=1)
        key = jax.random.key(seed)
        ks = jax.random.split(key, 16)
        nrm = lambda k, shape: jax.random.normal(k, shape, jnp.float32) * 0.02
        return {'pixel_values': jax.random.normal(ks[0], (B, 3, IMG, IMG), jnp.float32), 'pixel_masks': jnp.ones((B, 1, IMG, IMG), jnp.float32), 'conv_w': nrm(ks[1], (C, 3, PS, PS)), 'class_emb': nrm(ks[2], (C,)), 'la_ln_q_g': jnp.ones((C,)), 'la_ln_q_b': jnp.zeros((C,)), 'la_wq': nrm(ks[3], (C, C)), 'la_ln_kv_g': jnp.ones((C,)), 'la_ln_kv_b': jnp.zeros((C,)), 'la_wkv': nrm(ks[4], (C, 2 * C)), 'la_proj_w': nrm(ks[5], (C, C)), 'la_proj_b': jnp.zeros((C,)), 'ga_ln_q_g': jnp.ones((C,)), 'ga_ln_q_b': jnp.zeros((C,)), 'ga_wq': nrm(ks[6], (C, C)), 'ga_ln_kv_g': jnp.ones((C,)), 'ga_ln_kv_b': jnp.zeros((C,)), 'ga_wkv': nrm(ks[7], (C, 2 * C)), 'ga_proj_w': nrm(ks[8], (C, C)), 'ga_proj_b': jnp.zeros((C,)), 'mod_w': nrm(ks[9], (C, C)), 'mod_b': jnp.zeros((C,))}
    _L0_tok_all = _L0_tok_setup()
    _L0_tok_in = {k: v for k, v in _L0_tok_all.items() if k in ('pixel_masks', 'conv_w', 'class_emb', 'la_ln_q_g', 'la_ln_q_b', 'la_wq', 'la_ln_kv_g', 'la_ln_kv_b', 'la_wkv', 'la_proj_w', 'la_proj_b', 'ga_ln_q_g', 'ga_ln_q_b', 'ga_wq', 'ga_ln_kv_g', 'ga_ln_kv_b', 'ga_wkv', 'ga_proj_w', 'ga_proj_b', 'mod_w', 'mod_b')}
    del _L0_tok_all

    def _L0_attn_setup():
        import jax, jax.numpy as jnp
        import numpy as np
        NEG = -1000000000.0

        def _attention(x, Wq, bq, Wk, bk, Wv, bv, Wo, num_heads=16):
            B, N, E = x.shape
            H = num_heads
            D = E // H
            scale = D ** (-0.5)
            q = (jnp.einsum('bne,fe->bnf', x, Wq) + bq).reshape(B, N, H, D).transpose(0, 2, 1, 3)
            k = (jnp.einsum('bne,fe->bnf', x, Wk) + bk).reshape(B, N, H, D).transpose(0, 2, 1, 3)
            v = (jnp.einsum('bne,fe->bnf', x, Wv) + bv).reshape(B, N, H, D).transpose(0, 2, 1, 3)
            scores = jnp.einsum('bhqd,bhkd->bhqk', q, k) * scale
            scores = scores.at[:, :, 0, -1].set(NEG)
            scores = scores.at[:, :, -1, 0].set(NEG)
            weights = jax.nn.softmax(scores, axis=-1)
            out = jnp.einsum('bhqk,bhkd->bhqd', weights, v)
            out = out.transpose(0, 2, 1, 3).reshape(B, N, E)
            return jnp.einsum('bne,fe->bnf', out, Wo)
        key = jax.random.key(seed)
        ks = jax.random.split(key, 8)
        B, N, E = (4, 512, 256)
        s = E ** (-0.5)
        return {'x': jax.random.normal(ks[0], (B, N, E), jnp.float32), 'Wq': jax.random.normal(ks[1], (E, E), jnp.float32) * s, 'bq': jax.random.normal(ks[2], (E,), jnp.float32) * 0.02, 'Wk': jax.random.normal(ks[3], (E, E), jnp.float32) * s, 'bk': jax.random.normal(ks[4], (E,), jnp.float32) * 0.02, 'Wv': jax.random.normal(ks[5], (E, E), jnp.float32) * s, 'bv': jax.random.normal(ks[6], (E,), jnp.float32) * 0.02, 'Wo': jax.random.normal(ks[7], (E, E), jnp.float32) * s}
    _L0_attn_all = _L0_attn_setup()
    _L0_attn_in = {k: v for k, v in _L0_attn_all.items() if k in ('Wq', 'bq', 'Wk', 'bk', 'Wv', 'bv', 'Wo')}
    del _L0_attn_all

    def _L0_ffn_setup():
        import jax, jax.numpy as jnp
        import numpy as np
        D_MODEL = 256
        D_FF = 1024
        N_EXPERTS = 8
        TOP_K = 2
        LN_EPS = 1e-06

        def _moe(x, router_w, w1, b1, w2, b2, gamma, beta):
            B, S, D = x.shape
            x_flat = x.reshape(-1, D)
            N = x_flat.shape[0]
            logits = x_flat @ router_w
            gate_vals, gate_idx = jax.lax.top_k(logits, TOP_K)
            gate_w = jax.nn.softmax(gate_vals, axis=-1)
            gates = jnp.zeros_like(logits).at[jnp.arange(N)[:, None], gate_idx].set(gate_w)
            h = jax.nn.gelu(jnp.einsum('nd,edf->enf', x_flat, w1) + b1[:, None, :], approximate=False)
            out = jnp.einsum('enf,efd->end', h, w2) + b2[:, None, :]
            res = x_flat[None, :, :] + out
            mu = jnp.mean(res, axis=-1, keepdims=True)
            var = jnp.mean(jnp.square(res - mu), axis=-1, keepdims=True)
            normed = (res - mu) * jax.lax.rsqrt(var + LN_EPS)
            expert_out = normed * gamma[:, None, :] + beta[:, None, :]
            y = jnp.einsum('end,ne->nd', expert_out, gates)
            return y.reshape(B, S, D)
        key = jax.random.key(seed)
        ks = jax.random.split(key, 8)
        x = jax.random.normal(ks[0], (2, 512, D_MODEL), dtype=jnp.float32)
        router_w = jax.random.normal(ks[1], (D_MODEL, N_EXPERTS), dtype=jnp.float32) * 0.02
        w1 = jax.random.normal(ks[2], (N_EXPERTS, D_MODEL, D_FF), dtype=jnp.float32) * 0.02
        b1 = jnp.zeros((N_EXPERTS, D_FF), dtype=jnp.float32)
        w2 = jax.random.normal(ks[3], (N_EXPERTS, D_FF, D_MODEL), dtype=jnp.float32) * 0.02
        b2 = jnp.zeros((N_EXPERTS, D_MODEL), dtype=jnp.float32)
        gamma = jnp.ones((N_EXPERTS, D_MODEL), dtype=jnp.float32)
        beta = jnp.zeros((N_EXPERTS, D_MODEL), dtype=jnp.float32)
        return {'x': x, 'router_w': router_w, 'w1': w1, 'b1': b1, 'w2': w2, 'b2': b2, 'gamma': gamma, 'beta': beta}
    _L0_ffn_all = _L0_ffn_setup()
    _L0_ffn_in = {k: v for k, v in _L0_ffn_all.items() if k in ('router_w', 'w1', 'b1', 'w2', 'b2', 'gamma', 'beta')}
    del _L0_ffn_all

    def _L1_attn_setup():
        import jax, jax.numpy as jnp
        import numpy as np
        B, T, D, H = (1, 1024, 256, 16)
        DK = D // H
        SCALE = 1.0 / float(np.sqrt(DK))
        NEG = -1000000000.0
        key = jax.random.key(seed)
        k1, k2, k3 = jax.random.split(key, 3)
        x = jax.random.normal(k1, (B, T, D), dtype=jnp.float32)
        Wqkv = jax.random.normal(k2, (3 * D, D), dtype=jnp.float32) * 0.02
        Wout = jax.random.normal(k3, (D, D), dtype=jnp.float32) * 0.02
        return {'x': x, 'Wqkv': Wqkv, 'Wout': Wout}
    _L1_attn_all = _L1_attn_setup()
    _L1_attn_in = {k: v for k, v in _L1_attn_all.items() if k in ('Wqkv', 'Wout')}
    del _L1_attn_all

    def _L1_ffn_setup():
        import jax, jax.numpy as jnp
        import numpy as np
        B, S, D = (8, 1024, 256)
        E, R, K = (6, 16, 2)
        key = jax.random.key(seed)
        ks = jax.random.split(key, 9)
        sc = 0.02
        return {'x': jax.random.normal(ks[0], (B, S, D), jnp.float32), 'base_W': jax.random.normal(ks[1], (D, D), jnp.float32) * sc, 'base_b': jax.random.normal(ks[2], (D,), jnp.float32) * sc, 'shared_A': jax.random.normal(ks[3], (R, D), jnp.float32) * sc, 'shared_B': jax.random.normal(ks[4], (D, R), jnp.float32) * sc, 'routed_A': jax.random.normal(ks[5], (E, R, D), jnp.float32) * sc, 'routed_B': jax.random.normal(ks[6], (E, D, R), jnp.float32) * sc, 'router_W': jax.random.normal(ks[7], (E, D), jnp.float32) * sc, 'router_b': jax.random.normal(ks[8], (E,), jnp.float32) * sc}
    _L1_ffn_all = _L1_ffn_setup()
    _L1_ffn_in = {k: v for k, v in _L1_ffn_all.items() if k in ('base_W', 'base_b', 'shared_A', 'shared_B', 'routed_A', 'routed_B', 'router_W', 'router_b')}
    del _L1_ffn_all
    return {'x': x, 'L0_tok_pixel_masks': _L0_tok_in['pixel_masks'], 'L0_tok_conv_w': _L0_tok_in['conv_w'], 'L0_tok_class_emb': _L0_tok_in['class_emb'], 'L0_tok_la_ln_q_g': _L0_tok_in['la_ln_q_g'], 'L0_tok_la_ln_q_b': _L0_tok_in['la_ln_q_b'], 'L0_tok_la_wq': _L0_tok_in['la_wq'], 'L0_tok_la_ln_kv_g': _L0_tok_in['la_ln_kv_g'], 'L0_tok_la_ln_kv_b': _L0_tok_in['la_ln_kv_b'], 'L0_tok_la_wkv': _L0_tok_in['la_wkv'], 'L0_tok_la_proj_w': _L0_tok_in['la_proj_w'], 'L0_tok_la_proj_b': _L0_tok_in['la_proj_b'], 'L0_tok_ga_ln_q_g': _L0_tok_in['ga_ln_q_g'], 'L0_tok_ga_ln_q_b': _L0_tok_in['ga_ln_q_b'], 'L0_tok_ga_wq': _L0_tok_in['ga_wq'], 'L0_tok_ga_ln_kv_g': _L0_tok_in['ga_ln_kv_g'], 'L0_tok_ga_ln_kv_b': _L0_tok_in['ga_ln_kv_b'], 'L0_tok_ga_wkv': _L0_tok_in['ga_wkv'], 'L0_tok_ga_proj_w': _L0_tok_in['ga_proj_w'], 'L0_tok_ga_proj_b': _L0_tok_in['ga_proj_b'], 'L0_tok_mod_w': _L0_tok_in['mod_w'], 'L0_tok_mod_b': _L0_tok_in['mod_b'], 'L0_attn_Wq': _L0_attn_in['Wq'], 'L0_attn_bq': _L0_attn_in['bq'], 'L0_attn_Wk': _L0_attn_in['Wk'], 'L0_attn_bk': _L0_attn_in['bk'], 'L0_attn_Wv': _L0_attn_in['Wv'], 'L0_attn_bv': _L0_attn_in['bv'], 'L0_attn_Wo': _L0_attn_in['Wo'], 'L0_ffn_router_w': _L0_ffn_in['router_w'], 'L0_ffn_w1': _L0_ffn_in['w1'], 'L0_ffn_b1': _L0_ffn_in['b1'], 'L0_ffn_w2': _L0_ffn_in['w2'], 'L0_ffn_b2': _L0_ffn_in['b2'], 'L0_ffn_gamma': _L0_ffn_in['gamma'], 'L0_ffn_beta': _L0_ffn_in['beta'], 'L1_attn_Wqkv': _L1_attn_in['Wqkv'], 'L1_attn_Wout': _L1_attn_in['Wout'], 'L1_ffn_base_W': _L1_ffn_in['base_W'], 'L1_ffn_base_b': _L1_ffn_in['base_b'], 'L1_ffn_shared_A': _L1_ffn_in['shared_A'], 'L1_ffn_shared_B': _L1_ffn_in['shared_B'], 'L1_ffn_routed_A': _L1_ffn_in['routed_A'], 'L1_ffn_routed_B': _L1_ffn_in['routed_B'], 'L1_ffn_router_W': _L1_ffn_in['router_W'], 'L1_ffn_router_b': _L1_ffn_in['router_b']}

def reference(x, L0_tok_pixel_masks, L0_tok_conv_w, L0_tok_class_emb, L0_tok_la_ln_q_g, L0_tok_la_ln_q_b, L0_tok_la_wq, L0_tok_la_ln_kv_g, L0_tok_la_ln_kv_b, L0_tok_la_wkv, L0_tok_la_proj_w, L0_tok_la_proj_b, L0_tok_ga_ln_q_g, L0_tok_ga_ln_q_b, L0_tok_ga_wq, L0_tok_ga_ln_kv_g, L0_tok_ga_ln_kv_b, L0_tok_ga_wkv, L0_tok_ga_proj_w, L0_tok_ga_proj_b, L0_tok_mod_w, L0_tok_mod_b, L0_attn_Wq, L0_attn_bq, L0_attn_Wk, L0_attn_bk, L0_attn_Wv, L0_attn_bv, L0_attn_Wo, L0_ffn_router_w, L0_ffn_w1, L0_ffn_b1, L0_ffn_w2, L0_ffn_b2, L0_ffn_gamma, L0_ffn_beta, L1_attn_Wqkv, L1_attn_Wout, L1_ffn_base_W, L1_ffn_base_b, L1_ffn_shared_A, L1_ffn_shared_B, L1_ffn_routed_A, L1_ffn_routed_B, L1_ffn_router_W, L1_ffn_router_b):
    import jax
    import jax.numpy as jnp

    def _L0_tok_ref(pixel_values, pixel_masks, conv_w, class_emb, la_ln_q_g, la_ln_q_b, la_wq, la_ln_kv_g, la_ln_kv_b, la_wkv, la_proj_w, la_proj_b, ga_ln_q_g, ga_ln_q_b, ga_wq, ga_ln_kv_g, ga_ln_kv_b, ga_wkv, ga_proj_w, ga_proj_b, mod_w, mod_b):
        import jax, jax.numpy as jnp
        import numpy as np
        C = 256
        H8 = 8
        DH = C // H8
        PS = 14
        CS = 3
        IMG = 168
        B = 4

        def _ln(x, g, b):
            mu = jnp.mean(x, axis=-1, keepdims=True)
            xc = x - mu
            var = jnp.mean(xc * xc, axis=-1, keepdims=True)
            return xc * jax.lax.rsqrt(var + 1e-05) * g + b

        def _forward(pixel_values, conv_w, class_emb, la_ln_q_g, la_ln_q_b, la_wq, la_ln_kv_g, la_ln_kv_b, la_wkv, la_proj_w, la_proj_b, ga_ln_q_g, ga_ln_q_b, ga_wq, ga_ln_kv_g, ga_ln_kv_b, ga_wkv, ga_proj_w, ga_proj_b, mod_w, mod_b):
            b = pixel_values.shape[0]
            pe = jax.lax.conv_general_dilated(pixel_values, conv_w, (PS, PS), 'VALID', dimension_numbers=('NCHW', 'OIHW', 'NCHW'))
            HP = pe.shape[2]
            h = HP // CS
            hw, N = (h * h, CS * CS)
            scale = C ** (-0.5)
            grid = pe.reshape(b, C, h, CS, h, CS)
            red = grid.mean(axis=(3, 5)).reshape(b, C, hw).transpose(0, 2, 1)
            win = grid.transpose(0, 2, 4, 3, 5, 1).reshape(b, hw, N, C)
            q = _ln(red, la_ln_q_g, la_ln_q_b) @ la_wq
            q = q.reshape(b, hw, H8, DH).transpose(0, 2, 1, 3)
            kv = _ln(win, la_ln_kv_g, la_ln_kv_b) @ la_wkv
            kv = kv.reshape(b, hw, N, 2, H8, DH).transpose(3, 0, 4, 1, 2, 5)
            k_, v_ = (kv[0], kv[1])
            attn = jax.nn.softmax(jnp.einsum('bhnd,bhnkd->bhnk', q * scale, k_), axis=-1)
            agg = jnp.einsum('bhnk,bhnkd->bhnd', attn, v_)
            agg = agg.transpose(0, 2, 1, 3).reshape(b, hw, C)
            local_out = red + agg @ la_proj_w + la_proj_b
            cls = jnp.broadcast_to(class_emb, (b, 1, C))
            gq = (_ln(cls, ga_ln_q_g, ga_ln_q_b) @ ga_wq).reshape(b, H8, DH)
            gkv = _ln(local_out, ga_ln_kv_g, ga_ln_kv_b) @ ga_wkv
            gkv = gkv.reshape(b, hw, 2, H8, DH).transpose(2, 0, 3, 1, 4)
            gk, gv = (gkv[0], gkv[1])
            gattn = jax.nn.softmax(jnp.einsum('bhd,bhnd->bhn', gq * scale, gk), axis=-1)
            gagg = jnp.einsum('bhn,bhnd->bhd', gattn, gv).reshape(b, 1, C)
            cls_out = cls + gagg @ ga_proj_w + ga_proj_b
            patch_out = local_out @ mod_w + mod_b
            return jnp.concatenate([patch_out, cls_out], axis=1)
        del pixel_masks
        return _forward(pixel_values, conv_w, class_emb, la_ln_q_g, la_ln_q_b, la_wq, la_ln_kv_g, la_ln_kv_b, la_wkv, la_proj_w, la_proj_b, ga_ln_q_g, ga_ln_q_b, ga_wq, ga_ln_kv_g, ga_ln_kv_b, ga_wkv, ga_proj_w, ga_proj_b, mod_w, mod_b)

    def _L0_attn_ref(x, Wq, bq, Wk, bk, Wv, bv, Wo):
        import jax, jax.numpy as jnp
        import numpy as np
        NEG = -1000000000.0

        def _attention(x, Wq, bq, Wk, bk, Wv, bv, Wo, num_heads=16):
            B, N, E = x.shape
            H = num_heads
            D = E // H
            scale = D ** (-0.5)
            q = (jnp.einsum('bne,fe->bnf', x, Wq) + bq).reshape(B, N, H, D).transpose(0, 2, 1, 3)
            k = (jnp.einsum('bne,fe->bnf', x, Wk) + bk).reshape(B, N, H, D).transpose(0, 2, 1, 3)
            v = (jnp.einsum('bne,fe->bnf', x, Wv) + bv).reshape(B, N, H, D).transpose(0, 2, 1, 3)
            scores = jnp.einsum('bhqd,bhkd->bhqk', q, k) * scale
            scores = scores.at[:, :, 0, -1].set(NEG)
            scores = scores.at[:, :, -1, 0].set(NEG)
            weights = jax.nn.softmax(scores, axis=-1)
            out = jnp.einsum('bhqk,bhkd->bhqd', weights, v)
            out = out.transpose(0, 2, 1, 3).reshape(B, N, E)
            return jnp.einsum('bne,fe->bnf', out, Wo)
        return _attention(x, Wq, bq, Wk, bk, Wv, bv, Wo, num_heads=16)

    def _L0_ffn_ref(x, router_w, w1, b1, w2, b2, gamma, beta):
        import jax, jax.numpy as jnp
        import numpy as np
        D_MODEL = 256
        D_FF = 1024
        N_EXPERTS = 8
        TOP_K = 2
        LN_EPS = 1e-06

        def _moe(x, router_w, w1, b1, w2, b2, gamma, beta):
            B, S, D = x.shape
            x_flat = x.reshape(-1, D)
            N = x_flat.shape[0]
            logits = x_flat @ router_w
            gate_vals, gate_idx = jax.lax.top_k(logits, TOP_K)
            gate_w = jax.nn.softmax(gate_vals, axis=-1)
            gates = jnp.zeros_like(logits).at[jnp.arange(N)[:, None], gate_idx].set(gate_w)
            h = jax.nn.gelu(jnp.einsum('nd,edf->enf', x_flat, w1) + b1[:, None, :], approximate=False)
            out = jnp.einsum('enf,efd->end', h, w2) + b2[:, None, :]
            res = x_flat[None, :, :] + out
            mu = jnp.mean(res, axis=-1, keepdims=True)
            var = jnp.mean(jnp.square(res - mu), axis=-1, keepdims=True)
            normed = (res - mu) * jax.lax.rsqrt(var + LN_EPS)
            expert_out = normed * gamma[:, None, :] + beta[:, None, :]
            y = jnp.einsum('end,ne->nd', expert_out, gates)
            return y.reshape(B, S, D)
        return _moe(x, router_w, w1, b1, w2, b2, gamma, beta)

    def _L1_attn_ref(x, Wqkv, Wout):
        import jax, jax.numpy as jnp
        import numpy as np
        B, T, D, H = (1, 1024, 256, 16)
        DK = D // H
        SCALE = 1.0 / float(np.sqrt(DK))
        NEG = -1000000000.0
        b, t, d = x.shape
        qkv = jnp.einsum('btd,ed->bte', x, Wqkv)
        qkv = qkv.reshape(b, t, 3, H, DK).transpose(2, 0, 3, 1, 4)
        q, k, v = (qkv[0], qkv[1], qkv[2])
        scores = jnp.einsum('bhtd,bhsd->bhts', q, k) * SCALE
        scores = jnp.clip(scores, -10.0, 10.0)
        mask = jnp.triu(jnp.full((t, t), NEG, dtype=scores.dtype), k=1)
        scores = scores + mask[None, None, :, :]
        attn = jax.nn.softmax(scores, axis=-1)
        out = jnp.einsum('bhts,bhsd->bhtd', attn, v)
        out = out.transpose(0, 2, 1, 3).reshape(b, t, d)
        return jnp.einsum('btd,ed->bte', out, Wout)

    def _L1_ffn_ref(x, base_W, base_b, shared_A, shared_B, routed_A, routed_B, router_W, router_b):
        import jax, jax.numpy as jnp
        import numpy as np
        B, S, D = (8, 1024, 256)
        E, R, K = (6, 16, 2)
        base_out = jax.lax.stop_gradient(jnp.einsum('bsi,oi->bso', x, base_W) + base_b)
        shared_out = jnp.einsum('bsr,or->bso', jnp.einsum('bsi,ri->bsr', x, shared_A), shared_B)
        logits = jnp.einsum('bsi,ei->bse', x, router_W) + router_b
        gate = jax.nn.softmax(logits, axis=-1)
        topk_w, topk_i = jax.lax.top_k(gate, K)
        sparse_w = jnp.sum(jax.nn.one_hot(topk_i, E, dtype=gate.dtype) * topk_w[..., None], axis=-2)
        sparse_w = sparse_w / (jnp.sum(sparse_w, axis=-1, keepdims=True) + 1e-06)
        h = jnp.einsum('bsi,eri->bser', x, routed_A)
        routed_outs = jnp.einsum('bser,eor->bseo', h, routed_B)
        routed_out = jnp.einsum('bseo,bse->bso', routed_outs, sparse_w)
        return base_out + shared_out + routed_out
    h = _L0_tok_ref(x, L0_tok_pixel_masks, L0_tok_conv_w, L0_tok_class_emb, L0_tok_la_ln_q_g, L0_tok_la_ln_q_b, L0_tok_la_wq, L0_tok_la_ln_kv_g, L0_tok_la_ln_kv_b, L0_tok_la_wkv, L0_tok_la_proj_w, L0_tok_la_proj_b, L0_tok_ga_ln_q_g, L0_tok_ga_ln_q_b, L0_tok_ga_wq, L0_tok_ga_ln_kv_g, L0_tok_ga_ln_kv_b, L0_tok_ga_wkv, L0_tok_ga_proj_w, L0_tok_ga_proj_b, L0_tok_mod_w, L0_tok_mod_b)
    h = h + _L0_attn_ref(_layernorm(h, axis=-1), L0_attn_Wq, L0_attn_bq, L0_attn_Wk, L0_attn_bk, L0_attn_Wv, L0_attn_bv, L0_attn_Wo)
    h = h + _L0_ffn_ref(_layernorm(h, axis=-1), L0_ffn_router_w, L0_ffn_w1, L0_ffn_b1, L0_ffn_w2, L0_ffn_b2, L0_ffn_gamma, L0_ffn_beta)
    h = h + _L1_attn_ref(_layernorm(h, axis=-1), L1_attn_Wqkv, L1_attn_Wout)
    h = h + _L1_ffn_ref(_layernorm(h, axis=-1), L1_ffn_base_W, L1_ffn_base_b, L1_ffn_shared_A, L1_ffn_shared_B, L1_ffn_routed_A, L1_ffn_routed_B, L1_ffn_router_W, L1_ffn_router_b)
    return h

_drawn_inputs = setup_inputs


def setup_inputs(seed=0):
    import zlib

    import numpy as np

    out = dict(_drawn_inputs(seed))
    spreads = {'L0_tok_pixel_masks': (1.0, 0.2),
     'L0_tok_la_ln_q_g': (1.0, 0.6),
     'L0_tok_la_ln_q_b': (0.0, 0.8),
     'L0_tok_la_ln_kv_g': (1.0, 0.6),
     'L0_tok_la_ln_kv_b': (0.0, 0.1),
     'L0_tok_la_proj_b': (0.0, 0.1),
     'L0_tok_ga_ln_q_g': (1.0, 0.6),
     'L0_tok_ga_ln_q_b': (0.0, 0.8),
     'L0_tok_ga_ln_kv_g': (1.0, 0.2),
     'L0_tok_ga_ln_kv_b': (0.0, 0.1),
     'L0_tok_ga_proj_b': (0.0, 0.1),
     'L0_tok_mod_b': (0.0, 0.1),
     'L0_ffn_b1': (0.0, 0.553),
     'L0_ffn_b2': (0.0, 0.1),
     'L0_ffn_gamma': (1.0, 0.2),
     'L0_ffn_beta': (0.0, 0.1)}
    factors = {'L0_tok_la_wq': 8.0,
     'L0_tok_ga_wq': 8.0,
     'L0_attn_bq': 5.157,
     'L0_attn_bk': 8.0,
     'L1_ffn_base_b': 5.156,
     'L1_ffn_shared_A': 5.244,
     'L1_ffn_shared_B': 4.596,
     'L1_ffn_routed_A': 5.67,
     'L1_ffn_routed_B': 5.323,
     'L1_ffn_router_W': 5.388,
     'L1_ffn_router_b': 8.0}
    for name, (base, spread) in spreads.items():
        noise = np.random.default_rng([zlib.crc32(name.encode()), seed]).standard_normal(out[name].shape)
        drawn = base * np.exp(spread * noise) if base else spread * noise
        out[name] = jnp.asarray(drawn.astype(out[name].dtype))
    for name, factor in factors.items():
        out[name] = (out[name] * factor).astype(out[name].dtype)
    return out
```

```python
from contextlib import ExitStack

import concourse.bass as bass
from concourse import mybir

ALU = mybir.AluOpType
ACT = mybir.ActivationFunctionType
AX = mybir.AxisListType.X
F32 = mybir.dt.float32
F32R = mybir.dt.float32r
U32 = mybir.dt.uint32

P = 128
C = 256
CH = C // P
NW = 9
NP = 9
KC = 5
KREST = 588 - 4 * P
GRP = 3
H8, DH8 = 8, 32
H16, D16 = 16, 16
T = NW + 1
QKV = 3 * C
E, FF = 8, 1024
FC = FF // P
BT = 2
NB = T // BT
BW = BT * P
PIECES = 8
E6, R16 = 6, 16
LOW = (E6 + 1) * R16
ZW = LOW + E6
NEG4 = -4.0e9
VECS = ["la_ln_q_g", "la_ln_q_b", "la_ln_kv_g", "la_ln_kv_b", "ga_ln_q_g", "ga_ln_q_b", "ga_ln_kv_g", "ga_ln_kv_b"]
LAQ, LAKV, GAQ, GAKV = 0, 4, 8, 12
ROWS = ["la_proj_b", "mod_b", "ga_proj_b", "class_emb"]


def earlier(k, cycle, slots=2):
    return slots if k >= slots else k + cycle - (k + ((cycle - 1 - k) // slots) * slots)


def vision_tower(nc, d, out):
    ctx = ExitStack()
    with ctx:
        def sb(name, shape, dt=F32, scope=None):
            return (scope or ctx).enter_context(nc.sbuf_tensor(name, shape, dt))

        sems = {}

        def sem(name):
            if name not in sems:
                sems[name] = ctx.enter_context(nc.semaphore(name))
            return sems[name]

        pair = [ctx.enter_context(nc.psum_tensor(f"banks{2 * i}", [P, 2, 512], F32)) for i in range(4)]

        def bank(i, a=0, b=C):
            return pair[i // 2][:, i % 2, a:b]

        h = sb("h", [P, T * C])
        ident = sb("ident", [P, P])
        iota = sb("iota", [P, 8])
        stats = sb("stats", [P, 10, 6])
        mv = sb("mv", [P, 10, 2])
        veps = sb("veps", [P, 10])
        mhalf = sb("mhalf", [P, 10])
        spare = sb("spare", [P, 2])
        rstd = sb("rstd", [P, 10])
        nmr = sb("nmr", [P, 10])
        w1raw = [sb(f"w1raw{i}", [P, CH * FF]) for i in range(2)]
        w2raw = [sb(f"w2raw{i}", [P, FC * C]) for i in range(2)]

        def h_at(t, n=1):
            return h[:, t * C:(t + n) * C]

        tok = ExitStack()
        wc_raw = sb("wc_raw", [P, KC, C], F32, tok)
        wc_hi = sb("wc_hi", [P, KC, C], F32R, tok)
        wc_lo = sb("wc_lo", [P, KC, C], F32R, tok)
        wkv_raw = sb("wkv_raw", [P, CH, 2 * C], F32, tok)
        wkv_hi = sb("wkv_hi", [P, CH, 2 * C], F32R, tok)
        wkv_lo = sb("wkv_lo", [P, CH, 2 * C], F32R, tok)
        kvb = sb("kvb", [P, 2 * C], F32R, tok)
        kvb_f = sb("kvb_f", [P, 2 * C], F32, tok)
        ones_r = sb("ones_r", [P, P], F32R, tok)
        xraw = sb("xraw", [P, NP, KC, P], F32, tok)
        x_hi = sb("x_hi", [P, GRP, KC * P], F32R, tok)
        x_lo = sb("x_lo", [P, GRP, KC * P], F32R, tok)
        pe_sb = sb("pe_sb", [P, NP * C], F32, tok)
        xn = sb("xn", [P, NP * C], F32, tok)
        xg_hi = sb("xg_hi", [P, 2, C], F32R, tok)
        xg_lo = sb("xg_lo", [P, 2, C], F32R, tok)
        kv_sb = sb("kv_sb", [P, NP, 2 * C], F32, tok)
        prod = sb("prod", [P, NP * C], F32, tok)
        red = sb("red", [P, C], F32, tok)
        redn = sb("redn", [P, C], F32, tok)
        red_sum = sb("red_sum", [P, C], F32, tok)
        redT = sb("redT", [P, C], F32, tok)
        q_sb = sb("q_sb", [P, C], F32, tok)
        sc = sb("sc", [P, NP * H8], F32, tok)
        smax = sb("smax", [P, H8], F32, tok)
        pr = sb("pr", [P, NP * H8], F32, tok)
        den = sb("den", [P, H8], F32, tok)
        rden = sb("rden", [P, H8], F32, tok)
        attn = sb("attn", [P, NP * H8], F32, tok)
        agg = sb("agg", [P, C], F32, tok)
        aggT = sb("aggT", [P, C], F32, tok)
        local = sb("local", [P, NW * C], F32, tok)
        w_q = sb("w_q", [P, CH, C], F32, tok)
        w_proj = sb("w_proj", [P, CH, C], F32, tok)
        w_mod = sb("w_mod", [P, CH, C], F32, tok)
        w_gq = sb("w_gq", [P, CH, C], F32, tok)
        w_gkv = sb("w_gkv", [P, CH, 2 * C], F32, tok)
        w_gproj = sb("w_gproj", [P, CH, C], F32, tok)
        vecs = sb("vecs", [P, 2 * len(VECS)], F32, tok)
        rows = sb("rows", [P, len(ROWS) * C], F32, tok)
        localT = sb("localT", [P, 2, C], F32, tok)
        gnT = sb("gnT", [P, 2, C], F32, tok)
        tok.close()

        att = ExitStack()
        a_w = [sb(f"a_w{i}", [P, CH, QKV], F32, att) for i in range(2)]
        a_wo = [sb(f"a_wo{i}", [P, CH, C], F32, att) for i in range(2)]
        a_bias = sb("a_bias", [P, QKV], F32, att)
        a_xn = sb("a_xn", [P, 2, C], F32, att)
        a_xT = sb("a_xT", [P, 2, C], F32, att)
        a_qkv = sb("a_qkv", [P, T, QKV], F32, att)
        a_prod = sb("a_prod", [P, 2, T * C], F32, att)
        a_s = sb("a_s", [P, T * T * H16], F32, att)
        a_p = sb("a_p", [P, T * T * H16], F32, att)
        a_max = sb("a_max", [P, T * H16], F32, att)
        a_den = sb("a_den", [P, T * H16], F32, att)
        a_rden = sb("a_rden", [P, T * H16], F32, att)
        a_o = sb("a_o", [P, T * C], F32, att)
        a_oT = sb("a_oT", [P, 2, C], F32, att)
        att.close()

        moe = ExitStack()
        w1_hi = [sb(f"w1_hi{i}", [P, CH * FF], F32R, moe) for i in range(2)]
        w1_lo = [sb(f"w1_lo{i}", [P, CH * FF], F32R, moe) for i in range(2)]
        w2_hi = [sb(f"w2_hi{i}", [P, FC * C], F32R, moe) for i in range(2)]
        w2_lo = [sb(f"w2_lo{i}", [P, FC * C], F32R, moe) for i in range(2)]
        x2 = sb("x2", [P, T * C], F32, moe)
        x2T = sb("x2T", [P, T, C], F32, moe)
        xT_hi = sb("xT_hi", [P, CH, T * P], F32R, moe)
        xT_lo = sb("xT_lo", [P, CH, T * P], F32R, moe)
        gel = sb("gel", [P, 2, BW], F32, moe)
        hid_hi = sb("hid_hi", [P, FC, BW], F32R, moe)
        hid_lo = sb("hid_lo", [P, FC, BW], F32R, moe)
        b1 = [sb(f"b1_{i}", [P, FC], F32, moe) for i in range(2)]
        b2 = [sb(f"b2_{i}", [P, C], F32, moe) for i in range(2)]
        gam = [sb(f"gam{i}", [P, C], F32, moe) for i in range(2)]
        beta = sb("beta", [E, C], F32, moe)
        w_rt = sb("w_rt", [P, CH, E], F32, moe)
        lg = sb("lg", [P, T, E], F32, moe)
        top = sb("top", [P, T, 8], F32, moe)
        topi = sb("topi", [P, T, 8], U32, moe)
        topf = sb("topf", [P, T, 2], F32, moe)
        tw = sb("tw", [P, T, 2], F32, moe)
        te = sb("te", [P, T, 2], F32, moe)
        tsum = sb("tsum", [P, T], F32, moe)
        trec = sb("trec", [P, T], F32, moe)
        hot = sb("hot", [P, 2, T, E], F32, moe)
        gates = sb("gates", [P, T, E], F32, moe)
        gat_e = sb("gat_e", [P, E * T], F32, moe)
        gT = sb("gT", [E, T, P], F32, moe)
        xb = sb("xb", [P, BT * C], F32, moe)
        res = sb("res", [P, BT * C], F32, moe)
        nr = sb("nr", [P, 2, BT * C], F32, moe)
        gm = sb("gm", [P, BT * C], F32, moe)
        bst = sb("bst", [P, BT, 6], F32, moe)
        bmv = sb("bmv", [P, BT, 2], F32, moe)
        bve = sb("bve", [P, BT], F32, moe)
        brs = sb("brs", [P, BT], F32, moe)
        bsc = sb("bsc", [P, BT], F32, moe)
        moe.close()

        lora = ExitStack()
        z_w = sb("z_w", [P, CH, ZW], F32, lora)
        z_b = sb("z_b", [LOW, C], F32, lora)
        z_base = sb("z_base", [P, CH, C], F32, lora)
        z_rows = sb("z_rows", [P, C + E6], F32, lora)
        z_xn = sb("z_xn", [P, 2, C], F32, lora)
        z_xT = sb("z_xT", [P, T, C], F32, lora)
        z = sb("z", [P, T, ZW], F32, lora)
        z_s = sb("z_s", [P, T, LOW], F32, lora)
        z_l = sb("z_l", [P, T, E6], F32, lora)
        z_max = sb("z_max", [P, T], F32, lora)
        z_p = sb("z_p", [P, T, E6], F32, lora)
        z_g = sb("z_g", [P, T, 8], F32, lora)
        z_top = sb("z_top", [P, T, 8], F32, lora)
        z_topi = sb("z_topi", [P, T, 8], U32, lora)
        z_topf = sb("z_topf", [P, T, 2], F32, lora)
        z_tw = sb("z_tw", [P, T, 2], F32, lora)
        z_sum = sb("z_sum", [P, T], F32, lora)
        z_rec = sb("z_rec", [P, T], F32, lora)
        z_hot = sb("z_hot", [P, 2, T, E6], F32, lora)
        z_sw = sb("z_sw", [P, T, E6], F32, lora)
        z_sT = sb("z_sT", [P, 2, P], F32, lora)
        z_o = sb("z_o", [P, T, C], F32, lora)
        lora.close()

        block = ctx.enter_context(nc.Block())

        def phase(eng, n):
            eng.drain().then_inc(sem("phase_ended"), 1)
            eng.wait_ge(sem("phase_ended"), 5 * n)

        def mm3(pe, dst, a, b, start, stop):
            pe.matmul(dst, a[0], b[0], start=start, stop=False)
            pe.matmul(dst, a[0], b[1], start=False, stop=False)
            return pe.matmul(dst, a[1], b[0], start=False, stop=stop)

        def mm_rows(pe, dst, aT, w, a, b):
            for c in range(CH):
                last = pe.matmul(dst, aT[:, c * P:(c + 1) * P], w[:, c, a:b], start=(c == 0), stop=(c == CH - 1))
            return last

        def turn(pe, dst, src):
            for c in range(CH):
                last = pe.transpose(dst[:, c * P:(c + 1) * P], src[:, c * P:(c + 1) * P], ident[:, :])
            return last

        class Chain:

            def __init__(self, eng, name):
                self.eng, self.sem, self.n = eng, sem(name), 0

            def __call__(self, ins):
                ins.then_inc(self.sem, 1)
                self.n += 1
                self.eng.wait_ge(self.sem, self.n)

        LN = ["class", "attention 0", "experts", "attention 1", "low rank"]

        def inverse_std(pool, n):
            pool.wait_ge(sem("var_made"), n + 1)
            pool.tensor_tensor(rstd[:, :], veps[:, :], mhalf[:, :], ALU.pow).then_inc(sem("rstd_made"), 1)

        def shift_of(dve, n):
            dve.wait_ge(sem("rstd_made"), n + 1)
            dve.scalar_tensor_tensor(out=nmr[:, :], in0=mv[:, :, 0], scalar=-1.0, in1=rstd[:, :],
                                     op0=ALU.mult, op1=ALU.mult).then_inc(sem("nmr_made"), 1)

        def layer_stats(dve, which, src):
            n = NW + LN.index(which)
            for t in range(T):
                dve.bn_stats(stats[:, t, :], src(t)).then_inc(sem("stats_made"), 1)
                if t:
                    dve.bn_aggr(mv[:, t - 1, :], stats[:, t - 1, :]).then_inc(sem("aggr_made"), 1)
                dve.wait_ge(sem("stats_made"), T * n + t + 1)
            dve.tensor_copy(spare[:, 0:1], spare[:, 1:2]).then_inc(sem("spacer"), 1)
            dve.bn_aggr(mv[:, T - 1, :], stats[:, T - 1, :]).then_inc(sem("aggr_made"), 1)
            dve.wait_ge(sem("aggr_made"), T * (n + 1))
            dve.tensor_scalar(veps[:, :], mv[:, :, 1], 1e-5, None, ALU.add).then_inc(sem("var_made"), 1)
            shift_of(dve, n)

        def normalized_scales(act, which):
            act.wait_ge(sem("nmr_made"), NW + LN.index(which) + 1)

        def normalize(act, dst, src, t):
            return act.activation(dst, src, ACT.Identity, scale=rstd[:, t:t + 1], bias=nmr[:, t:t + 1])

        def affine(act, dst, src, v, name):
            for c in range(CH):
                act.activation(dst[:, c * P:(c + 1) * P], src[:, c * P:(c + 1) * P], ACT.Identity,
                               scale=vecs[:, v + c:v + c + 1], bias=vecs[:, v + 2 + c:v + 3 + c]).then_inc(sem(name), 1)

        def load_x(sp, n, g):
            if not isinstance(n, int) or n > 0:
                sp.wait_ge(sem("x_lo_made"), NP * (n - 1) + GRP * g + GRP)
            a, b = GRP * g, GRP * g + GRP
            sp.dma_start(xraw[:, a:b, 0:4, :], d["x_main"][bass.ds(n * P, P), a * 512:b * 512]
                         .rearrange("p (k c b) -> p k c b", k=GRP, c=4)).then_inc(sem(f"x_loaded{g}"), 16)
            sp.dma_start(xraw[0:KREST, a:b, 4, :], d["x_rest"][bass.ds(n * KREST, KREST), a * P:b * P]
                         .rearrange("p (k b) -> p k b", k=GRP)).then_inc(sem(f"x_loaded{g}"), 16)

        def split_x_hi(act, n, k):
            act.wait_ge(sem(f"x_loaded{k // GRP}"), 32 * (n + 1))
            if not isinstance(n, int) or NP * n + k >= GRP:
                act.wait_ge(sem("conv_done"), NP * n + k - GRP + 1)
            act.activation(x_hi[:, k % GRP, :], xraw[:, k].rearrange("p c b -> p (c b)"), ACT.Copy)\
               .then_inc(sem("x_hi_made"), 1)

        def split_x_lo(pool, n, k):
            if not isinstance(n, int) or NP * n + k >= GRP:
                pool.wait_ge(sem("conv_done"), NP * n + k - GRP + 1)
            pool.wait_ge(sem("x_hi_made"), NP * n + k + 1)
            pool.tensor_tensor(x_lo[:, k % GRP, :], xraw[:, k].rearrange("p c b -> p (c b)"), x_hi[:, k % GRP, :],
                               ALU.subtract).then_inc(sem("x_lo_made"), 1)

        def conv(pe, n, k):
            if not isinstance(n, int) or n > 0 or k >= 2:
                pe.wait_ge(sem("pe_copied"), NP * n + k + 1 - earlier(k, NP))
            pe.wait_ge(sem("x_lo_made"), NP * n + k + 1)
            for c in range(KC):
                a = [x[:, k % GRP, c * P:(c + 1) * P] for x in (x_hi, x_lo)]
                last = mm3(pe, bank(k % 2), a, (wc_hi[:, c, :], wc_lo[:, c, :]), c == 0, c == KC - 1)
            last.then_inc(sem("conv_done"), 1)

        def copy_pe(act, n, k):
            if not isinstance(n, int) or n > 0:
                act.wait_ge(sem("xn_made"), NP * (n - 1) + k + 1)
                act.wait_ge(sem("red_summed"), n)
            act.wait_ge(sem("conv_done"), NP * n + k + 1)
            act.activation(pe_sb[:, k * C:(k + 1) * C], bank(k % 2), ACT.Copy).then_inc(sem("pe_copied"), 1)

        def measure(dve, n, k):
            dve.wait_ge(sem("pe_copied"), NP * n + k + 1)
            dve.bn_stats(stats[:, k, :], pe_sb[:, k * C:(k + 1) * C]).then_inc(sem("stats_made"), 1)
            if k:
                dve.bn_aggr(mv[:, k - 1, :], stats[:, k - 1, :]).then_inc(sem("aggr_made"), 1)
            dve.wait_ge(sem("stats_made"), (NP + 1) * n + k + 1)

        def reduce_window(dve, n):
            if not isinstance(n, int) or n > 0:
                dve.wait_ge(sem("redn_made"), n)
            dve.tensor_reduce(red_sum[:, :], pe_sb[:, :].rearrange("p (k c) -> p c k", k=NP), AX, ALU.add)\
               .then_inc(sem("red_summed"), 1)
            dve.bn_aggr(mv[:, NP - 1, :], stats[:, NP - 1, :]).then_inc(sem("aggr_made"), 1)
            dve.wait_ge(sem("red_summed"), n + 1)
            dve.tensor_scalar(red[:, :], red_sum[:, :], 1.0 / NP, None, ALU.mult).then_inc(sem("red_made"), 1)
            dve.wait_ge(sem("red_made"), n + 1)
            dve.bn_stats(stats[:, NP, :], red[:, :]).then_inc(sem("stats_made"), 1)
            dve.tensor_tensor(local[:, bass.ds(n * C, C)], red[:, :], rows[:, 0:C], ALU.add).then_inc(sem("residual_made"), 1)
            dve.wait_ge(sem("stats_made"), (NP + 1) * (n + 1))
            dve.tensor_copy(spare[:, 0:1], spare[:, 1:2]).then_inc(sem("spacer"), 1)
            dve.bn_aggr(mv[:, NP, :], stats[:, NP, :]).then_inc(sem("aggr_made"), 1)
            dve.wait_ge(sem("aggr_made"), (NP + 1) * (n + 1))
            dve.tensor_scalar(veps[:, :], mv[:, :, 1], 1e-5, None, ALU.add).then_inc(sem("var_made"), 1)

        def normalize_patch(act, n, k):
            act.wait_ge(sem("nmr_made"), n + 1)
            if not isinstance(n, int) or n > 0:
                act.wait_ge(sem("xT_done"), NP * (n - 1) + k + 1)
            normalize(act, xn[:, k * C:(k + 1) * C], pe_sb[:, k * C:(k + 1) * C], k).then_inc(sem("xn_made"), 1)

        def turn_patch(pe, n, k):
            pe.wait_ge(sem("xn_made"), NP * n + k + 1)
            if not isinstance(n, int) or n > 0 or k >= 2:
                pe.wait_ge(sem("xg_lo_made"), NP * n + k + 1 - earlier(k, NP))
            turn(pe, bank(2 + k % 2), xn[:, k * C:(k + 1) * C]).then_inc(sem("xT_done"), 1)

        def split_xT_hi(act, n, k):
            if not isinstance(n, int) or n > 0 or k >= 2:
                act.wait_ge(sem("kv_done"), NP * n + k + 1 - earlier(k, NP))
            act.wait_ge(sem("xT_done"), NP * n + k + 1)
            act.activation(xg_hi[:, k % 2, :], bank(2 + k % 2), ACT.Copy).then_inc(sem("xg_hi_made"), 1)

        def split_xT_lo(dve, n, k):
            dve.wait_ge(sem("xg_hi_made"), NP * n + k + 1)
            dve.tensor_tensor(xg_lo[:, k % 2, :], bank(2 + k % 2), xg_hi[:, k % 2, :], ALU.subtract)\
               .then_inc(sem("xg_lo_made"), 1)

        def project_kv(pe, n, k):
            pe.wait_ge(sem("xg_lo_made"), NP * n + k + 1)
            if not isinstance(n, int) or n > 0 or k >= 2:
                pe.wait_ge(sem("kv_copied"), NP * n + k + 1 - earlier(k, NP))
            dst = bank(4 + k % 2, 0, 512)
            pe.matmul(dst, ones_r[:, :], kvb[:, :], start=True, stop=False)
            for c in range(CH):
                a = [x[:, k % 2, c * P:(c + 1) * P] for x in (xg_hi, xg_lo)]
                last = mm3(pe, dst, a, (wkv_hi[:, c, :], wkv_lo[:, c, :]), False, c == CH - 1)
            last.then_inc(sem("kv_done"), 1)

        def copy_kv(act, n, k):
            if not isinstance(n, int) or n > 0:
                act.wait_ge(sem("agg_made"), n)
            act.wait_ge(sem("kv_done"), NP * n + k + 1)
            act.activation(kv_sb[:, k, :], bank(4 + k % 2, 0, 512), ACT.Copy).then_inc(sem("kv_copied"), 1)

        def normalize_red(act, n):
            act.wait_ge(sem("nmr_made"), n + 1)
            if not isinstance(n, int) or n > 0:
                act.wait_ge(sem("redT_done"), n)
            normalize(act, redn[:, :], red[:, :], NP).then_inc(sem("redn_made"), 1)

        def turn_red(pe, n):
            pe.wait_ge(sem("redn_made"), n + 1)
            turn(pe, bank(6), redn).then_inc(sem("redT_done"), 1)

        def affine_red(act, n):
            if not isinstance(n, int) or n > 0:
                act.wait_ge(sem("q_done"), n)
            act.wait_ge(sem("redT_done"), n + 1)
            affine(act, redT, bank(6), LAQ, "redT_made")

        def project_q(pe, n):
            pe.wait_ge(sem("redT_made"), CH * (n + 1))
            mm_rows(pe, bank(7), redT, w_q, 0, C).then_inc(sem("q_done"), 1)

        def copy_q(act, n):
            act.wait_ge(sem("q_done"), n + 1)
            if not isinstance(n, int) or n > 0:
                act.wait_ge(sem("agg_made"), n)
            act.activation(q_sb[:, :], bank(7), ACT.Copy, scale=C ** -0.5).then_inc(sem("q_made"), 1)

        def attend(dve, n, chain_name, per):
            s, i = sem(chain_name), [0]

            def link(ins):
                ins.then_inc(s, 1)
                i[0] += 1
                dve.wait_ge(s, per * n + i[0])

            dve.wait_ge(sem("kv_copied"), NP * (n + 1))
            dve.wait_ge(sem("q_made"), n + 1)
            sk = sc[:, :].rearrange("p (k h) -> p k h", k=NP)
            by_head = lambda x: x[:, :].rearrange("p (k h) -> p h k", k=NP)
            over_k = lambda x: x[:, :].unsqueeze(1).broadcast_to([P, NP, H8])
            link(dve.tensor_tensor(prod[:, :].rearrange("p (k c) -> p k c", k=NP), kv_sb[:, :, 0:C],
                                   q_sb[:, :].unsqueeze(1).broadcast_to([P, NP, C]), ALU.mult))
            link(dve.tensor_reduce(sc[:, :], prod[:, :].rearrange("p (x d) -> p x d", d=DH8), AX, ALU.add))
            link(dve.tensor_reduce(smax[:, :], by_head(sc), AX, ALU.max))
            dve.tensor_tensor(sk, sk, over_k(smax), ALU.subtract).then_inc(sem("score_made"), 1)
            dve.wait_ge(sem("exp_made"), n + 1)
            link(dve.tensor_reduce(den[:, :], by_head(pr), AX, ALU.add))
            link(dve.reciprocal(rden[:, :], den[:, :]))
            link(dve.tensor_tensor(attn[:, :].rearrange("p (k h) -> p k h", k=NP),
                                   pr[:, :].rearrange("p (k h) -> p k h", k=NP), over_k(rden), ALU.mult))
            link(dve.tensor_tensor(prod[:, :].rearrange("p (k h d) -> p k h d", k=NP, d=DH8),
                                   kv_sb[:, :, C:2 * C].rearrange("p k (h d) -> p k h d", d=DH8),
                                   attn[:, :].rearrange("p (k h) -> p k h", k=NP).unsqueeze(3)
                                   .broadcast_to([P, NP, H8, DH8]), ALU.mult))
            if not isinstance(n, int) or n > 0:
                dve.wait_ge(sem("aggT_done"), n)
            dve.tensor_reduce(agg[:, :], prod[:, :].rearrange("p (k c) -> p c k", k=NP), AX, ALU.add)\
               .then_inc(sem("agg_made"), 1)
            assert i[0] == per
            return None

        ATTEND = 7

        def exponent(act, n):
            act.wait_ge(sem("score_made"), n + 1)
            act.activation(pr[:, :], sc[:, :], ACT.Exp).then_inc(sem("exp_made"), 1)

        def turn_agg(pe, n):
            pe.wait_ge(sem("agg_made"), n + 1)
            if not isinstance(n, int) or n < NW - 1:
                pe.wait_ge(sem("redT_made"), CH * (n + 2))
            else:
                pe.wait_ge(sem("aggT_copied"), n)
            turn(pe, bank(6), agg).then_inc(sem("aggT_done"), 1)

        def copy_aggT(act, n):
            act.wait_ge(sem("aggT_done"), n + 1)
            if not isinstance(n, int) or n > 0:
                act.wait_ge(sem("proj_done"), n)
            act.activation(aggT[:, :], bank(6), ACT.Copy).then_inc(sem("aggT_copied"), 1)

        def project_agg(pe, n):
            pe.wait_ge(sem("aggT_copied"), n + 1)
            if not isinstance(n, int) or n < NW - 1:
                pe.wait_ge(sem("q_made"), n + 2)
            else:
                pe.wait_ge(sem("local_made"), n)
            mm_rows(pe, bank(7), aggT, w_proj, 0, C).then_inc(sem("proj_done"), 1)

        def add_local(dve, n):
            dve.wait_ge(sem("residual_made"), n + 1)
            dve.wait_ge(sem("proj_done"), n + 1)
            dve.tensor_tensor(local[:, bass.ds(n * C, C)], bank(7), local[:, bass.ds(n * C, C)], ALU.add)\
               .then_inc(sem("local_made"), 1)

        def round_pe(pe, n, first, last):
            if not last:
                for k in range(NP):
                    conv(pe, n + 1, k)
            for k in range(NP):
                turn_patch(pe, n, k)
                if k:
                    project_kv(pe, n, k - 1)
                if k == 1:
                    turn_red(pe, n)
                if k == 3:
                    project_q(pe, n)
                if not first and k == 5:
                    turn_agg(pe, n - 1)
                if not first and k == 7:
                    project_agg(pe, n - 1)
            project_kv(pe, n, NP - 1)

        def round_act(act, n, first, last, second_last):
            normalize_red(act, n)
            for k in range(NP):
                normalize_patch(act, n, k)
                if not last:
                    if k >= GRP:
                        split_x_hi(act, n + 1, k)
                    if k:
                        copy_pe(act, n + 1, k - 1)
                if not first and k == 4:
                    exponent(act, n - 1)
            if not last:
                copy_pe(act, n + 1, NP - 1)
            for k in range(NP):
                split_xT_hi(act, n, k)
                if k == 1:
                    affine_red(act, n)
                if k == 3:
                    copy_q(act, n)
                if not first and k == 5:
                    copy_aggT(act, n - 1)
                if k:
                    copy_kv(act, n, k - 1)
                if not (last or second_last) and k >= NP - GRP:
                    split_x_hi(act, n + 2, k - (NP - GRP))
            copy_kv(act, n, NP - 1)

        def round_pool(pool, n, last, second_last):
            if not last:
                for k in range(GRP, NP):
                    split_x_lo(pool, n + 1, k)
                pool.wait_ge(sem("xn_made"), NP * (n + 1))
                pool.wait_ge(sem("redn_made"), n + 1)
                inverse_std(pool, n + 1)
            if not (last or second_last):
                for k in range(GRP):
                    split_x_lo(pool, n + 2, k)

        def round_dve(dve, n, first, last):
            if not first:
                attend(dve, n - 1, "att_link", ATTEND)
            if not last:
                for k in range(NP):
                    measure(dve, n + 1, k)
                reduce_window(dve, n + 1)
            for k in range(NP):
                split_xT_lo(dve, n, k)
                if not last and k == 1:
                    shift_of(dve, n + 1)
                if not first and k == 7:
                    add_local(dve, n - 1)

        def pe_global(pe):
            for s in range(1 + NW):
                pe.wait_ge(sem("ga_xn_made"), s + 1)
                if s >= 2:
                    pe.wait_ge(sem("gnT_made"), CH * (s - 1))
                turn(pe, bank(2 + s % 2), redn[:, :] if s == 0 else xn[:, (s - 1) * C:s * C]).then_inc(sem("ga_turned"), 1)
                if s:
                    pe.wait_ge(sem("local_made"), NW)
                    if s >= 3:
                        pe.wait_ge(sem("localT_made"), s - 2)
                    turn(pe, bank(s % 2), local[:, (s - 1) * C:s * C]).then_inc(sem("local_turned"), 1)
                pe.wait_ge(sem("gnT_made"), CH * (s + 1))
                if s == 0:
                    mm_rows(pe, bank(4), gnT[:, 0, :], w_gq, 0, C).then_inc(sem("q_done"), 1)
                    continue
                if s == 2:
                    pe.wait_ge(sem("q_made"), NW + 1)
                elif s >= 3:
                    pe.wait_ge(sem("kv_copied"), NP * NW + s - 2)
                mm_rows(pe, bank(4 + s % 2, 0, 2 * C), gnT[:, s % 2, :], w_gkv, 0, 2 * C).then_inc(sem("kv_done"), 1)
                pe.wait_ge(sem("localT_made"), s)
                if s >= 3:
                    pe.wait_ge(sem("patch_made"), s - 2)
                mm_rows(pe, bank(6 + s % 2), localT[:, s % 2, :], w_mod, 0, C).then_inc(sem("mod_done"), 1)
            pe.wait_ge(sem("agg_made"), NW + 1)
            pe.wait_ge(sem("patch_made"), NW)
            turn(pe, bank(6), agg).then_inc(sem("aggT_done"), 1)
            pe.wait_ge(sem("aggT_copied"), NW + 1)
            mm_rows(pe, bank(7), aggT, w_gproj, 0, C).then_inc(sem("proj_done"), 1)

        def act_global(act):
            normalized_scales(act, "class")
            act.wait_ge(sem("redT_done"), NW)
            for s in range(1 + NW):
                if s == 0:
                    normalize(act, redn[:, :], rows[:, 3 * C:4 * C], NW).then_inc(sem("ga_xn_made"), 1)
                else:
                    normalize(act, xn[:, (s - 1) * C:s * C], local[:, (s - 1) * C:s * C], s - 1).then_inc(sem("ga_xn_made"), 1)
                act.wait_ge(sem("ga_turned"), s + 1)
                if s == 2:
                    act.wait_ge(sem("q_done"), NW + 1)
                elif s >= 3:
                    act.wait_ge(sem("kv_done"), NP * NW + s - 2)
                affine(act, gnT[:, s % 2, :], bank(2 + s % 2), GAQ if s == 0 else GAKV, "gnT_made")
                if s == 1:
                    copy_q_global(act)
                if s >= 2:
                    copy_gkv(act, s - 1)
            copy_gkv(act, NW)
            exponent(act, NW)
            copy_aggT(act, NW)

        def copy_q_global(act):
            act.wait_ge(sem("q_done"), NW + 1)
            act.wait_ge(sem("agg_made"), NW)
            act.activation(q_sb[:, :], bank(4), ACT.Copy, scale=C ** -0.5).then_inc(sem("q_made"), 1)

        def copy_gkv(act, s):
            act.wait_ge(sem("kv_done"), NP * NW + s)
            act.activation(kv_sb[:, s - 1, :], bank(4 + s % 2, 0, 2 * C), ACT.Copy).then_inc(sem("kv_copied"), 1)

        def dve_global(dve):
            dve.wait_ge(sem("local_made"), NW)
            layer_stats(dve, "class", lambda t: local[:, t * C:(t + 1) * C] if t < NW else rows[:, 3 * C:4 * C])
            for s in range(1, 1 + NW):
                dve.wait_ge(sem("local_turned"), s)
                if s >= 3:
                    dve.wait_ge(sem("mod_done"), s - 2)
                dve.tensor_copy(localT[:, s % 2, :], bank(s % 2)).then_inc(sem("localT_made"), 1)
                if s >= 2:
                    patch_out(dve, s - 1)
            patch_out(dve, NW)
            attend(dve, NW, "att_link", ATTEND)
            dve.tensor_tensor(redT[:, :], rows[:, 2 * C:3 * C], rows[:, 3 * C:4 * C], ALU.add).then_inc(sem("cls_bias"), 1)
            dve.wait_ge(sem("cls_bias"), 1)
            dve.wait_ge(sem("proj_done"), NW + 1)
            dve.tensor_tensor(h_at(NW), bank(7), redT[:, :], ALU.add).then_inc(sem("patch_made"), 1)
            dve.wait_ge(sem("patch_made"), NW + 1)

        def patch_out(dve, s):
            dve.wait_ge(sem("mod_done"), s)
            dve.tensor_tensor(h_at(s - 1), bank(6 + s % 2), rows[:, C:2 * C], ALU.add).then_inc(sem("patch_made"), 1)

        ENDS = {"w_loaded": 48, "qkv_made": 2 * T, "pool_prod_made": T, "pool_prod_used": T,
                "s_made": 1, "exp_made": 1, "p_made": 1}

        def seen(layer, name, count):
            return count + layer * ENDS.get(name, T)

        def keys(layer, t):
            return T if layer == 0 else t + 1

        def on_pool(layer, t):
            return t % 2 == 1

        def of_query(x, t, layer, ns):
            return x[:, t * T * H16:(t * T + ns) * H16]

        def score_products(eng, layer, t, dst):
            ns = keys(layer, t)
            return eng.tensor_tensor(dst[:, 0:ns * C].rearrange("p (s c) -> p s c", s=ns), a_qkv[:, 0:ns, C:2 * C],
                                     a_qkv[:, t, 0:C].unsqueeze(1).broadcast_to([P, ns, C]), ALU.mult)

        def value_products(eng, layer, t, dst):
            ns = keys(layer, t)
            return eng.tensor_tensor(dst[:, 0:ns * C].rearrange("p (s h d) -> p s h d", s=ns, d=D16),
                                     a_qkv[:, 0:ns, 2 * C:3 * C].rearrange("p s (h d) -> p s h d", d=D16),
                                     of_query(a_p, t, layer, ns).rearrange("p (s h) -> p s h", s=ns).unsqueeze(3)
                                     .broadcast_to([P, ns, H16, D16]), ALU.mult)

        def pool_attention(pool, layer):
            inverse_std(pool, NW + LN.index(f"attention {layer}"))
            pool.wait_ge(sem("a_qkv_made"), seen(layer, "qkv_made", 2 * T))
            n = 0
            for make, ready in ((score_products, False), (value_products, True)):
                if ready:
                    pool.wait_ge(sem("a_p_made"), seen(layer, "p_made", 1))
                for t in range(T):
                    if on_pool(layer, t):
                        if n:
                            pool.wait_ge(sem("a_pool_prod_used"), seen(layer, "pool_prod_used", n))
                        make(pool, layer, t, a_prod[:, 1, :]).then_inc(sem("a_pool_prod_made"), 1)
                        n += 1

        def pe_attention(pe, layer):
            w, wo = a_w[layer], a_wo[layer]
            pe.wait_ge(sem("a_w_loaded"), seen(layer, "w_loaded", 48 if layer == 0 else 32))
            for t in range(T):
                pe.wait_ge(sem("a_xn_made"), seen(layer, "xn_made", t + 1))
                if t >= 2:
                    pe.wait_ge(sem("a_xT_made"), seen(layer, "xT_made", t - 1))
                turn(pe, bank(t % 2), a_xn[:, t % 2, :]).then_inc(sem("a_turned"), 1)
                pe.wait_ge(sem("a_xT_made"), seen(layer, "xT_made", t + 1))
                if t >= 2:
                    pe.wait_ge(sem("a_qkv_made"), seen(layer, "qkv_made", 2 * (t - 1)))
                mm_rows(pe, bank(2 + t % 2, 0, 2 * C), a_xT[:, t % 2, :], w, 0, 2 * C)
                mm_rows(pe, bank(4 + t % 2), a_xT[:, t % 2, :], w, 2 * C, 3 * C).then_inc(sem("a_qkv_done"), 1)
            for t in range(T):
                pe.wait_ge(sem("a_o_made"), seen(layer, "o_made", t + 1))
                if t >= 2:
                    pe.wait_ge(sem("a_oT_made"), seen(layer, "oT_made", t - 1))
                turn(pe, bank(t % 2), a_o[:, t * C:(t + 1) * C]).then_inc(sem("a_o_turned"), 1)
                pe.wait_ge(sem("a_oT_made"), seen(layer, "oT_made", t + 1))
                if t >= 2:
                    pe.wait_ge(sem("a_h_made"), seen(layer, "h_made", t - 1))
                mm_rows(pe, bank(6 + t % 2), a_oT[:, t % 2, :], wo, 0, C).then_inc(sem("a_o_done"), 1)

        def act_attention(act, layer):
            normalized_scales(act, f"attention {layer}")
            for t in range(T):
                if t >= 2:
                    act.wait_ge(sem("a_turned"), seen(layer, "turned", t - 1))
                normalize(act, a_xn[:, t % 2, :], h_at(t), t).then_inc(sem("a_xn_made"), 1)
                act.wait_ge(sem("a_turned"), seen(layer, "turned", t + 1))
                if t >= 2:
                    act.wait_ge(sem("a_qkv_done"), seen(layer, "qkv_done", t - 1))
                act.activation(a_xT[:, t % 2, :], bank(t % 2), ACT.Copy).then_inc(sem("a_xT_made"), 1)
                if layer == 1 and t:
                    copy_qkv(act, t - 1)
            if layer == 1:
                copy_qkv(act, T - 1)
            act.wait_ge(sem("a_s_made"), seen(layer, "s_made", 1))
            act.activation(a_p[:, :], a_s[:, :], ACT.Exp, scale=D16 ** -0.5).then_inc(sem("a_exp_made"), 1)
            for t in range(T):
                act.wait_ge(sem("a_o_turned"), seen(layer, "o_turned", t + 1))
                if t >= 2:
                    act.wait_ge(sem("a_o_done"), seen(layer, "o_done", t - 1))
                act.activation(a_oT[:, t % 2, :], bank(t % 2), ACT.Copy).then_inc(sem("a_oT_made"), 1)

        def copy_qkv(act, t):
            act.wait_ge(sem("a_qkv_done"), seen(1, "qkv_done", t + 1))
            act.activation(a_qkv[:, t, 0:2 * C], bank(2 + t % 2, 0, 2 * C), ACT.Copy).then_inc(sem("a_qkv_made"), 1)
            act.activation(a_qkv[:, t, 2 * C:3 * C], bank(4 + t % 2), ACT.Copy).then_inc(sem("a_qkv_made"), 1)

        def dve_attention(dve, layer):
            link = Chain(dve, f"a{layer}_link")
            layer_stats(dve, f"attention {layer}", h_at)
            if layer == 0:
                dve.wait_ge(sem("a_w_loaded"), seen(layer, "w_loaded", 48))
                for t in range(T):
                    dve.wait_ge(sem("a_qkv_done"), seen(layer, "qkv_done", t + 1))
                    dve.tensor_tensor(a_qkv[:, t, 0:2 * C], bank(2 + t % 2, 0, 2 * C), a_bias[:, 0:2 * C], ALU.add)\
                       .then_inc(sem("a_qkv_made"), 1)
                    dve.tensor_tensor(a_qkv[:, t, 2 * C:3 * C], bank(4 + t % 2), a_bias[:, 2 * C:3 * C], ALU.add)\
                       .then_inc(sem("a_qkv_made"), 1)
            else:
                link(dve.memset(a_s[:, :], NEG4))
            dve.wait_ge(sem("a_qkv_made"), seen(layer, "qkv_made", 2 * T))
            pooled = 0
            for t in range(T):
                ns = keys(layer, t)
                slot = a_prod[:, int(on_pool(layer, t)), 0:ns * C]
                if on_pool(layer, t):
                    pooled += 1
                    dve.wait_ge(sem("a_pool_prod_made"), seen(layer, "pool_prod_made", pooled))
                else:
                    link(score_products(dve, layer, t, a_prod[:, 0, :]))
                st = of_query(a_s, t, layer, ns)
                ins = dve.tensor_reduce(st, slot.rearrange("p (x d) -> p x d", d=D16), AX, ALU.add)
                if on_pool(layer, t):
                    ins.then_inc(sem("a_pool_prod_used"), 1)
                    dve.wait_ge(sem("a_pool_prod_used"), seen(layer, "pool_prod_used", pooled))
                else:
                    link(ins)
                if layer == 1:
                    link(dve.tensor_scalar(st, st, -40.0, 40.0, ALU.max, ALU.min))
            s4 = a_s[:, :].rearrange("p (t s h) -> p t s h", t=T, s=T)
            p4 = a_p[:, :].rearrange("p (t s h) -> p t s h", t=T, s=T)
            if layer == 0:
                link(dve.memset(s4[:, 0, T - 1, :], NEG4))
                link(dve.memset(s4[:, T - 1, 0, :], NEG4))
            th = lambda x: x[:, :].rearrange("p (t h) -> p t h", t=T)
            over_s = lambda x: th(x).unsqueeze(2).broadcast_to([P, T, T, H16])
            link(dve.tensor_reduce(th(a_max), s4.rearrange("p t s h -> p t h s"), AX, ALU.max))
            dve.tensor_tensor(s4, s4, over_s(a_max), ALU.subtract).then_inc(sem("a_s_made"), 1)
            dve.wait_ge(sem("a_exp_made"), seen(layer, "exp_made", 1))
            link(dve.tensor_reduce(th(a_den), p4.rearrange("p t s h -> p t h s"), AX, ALU.add))
            link(dve.reciprocal(a_rden[:, :], a_den[:, :]))
            dve.tensor_tensor(p4, p4, over_s(a_rden), ALU.mult).then_inc(sem("a_p_made"), 1)
            dve.wait_ge(sem("a_p_made"), seen(layer, "p_made", 1))
            for t in range(T):
                ns = keys(layer, t)
                slot = a_prod[:, int(on_pool(layer, t)), 0:ns * C]
                if on_pool(layer, t):
                    pooled += 1
                    dve.wait_ge(sem("a_pool_prod_made"), seen(layer, "pool_prod_made", pooled))
                else:
                    link(value_products(dve, layer, t, a_prod[:, 0, :]))
                dve.tensor_reduce(a_o[:, t * C:(t + 1) * C], slot.rearrange("p (s c) -> p c s", s=ns), AX, ALU.add)\
                   .then_inc(sem("a_o_made"), 1)
                dve.wait_ge(sem("a_o_made"), seen(layer, "o_made", t + 1))
                if on_pool(layer, t):
                    dve.sem_inc(sem("a_pool_prod_used"), 1)
                if t >= 2:
                    add_o(dve, layer, t - 2)
            add_o(dve, layer, T - 2)
            add_o(dve, layer, T - 1)

        def add_o(dve, layer, t):
            dve.wait_ge(sem("a_o_done"), seen(layer, "o_done", t + 1))
            dve.tensor_tensor(h_at(t), bank(6 + t % 2), h_at(t), ALU.add).then_inc(sem("a_h_made"), 1)

        def top_two(dve, link, x, t8, ti, tf, count):
            for t in range(count):
                dve.max(t8[:, t, :], x[:, t, :])
            link(dve.memset(spare[:, :], 0.0))
            for t in range(count):
                dve.max_index(ti[:, t, :], t8[:, t, :], x[:, t, :])
            link(dve.memset(spare[:, :], 0.0))
            link(dve.tensor_copy(tf[:, :, :], ti[:, :, 0:2]))

        def spread(dve, link, tf, w, hots, dst, n):
            for j in range(2):
                link(dve.tensor_tensor(hots[:, j], iota[:, 0:n].unsqueeze(1).broadcast_to([P, T, n]),
                                       tf[:, :, j:j + 1].broadcast_to([P, T, n]), ALU.is_equal))
                link(dve.tensor_tensor(hots[:, j], hots[:, j], w[:, :, j:j + 1].broadcast_to([P, T, n]), ALU.mult))
            link(dve.tensor_tensor(dst[:, :, :], hots[:, 0], hots[:, 1], ALU.add))

        STEPS = 2 * NB * FC
        LAG = 2
        START = {"gelu_made": 2, "hid_made": 2, "down_made": FC, "res_made": 2, "gm_made": 2}

        def made(name, count):
            return count + START.get(name, 0)

        def where(j):
            par, r = divmod(j, NB * FC)
            b, fc = divmod(r, FC)
            return par, b, fc, par * NB + b

        def pe_experts(pe):
            pe.wait_ge(sem("moe_small_loaded"), 32)
            for t in range(T):
                pe.wait_ge(sem("x2_made"), t + 1)
                if t >= 2:
                    pe.wait_ge(sem("x2T_made"), t - 1)
                turn(pe, bank(t % 2), x2[:, t * C:(t + 1) * C]).then_inc(sem("x2_turned"), 1)
                pe.wait_ge(sem("x2T_made"), t + 1)
                if t >= 2:
                    pe.wait_ge(sem("lg_made"), t - 1)
                mm_rows(pe, bank(2 + t % 2, 0, E), x2T[:, t, :], w_rt, 0, E).then_inc(sem("lg_done"), 1)
            pe.wait_ge(sem("lg_made"), T)
            pe.wait_ge(sem("gates_made"), 1)
            for t in range(T):
                if t >= 2:
                    pe.wait_ge(sem("gT_made"), t - 1)
                pe.transpose(bank(2 + t % 2, 0, P)[0:E, :], gates[:, t, :], ident[:, :]).then_inc(sem("g_turned"), 1)
                pe.wait_ge(sem("gT_made"), t + 1)
                if t >= 2:
                    pe.wait_ge(sem("beta_added"), t - 1)
                pe.matmul(bank(4 + t % 2), gT[:, t, :], beta[:, :], start=True, stop=True).then_inc(sem("beta_done"), 1)
            pe.wait_ge(sem("beta_added"), T)
            pe.wait_ge(sem("xT_split"), 2 * T)

            def up(ep, j):
                par, b, fc, blk = where(j)
                if b == 0 and fc == 0:
                    pe.wait_ge(sem("w_lo_made"), PIECES * (2 * ep + par + 1))
                pe.wait_ge(sem("gelu_made"), made("gelu_made", STEPS * ep + j - 1))
                for c in range(CH):
                    at = c * FF + fc * P
                    last = mm3(pe, bank(fc % 2), (w1_hi[par][:, at:at + P], w1_lo[par][:, at:at + P]),
                               (xT_hi[:, c, b * BW:(b + 1) * BW], xT_lo[:, c, b * BW:(b + 1) * BW]), c == 0, c == CH - 1)
                last.then_inc(sem("up_done"), 1)

            def down(ep, j):
                par, b, fc, blk = where(j)
                pe.wait_ge(sem("hid_made"), made("hid_made", STEPS * ep + j + 1))
                if fc == 0:
                    pe.wait_ge(sem("res_made"), made("res_made", 2 * NB * ep + blk - 1))
                for u in range(BT):
                    last = mm3(pe, pair[1 + blk % 2][:, u, 0:C],
                               (hid_hi[:, fc, u * P:(u + 1) * P], hid_lo[:, fc, u * P:(u + 1) * P]),
                               (w2_hi[par][:, fc * C:(fc + 1) * C], w2_lo[par][:, fc * C:(fc + 1) * C]),
                               fc == 0, fc == FC - 1)
                last.then_inc(sem("down_made"), 1)

            def experts(ep):
                for j in range(STEPS):
                    up(ep, j)
                    if j >= LAG:
                        down(ep, j - LAG)
                for j in range(STEPS - LAG, STEPS):
                    down(ep, j)

            with pe.Fori(0, E // 2 - 1) as ep:
                experts(ep)
            experts(E // 2 - 1)

        def load_vectors(sp, ep, par):
            sp.dma_start(b1[par][:, :], d["b1"][:, bass.ds((2 * ep + par) * FC, FC)]).then_inc(sem(f"v_loaded{par}"), 16)
            for dst, name in ((b2, "b2"), (gam, "gamma")):
                sp.dma_start(dst[par][:, :], d[name][:, bass.ds((2 * ep + par) * C, C)].broadcast_to([P, C]))\
                  .then_inc(sem(f"v_loaded{par}"), 16)

        def piece(j):
            r = j % (NB * FC)
            return r // 4 if r % 4 == 2 and r // 4 < PIECES else None

        def weight_piece(par, i):
            n = CH * FF * 2 // PIECES
            a = (i % 4) * n
            return [x[par][:, a:a + n] for x in ((w1raw, w1_hi, w1_lo) if i < 4 else (w2raw, w2_hi, w2_lo))]

        def split_w_hi(act, ep, par, i):
            raw, hi, _ = weight_piece(par, i)
            if i == 0:
                act.wait_ge(sem(f"w_loaded{par}"), 32 * (ep + 1))
                act.wait_ge(sem("down_made"), made("down_made", NB * FC * (2 * ep + par - 1) if not isinstance(ep, int) or 2 * ep + par > 1 else 0))
            act.activation(hi, raw, ACT.Copy).then_inc(sem("w_hi_made"), 1)

        def split_w_lo(pool, ep, par, i):
            raw, hi, lo = weight_piece(par, i)
            if i == 0:
                pool.wait_ge(sem("down_made"), made("down_made", NB * FC * (2 * ep + par - 1) if not isinstance(ep, int) or 2 * ep + par > 1 else 0))
            pool.wait_ge(sem("w_hi_made"), PIECES * (2 * ep + par) + i + 1)
            pool.tensor_tensor(lo, raw, hi, ALU.subtract).then_inc(sem("w_lo_made"), 1)

        def act_experts(act):
            act.sem_inc(sem("gelu_made"), START["gelu_made"])
            normalized_scales(act, "experts")
            for t in range(T):
                normalize(act, x2[:, t * C:(t + 1) * C], h_at(t), t).then_inc(sem("x2_made"), 1)
                act.wait_ge(sem("x2_turned"), t + 1)
                act.activation(x2T[:, t, :], bank(t % 2), ACT.Copy).then_inc(sem("x2T_made"), 1)
            for i in range(PIECES):
                split_w_hi(act, 0, 0, i)
            act.wait_ge(sem("tw_made"), 1)
            act.activation(te[:, :, :], tw[:, :, :], ACT.Exp).then_inc(sem("te_made"), 1)
            for t in range(T):
                act.wait_ge(sem("g_turned"), t + 1)
                act.activation(gT[:, t, :], bank(2 + t % 2, 0, P)[0:E, :], ACT.Copy).then_inc(sem("gT_made"), 1)

            def experts(ep, end):
                for j in range(STEPS):
                    par, b, fc, blk = where(j)
                    g = STEPS * ep + j
                    if b == 0 and fc == 0:
                        act.wait_ge(sem(f"v_loaded{par}"), 48 * (ep + 1))
                    act.wait_ge(sem("hid_made"), made("hid_made", g - 1))
                    act.wait_ge(sem("up_done"), g + 1)
                    act.activation(gel[:, fc % 2, :], bank(fc % 2), ACT.Gelu,
                                   bias=b1[par][:, fc:fc + 1]).then_inc(sem("gelu_made"), 1)
                    if piece(j) is not None and not (end and par == 1):
                        split_w_hi(act, ep + par, 1 - par, piece(j))

            with act.Fori(0, E // 2 - 1) as ep:
                experts(ep, False)
            experts(E // 2 - 1, True)

        def pool_experts(pool):
            inverse_std(pool, NW + LN.index("experts"))
            pool.sem_inc(sem("gm_made"), START["gm_made"])
            for i in range(PIECES):
                split_w_lo(pool, 0, 0, i)
            pool.wait_ge(sem("x2_made"), T)
            pool.wait_ge(sem("beta_added"), T)

            def block_input(ep, blk):
                par, b = divmod(blk, NB)
                if b == 0:
                    pool.wait_ge(sem(f"v_loaded{par}"), 48 * (ep + 1))
                pool.wait_ge(sem("res_made"), made("res_made", 2 * NB * ep + blk))
                pool.tensor_tensor(xb[:, :].rearrange("p (u c) -> p u c", u=BT),
                                   x2[:, b * BT * C:(b + 1) * BT * C].rearrange("p (u c) -> p u c", u=BT),
                                   b2[par][:, :].unsqueeze(1).broadcast_to([P, BT, C]), ALU.add)\
                    .then_inc(sem("xb_made"), 1)

            def block_scale(ep, blk):
                pool.wait_ge(sem("bvar_made"), 2 * NB * ep + blk + 1)
                pool.tensor_tensor(brs[:, :], bve[:, :], mhalf[:, 0:BT], ALU.pow).then_inc(sem("brstd_made"), 1)

            def block_output(ep, blk):
                par, b = divmod(blk, NB)
                n = 2 * NB * ep + blk
                pool.wait_ge(sem("nr_made"), BT * (n + 1))
                pool.tensor_tensor(gm[:, :].rearrange("p (u c) -> p u c", u=BT),
                                   nr[:, blk % 2, :].rearrange("p (u c) -> p u c", u=BT),
                                   gam[par][:, :].unsqueeze(1).broadcast_to([P, BT, C]), ALU.mult)\
                    .then_inc(sem("gm_made"), 1)
                pool.wait_ge(sem("gm_made"), made("gm_made", n + 1))
                pool.tensor_tensor(h_at(BT * b, BT), h_at(BT * b, BT), gm[:, :], ALU.add).then_inc(sem("y_added"), 1)
                pool.wait_ge(sem("y_added"), n + 1)

            def experts(ep, end):
                for blk in range(2 * NB):
                    par = blk // NB
                    todo = [piece(j) for j in range(blk * FC, (blk + 1) * FC) if piece(j) is not None]
                    if end and par == 1:
                        todo = []
                    for i in todo:
                        split_w_lo(pool, ep + par, 1 - par, i)
                    if blk == 0:
                        block_input(ep, 0)
                    else:
                        block_scale(ep, blk - 1)
                        block_input(ep, blk)
                        block_output(ep, blk - 1)
                block_scale(ep, 2 * NB - 1)
                block_output(ep, 2 * NB - 1)

            with pool.Fori(0, E // 2 - 1) as ep:
                experts(ep, False)
            experts(E // 2 - 1, True)

        def dve_experts(dve):
            link = Chain(dve, "moe_link")
            layer_stats(dve, "experts", h_at)
            for name in ("hid_made", "res_made", "down_made"):
                dve.sem_inc(sem(name), START[name])
            for t in range(T):
                dve.wait_ge(sem("x2T_made"), t + 1)
                src = x2T[:, t, :].rearrange("p (c b) -> p c b", c=CH)
                at = slice(t * P, (t + 1) * P)
                dve.tensor_copy(xT_hi[:, :, at], src).then_inc(sem("xT_split"), 1)
                dve.wait_ge(sem("xT_split"), 2 * t + 1)
                dve.tensor_tensor(xT_lo[:, :, at], src, xT_hi[:, :, at], ALU.subtract).then_inc(sem("xT_split"), 1)
                dve.wait_ge(sem("lg_done"), t + 1)
                dve.tensor_copy(lg[:, t, :], bank(2 + t % 2, 0, E)).then_inc(sem("lg_made"), 1)
            dve.wait_ge(sem("lg_made"), T)
            top_two(dve, link, lg, top, topi, topf, T)
            dve.tensor_tensor(tw[:, :, :], top[:, :, 0:2], top[:, :, 0:1].broadcast_to([P, T, 2]), ALU.subtract)\
               .then_inc(sem("tw_made"), 1)
            dve.wait_ge(sem("te_made"), 1)
            link(dve.tensor_reduce(tsum[:, :], te[:, :, :], AX, ALU.add))
            link(dve.reciprocal(trec[:, :], tsum[:, :]))
            link(dve.tensor_tensor(tw[:, :, :], te[:, :, :], trec[:, :].unsqueeze(2).broadcast_to([P, T, 2]), ALU.mult))
            spread(dve, link, topf, tw, hot, gates, E)
            dve.tensor_copy(gat_e[:, :].rearrange("p (e t) -> p t e", e=E), gates[:, :, :]).then_inc(sem("gates_made"), 1)
            dve.wait_ge(sem("gates_made"), 1)
            for t in range(T):
                dve.wait_ge(sem("beta_done"), t + 1)
                dve.tensor_tensor(h_at(t), bank(4 + t % 2), h_at(t), ALU.add).then_inc(sem("beta_added"), 1)

            def split_hidden(ep, j):
                par, b, fc, blk = where(j)
                g = STEPS * ep + j
                dve.wait_ge(sem("down_made"), made("down_made", g + 1 - FC))
                dve.wait_ge(sem("gelu_made"), made("gelu_made", g + 1))
                dve.tensor_copy(hid_hi[:, fc, :], gel[:, fc % 2, :]).then_inc(sem("hid_hi_made"), 1)
                dve.wait_ge(sem("hid_hi_made"), g + 1)
                dve.tensor_tensor(hid_lo[:, fc, :], gel[:, fc % 2, :], hid_hi[:, fc, :], ALU.subtract)\
                   .then_inc(sem("hid_made"), 1)

            def block_stats(ep, blk):
                n = 2 * NB * ep + blk
                dve.wait_ge(sem("xb_made"), n + 1)
                dve.wait_ge(sem("down_made"), made("down_made", FC * (n + 1)))
                dve.tensor_tensor(res[:, :].rearrange("p (u c) -> p u c", u=BT), pair[1 + blk % 2][:, :, 0:C],
                                  xb[:, :].rearrange("p (u c) -> p u c", u=BT), ALU.add).then_inc(sem("res_made"), 1)
                dve.wait_ge(sem("res_made"), made("res_made", n + 1))
                for u in range(BT):
                    dve.bn_stats(bst[:, u, :], res[:, u * C:(u + 1) * C]).then_inc(sem("bstats_made"), 1)
                dve.wait_ge(sem("bstats_made"), BT * (n + 1))
                dve.tensor_copy(spare[:, 0:1], spare[:, 1:2]).then_inc(sem("spacer"), 1)
                for u in range(BT):
                    dve.bn_aggr(bmv[:, u, :], bst[:, u, :]).then_inc(sem("baggr_made"), 1)
                dve.wait_ge(sem("baggr_made"), BT * (n + 1))
                dve.tensor_scalar(bve[:, :], bmv[:, :, 1], 1e-6, None, ALU.add).then_inc(sem("bvar_made"), 1)

            def block_normalize(ep, blk):
                par, b = divmod(blk, NB)
                n = 2 * NB * ep + blk
                dve.wait_ge(sem("brstd_made"), n + 1)
                dve.tensor_tensor(bsc[:, :], brs[:, :], gat_e[:, bass.ds((2 * ep + par) * T + BT * b, BT)], ALU.mult)\
                   .then_inc(sem("bscale_made"), 1)
                dve.wait_ge(sem("bscale_made"), n + 1)
                dve.wait_ge(sem("gm_made"), made("gm_made", n - 1))
                for u in range(BT):
                    dve.tensor_scalar(nr[:, blk % 2, u * C:(u + 1) * C], res[:, u * C:(u + 1) * C], bmv[:, u, 0:1],
                                      bsc[:, u:u + 1], ALU.subtract, ALU.mult).then_inc(sem("nr_made"), 1)
                dve.wait_ge(sem("nr_made"), BT * (n + 1))

            def experts(ep):
                for j in range(STEPS):
                    par, b, fc, blk = where(j)
                    split_hidden(ep, j)
                    if blk and fc == 2:
                        block_stats(ep, blk - 1)
                    if blk and fc == 4:
                        block_normalize(ep, blk - 1)
                block_stats(ep, 2 * NB - 1)
                block_normalize(ep, 2 * NB - 1)

            with dve.Fori(0, E // 2 - 1) as ep:
                experts(ep)
            experts(E // 2 - 1)

        def pe_lora(pe):
            pe.wait_ge(sem("z_loaded"), 64)
            for t in range(T):
                pe.wait_ge(sem("z_xn_made"), t + 1)
                if t >= 2:
                    pe.wait_ge(sem("z_xT_made"), t - 1)
                turn(pe, bank(t % 2), z_xn[:, t % 2, :]).then_inc(sem("z_turned"), 1)
                pe.wait_ge(sem("z_xT_made"), t + 1)
                if t >= 2:
                    pe.wait_ge(sem("z_made"), t - 1)
                mm_rows(pe, bank(2 + t % 2, 0, ZW), z_xT[:, t, :], z_w, 0, ZW).then_inc(sem("z_done"), 1)
            for t in range(T):
                pe.wait_ge(sem("z_s_made"), t + 1)
                if t >= 2:
                    pe.wait_ge(sem("z_sT_made"), t - 1)
                pe.transpose(bank(4 + t % 2, 0, P)[0:LOW, :], z_s[:, t, :], ident[:, :]).then_inc(sem("z_s_turned"), 1)
                if t >= 2:
                    pe.wait_ge(sem("z_out_made"), t - 1)
                for c in range(CH):
                    pe.matmul(bank(6 + t % 2), z_xT[:, t, c * P:(c + 1) * P], z_base[:, c, :], start=(c == 0), stop=False)
                pe.wait_ge(sem("z_sT_made"), t + 1)
                pe.matmul(bank(6 + t % 2), z_sT[0:LOW, t % 2, :], z_b[:, :], start=False, stop=True)\
                  .then_inc(sem("z_out_done"), 1)

        def act_lora(act):
            normalized_scales(act, "low rank")
            for t in range(T):
                if t >= 2:
                    act.wait_ge(sem("z_turned"), t - 1)
                normalize(act, z_xn[:, t % 2, :], h_at(t), t).then_inc(sem("z_xn_made"), 1)
                act.wait_ge(sem("z_turned"), t + 1)
                act.activation(z_xT[:, t, :], bank(t % 2), ACT.Copy).then_inc(sem("z_xT_made"), 1)
            act.wait_ge(sem("z_l_made"), 1)
            act.activation(z_p[:, :, :], z_l[:, :, :], ACT.Exp).then_inc(sem("z_exp_made"), 1)
            for t in range(T):
                act.wait_ge(sem("z_s_turned"), t + 1)
                if t >= 2:
                    act.wait_ge(sem("z_out_done"), t - 1)
                act.activation(z_sT[0:LOW, t % 2, :], bank(4 + t % 2, 0, P)[0:LOW, :], ACT.Copy).then_inc(sem("z_sT_made"), 1)

        def dve_lora(dve):
            link = Chain(dve, "z_link")
            layer_stats(dve, "low rank", h_at)
            dve.wait_ge(sem("z_loaded"), 64)
            for t in range(T):
                link(dve.tensor_tensor(h_at(t), h_at(t), z_rows[:, 0:C], ALU.add) if t == -1 else
                     dve.memset(z_g[:, t, :], -1.0))
                dve.wait_ge(sem("z_done"), t + 1)
                dve.tensor_copy(z[:, t, :], bank(2 + t % 2, 0, ZW)).then_inc(sem("z_made"), 1)
            dve.wait_ge(sem("z_made"), T)
            over = lambda x, n: x[:, :].unsqueeze(2).broadcast_to([P, T, n])
            link(dve.tensor_tensor(z_l[:, :, :], z[:, :, LOW:ZW],
                                   z_rows[:, C:C + E6].unsqueeze(1).broadcast_to([P, T, E6]), ALU.add))
            link(dve.tensor_reduce(z_max[:, :], z_l[:, :, :], AX, ALU.max))
            dve.tensor_tensor(z_l[:, :, :], z_l[:, :, :], over(z_max, E6), ALU.subtract).then_inc(sem("z_l_made"), 1)
            dve.wait_ge(sem("z_exp_made"), 1)
            link(dve.tensor_reduce(z_sum[:, :], z_p[:, :, :], AX, ALU.add))
            link(dve.reciprocal(z_rec[:, :], z_sum[:, :]))
            link(dve.tensor_tensor(z_g[:, :, 0:E6], z_p[:, :, :], over(z_rec, E6), ALU.mult))
            top_two(dve, link, z_g, z_top, z_topi, z_topf, T)
            link(dve.tensor_reduce(z_sum[:, :], z_top[:, :, 0:2], AX, ALU.add))
            link(dve.tensor_scalar(z_sum[:, :], z_sum[:, :], 1e-6, None, ALU.add))
            link(dve.reciprocal(z_rec[:, :], z_sum[:, :]))
            link(dve.tensor_tensor(z_tw[:, :, :], z_top[:, :, 0:2], over(z_rec, 2), ALU.mult))
            spread(dve, link, z_topf, z_tw, z_hot, z_sw, E6)
            for t in range(T):
                link(dve.tensor_copy(z_s[:, t, 0:R16], z[:, t, 0:R16]))
                dve.tensor_tensor(z_s[:, t, R16:LOW].rearrange("p (e r) -> p e r", e=E6),
                                  z[:, t, R16:LOW].rearrange("p (e r) -> p e r", e=E6),
                                  z_sw[:, t, :].unsqueeze(2).broadcast_to([P, E6, R16]), ALU.mult)\
                   .then_inc(sem("z_s_made"), 1)
                link(dve.tensor_tensor(h_at(t), h_at(t), z_rows[:, 0:C], ALU.add))
            for t in range(T):
                dve.wait_ge(sem("z_out_done"), t + 1)
                dve.tensor_tensor(z_o[:, t, :], bank(6 + t % 2), h_at(t), ALU.add).then_inc(sem("z_out_made"), 1)

        @block.sync
        def _(sp):
            sp.dma_start(wc_raw[:, 0:4, :], d["conv_main"].rearrange("p (c n) -> p c n", c=4)).then_inc(sem("wc_loaded"), 16)
            sp.wait_ge(sem("pads_zeroed"), 2)
            sp.dma_start(wc_raw[0:KREST, 4, :], d["conv_rest"]).then_inc(sem("wc_loaded"), 16)
            for g in range(NP // GRP):
                load_x(sp, 0, g)
            two = lambda name: d[name].rearrange("(c p) n -> p c n", p=P)
            sp.dma_start(wkv_raw[:, :, :], two("la_wkv")).then_inc(sem("wkv_loaded"), 16)
            sp.dma_start(vecs[:, :], d["vecs"]).then_inc(sem("wkv_loaded"), 16)
            sp.dma_start(rows[:, :], d["rows"].broadcast_to([P, len(ROWS) * C])).then_inc(sem("wkv_loaded"), 16)
            for dst, name in ((w_q, "la_wq"), (w_proj, "la_proj_w"), (w_mod, "mod_w"), (w_gq, "ga_wq"),
                              (w_gkv, "ga_wkv"), (w_gproj, "ga_proj_w")):
                sp.dma_start(dst[:, :, :], two(name)).then_inc(sem("tok_w_loaded"), 16)
            with sp.Fori(1, NW) as n:
                for g in range(NP // GRP):
                    load_x(sp, n, g)
            for e in range(2):
                sp.dma_start(w1raw[e][:, :], d["w1"][e * P:(e + 1) * P, :]).then_inc(sem(f"w_loaded{e}"), 16)
                sp.dma_start(w2raw[e][:, :], d["w2"][e * P:(e + 1) * P, :]).then_inc(sem(f"w_loaded{e}"), 16)
            phase(sp, 1)
            for layer in range(2):
                sp.dma_start(a_w[layer][:, :, :], two(f"qkv_w{layer}")).then_inc(sem("a_w_loaded"), 16)
                sp.dma_start(a_wo[layer][:, :, :], two(f"o_w{layer}")).then_inc(sem("a_w_loaded"), 16)
                if layer == 0:
                    sp.dma_start(a_bias[:, :], d["qkv_b"].broadcast_to([P, QKV])).then_inc(sem("a_w_loaded"), 16)
                    phase(sp, 2)
                    sp.dma_start(w_rt[:, :, :], two("router_w")).then_inc(sem("moe_small_loaded"), 16)
                    sp.dma_start(beta[:, :], d["beta"]).then_inc(sem("moe_small_loaded"), 16)
                    for e in range(2):
                        load_vectors(sp, 0, e)
                    with sp.Fori(1, E // 2) as ep:
                        for par in range(2):
                            sp.wait_ge(sem("w_lo_made"), PIECES * (2 * ep + par - 1))
                            at = bass.ds((2 * ep + par) * P, P)
                            sp.dma_start(w1raw[par][:, :], d["w1"][at, :]).then_inc(sem(f"w_loaded{par}"), 16)
                            sp.dma_start(w2raw[par][:, :], d["w2"][at, :]).then_inc(sem(f"w_loaded{par}"), 16)
                            sp.wait_ge(sem("y_added"), NB * (2 * ep + par - 1))
                            load_vectors(sp, ep, par)
                    phase(sp, 3)
            phase(sp, 4)
            sp.dma_start(z_w[:, :, :], two("z_w")).then_inc(sem("z_loaded"), 16)
            sp.dma_start(z_b[:, :], d["z_b"]).then_inc(sem("z_loaded"), 16)
            sp.dma_start(z_base[:, :, :], two("base_w")).then_inc(sem("z_loaded"), 16)
            sp.dma_start(z_rows[:, :], d["z_rows"].broadcast_to([P, C + E6])).then_inc(sem("z_loaded"), 16)
            for t in range(T):
                sp.wait_ge(sem("z_out_made"), t + 1)
                sp.dma_start(out[:, t, :], z_o[:, t, :]).then_inc(sem("stored"), 16)
            sp.wait_ge(sem("stored"), 16 * T)

        @block.gpsimd
        def _(pool):
            pool.memset(ident[:, :], 0.0).then_inc(sem("ident_zeroed"), 1)
            pool.memset(mhalf[:, :], -0.5).then_inc(sem("consts_made"), 1)
            pool.memset(xraw[:, :, 4, :], 0.0).then_inc(sem("pads_zeroed"), 1)
            pool.wait_ge(sem("ident_zeroed"), 1)
            pool.affine_select(out=ident[:, :], in_=ident[:, :], compare_op=ALU.not_equal, fill=1.0,
                               base=0, pattern=[[-1, P]], channel_multiplier=1).then_inc(sem("consts_made"), 1)
            pool.iota(iota[:, :], pattern=[[1, 8]], base=0, channel_multiplier=0,
                      allow_small_or_imprecise_dtypes=True).then_inc(sem("consts_made"), 1)
            for k in range(NP):
                split_x_lo(pool, 0, k)
            pool.wait_ge(sem("consts_made"), 1)
            inverse_std(pool, 0)
            for k in range(GRP):
                split_x_lo(pool, 1, k)
            with pool.Fori(0, NW - 2) as n:
                round_pool(pool, n, False, False)
            round_pool(pool, NW - 2, False, True)
            pool.wait_ge(sem("xn_made"), NP * NW)
            pool.wait_ge(sem("redn_made"), NW)
            inverse_std(pool, NW)
            phase(pool, 1)
            pool_attention(pool, 0)
            phase(pool, 2)
            pool_experts(pool)
            phase(pool, 3)
            pool_attention(pool, 1)
            phase(pool, 4)
            inverse_std(pool, NW + LN.index("low rank"))

        @block.tensor
        def _(pe):
            pe.wait_ge(sem("consts_made"), 3)
            pe.wait_ge(sem("wc_made"), 2)
            for k in range(NP):
                conv(pe, 0, k)
            pe.wait_ge(sem("wkv_loaded"), 48)
            for c in range(CH):
                last = pe.matmul(pair[2][0:1, 0, 0:512], vecs[:, LAKV + 2 + c:LAKV + 3 + c], wkv_raw[:, c, :],
                                 start=(c == 0), stop=(c == CH - 1))
            last.then_inc(sem("kvb_done"), 1)
            pe.wait_ge(sem("wkv_lo_made"), CH)
            pe.wait_ge(sem("kvb_made"), 3)
            pe.wait_ge(sem("tok_w_loaded"), 96)
            round_pe(pe, 0, True, False)
            with pe.Fori(1, NW - 1) as n:
                round_pe(pe, n, False, False)
            round_pe(pe, NW - 1, False, True)
            turn_agg(pe, NW - 1)
            project_agg(pe, NW - 1)
            pe_global(pe)
            phase(pe, 1)
            pe_attention(pe, 0)
            phase(pe, 2)
            pe_experts(pe)
            phase(pe, 3)
            pe_attention(pe, 1)
            phase(pe, 4)
            pe_lora(pe)

        @block.scalar
        def _(act):
            act.wait_ge(sem("wc_loaded"), 32)
            act.activation(wc_hi[:, :, :], wc_raw[:, :, :], ACT.Copy).then_inc(sem("wc_made"), 1)
            for k in range(NP):
                split_x_hi(act, 0, k)
                if k:
                    copy_pe(act, 0, k - 1)
            copy_pe(act, 0, NP - 1)
            for k in range(GRP):
                split_x_hi(act, 1, k)
            act.wait_ge(sem("wkv_scaled"), 2)
            for c in range(CH):
                act.activation(wkv_hi[:, c, :], wkv_raw[:, c, :], ACT.Copy).then_inc(sem("wkv_hi_made"), 1)
            round_act(act, 0, True, False, False)
            with act.Fori(1, NW - 2) as n:
                round_act(act, n, False, False, False)
            round_act(act, NW - 2, False, False, True)
            round_act(act, NW - 1, False, True, False)
            exponent(act, NW - 1)
            copy_aggT(act, NW - 1)
            act_global(act)
            phase(act, 1)
            act_attention(act, 0)
            phase(act, 2)
            act_experts(act)
            phase(act, 3)
            act_attention(act, 1)
            phase(act, 4)
            act_lora(act)

        @block.vector
        def _(dve):
            dve.memset(wc_raw[:, 4, :], 0.0).then_inc(sem("pads_zeroed"), 1)
            dve.memset(ones_r[:, :].bitcast(F32), 1.0).then_inc(sem("ones_made"), 1)
            dve.memset(kvb[:, :].bitcast(F32), 0.0).then_inc(sem("ones_made"), 1)
            dve.wait_ge(sem("wc_made"), 1)
            dve.tensor_tensor(wc_lo[:, :, :], wc_raw[:, :, :], wc_hi[:, :, :], ALU.subtract).then_inc(sem("wc_made"), 1)
            dve.memset(spare[:, :], 0.0).then_inc(sem("ones_made"), 1)
            dve.wait_ge(sem("ones_made"), 3)
            dve.wait_ge(sem("wkv_loaded"), 48)
            for k in range(NP):
                measure(dve, 0, k)
            reduce_window(dve, 0)
            dve.wait_ge(sem("kvb_done"), 1)
            dve.tensor_copy(kvb[0:1, :], pair[2][0:1, 0, 0:512]).then_inc(sem("kvb_made"), 1)
            dve.tensor_copy(kvb_f[0:1, :], pair[2][0:1, 0, 0:512]).then_inc(sem("kvb_made"), 1)
            dve.wait_ge(sem("kvb_made"), 2)
            dve.tensor_tensor(kvb[32:33, :], kvb_f[0:1, :], kvb[0:1, :], ALU.subtract).then_inc(sem("kvb_made"), 1)
            for c in range(CH):
                dve.tensor_scalar(wkv_raw[:, c, :], wkv_raw[:, c, :], vecs[:, LAKV + c:LAKV + c + 1], None, ALU.mult)\
                   .then_inc(sem("wkv_scaled"), 1)
            shift_of(dve, 0)
            dve.wait_ge(sem("wkv_hi_made"), CH)
            for c in range(CH):
                dve.tensor_tensor(wkv_lo[:, c, :], wkv_raw[:, c, :], wkv_hi[:, c, :], ALU.subtract)\
                   .then_inc(sem("wkv_lo_made"), 1)
            round_dve(dve, 0, True, False)
            with dve.Fori(1, NW - 1) as n:
                round_dve(dve, n, False, False)
            round_dve(dve, NW - 1, False, True)
            attend(dve, NW - 1, "att_link", ATTEND)
            add_local(dve, NW - 1)
            dve_global(dve)
            phase(dve, 1)
            dve_attention(dve, 0)
            phase(dve, 2)
            dve_experts(dve)
            phase(dve, 3)
            dve_attention(dve, 1)
            phase(dve, 4)
            dve_lora(dve)


def kernel(**inputs):
    import numpy as np
    import concourse.bacc as bacc
    from concourse.bass_utils import run_bass_kernel_spmd

    a = {k: np.asarray(v) for k, v in inputs.items()}
    cat, tidy = np.concatenate, np.ascontiguousarray
    tok = lambda name: a["L0_tok_" + name]
    x = a["x"][:, :, :126, :126].reshape(P, 3, 3, 3, 14, 3, 3, 14).transpose(2, 5, 1, 4, 7, 3, 6, 0)
    x = x.reshape(NW, 588, NP, P)
    conv = tok("conv_w").reshape(C, 588).T
    arrays = {
        "x_main": x[:, :512].reshape(NW, 4, P, NP, P).transpose(0, 2, 3, 1, 4).reshape(NW * P, NP * 512),
        "x_rest": x[:, 512:].reshape(NW * KREST, NP * P),
        "conv_main": conv[:512].reshape(4, P, C).transpose(1, 0, 2).reshape(P, 4 * C),
        "conv_rest": conv[512:],
        "vecs": np.stack([tok(n) for n in VECS]).reshape(len(VECS), CH, P).transpose(2, 0, 1).reshape(P, -1),
        "rows": cat([tok(n) for n in ROWS])[None],
        "la_wq": tok("la_wq"), "la_wkv": tok("la_wkv"), "la_proj_w": tok("la_proj_w"),
        "ga_wq": tok("ga_wq"), "ga_wkv": tok("ga_wkv"), "ga_proj_w": tok("ga_proj_w"), "mod_w": tok("mod_w"),
        "qkv_w0": cat([a["L0_attn_" + n].T for n in ("Wq", "Wk", "Wv")], axis=1),
        "qkv_b": cat([a["L0_attn_" + n] for n in ("bq", "bk", "bv")])[None],
        "o_w0": a["L0_attn_Wo"].T,
        "qkv_w1": a["L1_attn_Wqkv"].T, "o_w1": a["L1_attn_Wout"].T,
        "router_w": a["L0_ffn_router_w"],
        "w1": a["L0_ffn_w1"].reshape(E, CH, P, FF).transpose(0, 2, 1, 3).reshape(E * P, CH * FF),
        "w2": a["L0_ffn_w2"].reshape(E, FC, P, C).transpose(0, 2, 1, 3).reshape(E * P, FC * C),
        "b1": a["L0_ffn_b1"].reshape(E * FC, P).T,
        "b2": a["L0_ffn_b2"].reshape(1, E * C), "gamma": a["L0_ffn_gamma"].reshape(1, E * C),
        "beta": a["L0_ffn_beta"],
        "z_w": cat([a["L1_ffn_shared_A"], a["L1_ffn_routed_A"].reshape(E6 * R16, C), a["L1_ffn_router_W"]]).T,
        "z_b": cat([a["L1_ffn_shared_B"].T, a["L1_ffn_routed_B"].transpose(0, 2, 1).reshape(E6 * R16, C)]),
        "z_rows": cat([a["L1_ffn_base_b"], a["L1_ffn_router_b"]])[None],
        "base_w": a["L1_ffn_base_W"].T,
    }
    nc = bacc.Bacc("TRN2", target_bir_lowering=False, num_devices=1)
    feed, d = {}, {}
    for name, value in arrays.items():
        feed[f"in_{name}"] = tidy(value)
        d[name] = nc.dram_tensor(f"in_{name}", value.shape, F32, kind="ExternalInput").ap()
    out = nc.dram_tensor("out_h", (P, T, C), F32, kind="ExternalOutput").ap()
    vision_tower(nc, d, out)
    return run_bass_kernel_spmd(nc, [feed], core_ids=[0]).results[0]["out_h"]
```

```python
from contextlib import ExitStack

import concourse.bass as bass
from concourse import mybir

ALU = mybir.AluOpType
ACT = mybir.ActivationFunctionType
AX = mybir.AxisListType.X
F32 = mybir.dt.float32
F32R = mybir.dt.float32r
U32 = mybir.dt.uint32

P = 128
C = 256
CH = C // P
NW = 9
NP = 9
KC = 5
KREST = 588 - 4 * P
GRP = 3
H8, DH8 = 8, 32
H16, D16 = 16, 16
T = NW + 1
QKV = 3 * C
E, FF = 8, 1024
FC = FF // P
BT = 2
NB = T // BT
BW = BT * P
PIECES = 8
E6, R16 = 6, 16
LOW = (E6 + 1) * R16
ZW = LOW + E6
NEG4 = -4.0e9
VECS = ["la_ln_q_g", "la_ln_q_b", "la_ln_kv_g", "la_ln_kv_b", "ga_ln_q_g", "ga_ln_q_b", "ga_ln_kv_g", "ga_ln_kv_b"]
LAQ, LAKV, GAQ, GAKV = 0, 4, 8, 12
ROWS = ["la_proj_b", "mod_b", "ga_proj_b", "class_emb"]


def earlier(k, cycle, slots=2):
    return slots if k >= slots else k + cycle - (k + ((cycle - 1 - k) // slots) * slots)


def vision_tower(nc, d, out):
    ctx = ExitStack()
    with ctx:
        def sb(name, shape, dt=F32, scope=None):
            return (scope or ctx).enter_context(nc.sbuf_tensor(name, shape, dt))

        sems = {}

        def sem(name):
            if name not in sems:
                sems[name] = ctx.enter_context(nc.semaphore(name))
            return sems[name]

        pair = [ctx.enter_context(nc.psum_tensor(f"banks{2 * i}", [P, 2, 512], F32)) for i in range(4)]

        def bank(i, a=0, b=C):
            return pair[i // 2][:, i % 2, a:b]

        h = sb("h", [P, T * C])
        ident = sb("ident", [P, P])
        iota = sb("iota", [P, 8])
        stats = [sb(f"stats{i}", [P, T, 6]) for i in range(2)]
        mv = [sb(f"mv{i}", [P, T, 2]) for i in range(2)]
        veps = [sb(f"veps{i}", [P, T]) for i in range(2)]
        mhalf = sb("mhalf", [P, 10])
        spare = sb("spare", [P, 2])
        rstd = [sb(f"rstd{i}", [P, T]) for i in range(2)]
        nmr = [sb(f"nmr{i}", [P, T]) for i in range(2)]

        def h_at(t, n=1):
            return h[:, t * C:(t + n) * C]

        tok = ExitStack()
        wc_raw = sb("wc_raw", [P, KC, C], F32, tok)
        wc_hi = sb("wc_hi", [P, KC, C], F32R, tok)
        wc_lo = sb("wc_lo", [P, KC, C], F32R, tok)
        wkv_raw = sb("wkv_raw", [P, CH, 2 * C], F32, tok)
        wkv_hi = sb("wkv_hi", [P, CH, 2 * C], F32R, tok)
        wkv_lo = sb("wkv_lo", [P, CH, 2 * C], F32R, tok)
        xraw = sb("xraw", [P, NP, KC, P], F32, tok)
        x_hi = sb("x_hi", [P, NP, KC * P], F32R, tok)
        x_lo = sb("x_lo", [P, NP, KC * P], F32R, tok)
        pe_sb = sb("pe_sb", [P, NP * C], F32, tok)
        xn = sb("xn", [P, NP * C], F32, tok)
        xg_hi = sb("xg_hi", [P, 2, C], F32R, tok)
        xg_lo = sb("xg_lo", [P, 2, C], F32R, tok)
        kv_sb = sb("kv_sb", [P, NP + 1, 2 * C], F32, tok)
        prod = sb("prod", [P, (NP + 1) * C], F32, tok)
        vprod = sb("vprod", [P, (NP + 1) * C], F32, tok)
        red = sb("red", [P, C], F32, tok)
        redn = sb("redn", [P, C], F32, tok)
        red_sum = sb("red_sum", [P, C], F32, tok)
        redT = sb("redT", [P, C], F32, tok)
        q_sb = sb("q_sb", [P, C], F32, tok)
        sc = sb("sc", [P, (NP + 1) * H8], F32, tok)
        smax = sb("smax", [P, H8], F32, tok)
        pr = sb("pr", [P, NP * H8], F32, tok)
        den = sb("den", [P, H8], F32, tok)
        rden = sb("rden", [P, H8], F32, tok)
        attn = sb("attn", [P, (NP + 1) * H8], F32, tok)
        agg = sb("agg", [P, C], F32, tok)
        aggT = sb("aggT", [P, C], F32, tok)
        local = sb("local", [P, NW * C], F32, tok)
        w_q = sb("w_q", [P, CH, C], F32, tok)
        w_proj = sb("w_proj", [P, CH, C], F32, tok)
        w_mod = sb("w_mod", [P, CH, C], F32, tok)
        w_gq = sb("w_gq", [P, CH, C], F32, tok)
        w_gkv = sb("w_gkv", [P, CH, 2 * C], F32, tok)
        w_gproj = sb("w_gproj", [P, CH, C], F32, tok)
        vecs = sb("vecs", [P, 2 * len(VECS)], F32, tok)
        rows = sb("rows", [P, len(ROWS) * C], F32, tok)
        localT = sb("localT", [P, 2, C], F32, tok)
        gnT = sb("gnT", [P, 2, C], F32, tok)
        tok.close()

        w1raw = [sb(f"w1raw{i}", [P, CH * FF]) for i in range(2)]
        w2raw = [sb(f"w2raw{i}", [P, FC * C]) for i in range(2)]

        att = ExitStack()
        a_w = [sb(f"a_w{i}", [P, CH, QKV], F32, att) for i in range(2)]
        a_wo = [sb(f"a_wo{i}", [P, CH, C], F32, att) for i in range(2)]
        a_bias = sb("a_bias", [P, QKV], F32, att)
        a_xn = sb("a_xn", [P, 2, C], F32, att)
        a_xT = sb("a_xT", [P, 2, C], F32, att)
        a_qkv = sb("a_qkv", [P, T, QKV], F32, att)
        a_prod = sb("a_prod", [P, 2, T * C], F32, att)
        a_s = sb("a_s", [P, T * T * H16], F32, att)
        a_p = sb("a_p", [P, T * T * H16], F32, att)
        a_max = sb("a_max", [P, T * H16], F32, att)
        a_den = sb("a_den", [P, T * H16], F32, att)
        a_rden = sb("a_rden", [P, T * H16], F32, att)
        a_o = sb("a_o", [P, T * C], F32, att)
        a_oT = sb("a_oT", [P, 2, C], F32, att)
        att.close()

        moe = ExitStack()
        w1_hi = [sb(f"w1_hi{i}", [P, CH * FF], F32R, moe) for i in range(2)]
        w1_lo = [sb(f"w1_lo{i}", [P, CH * FF], F32R, moe) for i in range(2)]
        w2_hi = [sb(f"w2_hi{i}", [P, FC * C], F32R, moe) for i in range(2)]
        w2_lo = [sb(f"w2_lo{i}", [P, FC * C], F32R, moe) for i in range(2)]
        x2 = sb("x2", [P, T * C], F32, moe)
        x2T = sb("x2T", [P, T, C], F32, moe)
        xT_hi = sb("xT_hi", [P, CH, T * P], F32R, moe)
        xT_lo = sb("xT_lo", [P, CH, T * P], F32R, moe)
        gel = sb("gel", [P, 2, BW], F32, moe)
        hid_hi = sb("hid_hi", [P, FC, BW], F32R, moe)
        hid_lo = sb("hid_lo", [P, FC, BW], F32R, moe)
        b1 = [sb(f"b1_{i}", [P, FC], F32, moe) for i in range(2)]
        b2 = [sb(f"b2_{i}", [P, C], F32, moe) for i in range(2)]
        gam = [sb(f"gam{i}", [P, C], F32, moe) for i in range(2)]
        beta = sb("beta", [E, C], F32, moe)
        w_rt = sb("w_rt", [P, CH, E], F32, moe)
        lg = sb("lg", [P, T, E], F32, moe)
        top = sb("top", [P, T, 8], F32, moe)
        topi = sb("topi", [P, T, 8], U32, moe)
        topf = sb("topf", [P, T, 2], F32, moe)
        tw = sb("tw", [P, T, 2], F32, moe)
        te = sb("te", [P, T, 2], F32, moe)
        tsum = sb("tsum", [P, T], F32, moe)
        trec = sb("trec", [P, T], F32, moe)
        hot = sb("hot", [P, 2, T, E], F32, moe)
        gates = sb("gates", [P, T, E], F32, moe)
        gat_e = sb("gat_e", [P, E * T], F32, moe)
        gT = sb("gT", [E, T, P], F32, moe)
        xb = sb("xb", [P, BT * C], F32, moe)
        res = sb("res", [P, BT * C], F32, moe)
        nr = sb("nr", [P, 2, BT * C], F32, moe)
        gm = sb("gm", [P, BT * C], F32, moe)
        bst = sb("bst", [P, BT, 6], F32, moe)
        bmv = sb("bmv", [P, BT, 2], F32, moe)
        bve = sb("bve", [P, BT], F32, moe)
        brs = sb("brs", [P, BT], F32, moe)
        bsc = sb("bsc", [P, BT], F32, moe)
        moe.close()

        lora = ExitStack()
        z_w = sb("z_w", [P, CH, ZW], F32, lora)
        z_b = sb("z_b", [LOW, C], F32, lora)
        z_base = sb("z_base", [P, CH, C], F32, lora)
        z_rows = sb("z_rows", [P, C + E6], F32, lora)
        z_xn = sb("z_xn", [P, 2, C], F32, lora)
        z_xT = sb("z_xT", [P, T, C], F32, lora)
        z = sb("z", [P, T, ZW], F32, lora)
        z_s = sb("z_s", [P, T, LOW], F32, lora)
        z_l = sb("z_l", [P, T, E6], F32, lora)
        z_max = sb("z_max", [P, T], F32, lora)
        z_p = sb("z_p", [P, T, E6], F32, lora)
        z_g = sb("z_g", [P, T, 8], F32, lora)
        z_top = sb("z_top", [P, T, 8], F32, lora)
        z_topi = sb("z_topi", [P, T, 8], U32, lora)
        z_topf = sb("z_topf", [P, T, 2], F32, lora)
        z_tw = sb("z_tw", [P, T, 2], F32, lora)
        z_sum = sb("z_sum", [P, T], F32, lora)
        z_rec = sb("z_rec", [P, T], F32, lora)
        z_hot = sb("z_hot", [P, 2, T, E6], F32, lora)
        z_sw = sb("z_sw", [P, T, E6], F32, lora)
        z_sT = sb("z_sT", [P, 2, P], F32, lora)
        z_o = sb("z_o", [P, T, C], F32, lora)
        lora.close()

        block = ctx.enter_context(nc.Block())

        def phase(eng, n):
            eng.drain().then_inc(sem("phase_ended"), 1)
            eng.wait_ge(sem("phase_ended"), 5 * n)

        def mm3(pe, dst, a, b, start, stop):
            pe.matmul(dst, a[0], b[0], start=start, stop=False)
            pe.matmul(dst, a[0], b[1], start=False, stop=False)
            return pe.matmul(dst, a[1], b[0], start=False, stop=stop)

        def mm_rows(pe, dst, aT, w, a, b):
            for c in range(CH):
                last = pe.matmul(dst, aT[:, c * P:(c + 1) * P], w[:, c, a:b], start=(c == 0), stop=(c == CH - 1))
            return last

        def turn(pe, dst, src):
            for c in range(CH):
                last = pe.transpose(dst[:, c * P:(c + 1) * P], src[:, c * P:(c + 1) * P], ident[:, :])
            return last

        class Chain:

            def __init__(self, eng, name):
                self.eng, self.sem, self.n = eng, sem(name), 0

            def __call__(self, ins):
                ins.then_inc(self.sem, 1)
                self.n += 1
                self.eng.wait_ge(self.sem, self.n)

        LN = ["class", "attention 0", "experts", "attention 1", "low rank"]

        def ln_place(which):
            return NW + LN.index(which), 1 - LN.index(which) % 2

        def inverse_std(pool, n, i=0):
            pool.wait_ge(sem("var_made"), n + 1)
            pool.tensor_tensor(rstd[i][:, :], veps[i][:, :], mhalf[:, :], ALU.pow).then_inc(sem("rstd_made"), 1)

        def shift_of(dve, n, i=0):
            dve.wait_ge(sem("rstd_made"), n + 1)
            dve.scalar_tensor_tensor(out=nmr[i][:, :], in0=mv[i][:, :, 0], scalar=-1.0, in1=rstd[i][:, :],
                                     op0=ALU.mult, op1=ALU.mult).then_inc(sem("nmr_made"), 1)

        def tile_stats(dve, which, t, src):
            n, i = ln_place(which)
            dve.bn_stats(stats[i][:, t, :], src).then_inc(sem(f"stats_made{i}"), 1)
            dve.wait_ge(sem(f"stats_made{i}"), T * stats_before(which) + t + 1)
            dve.tensor_copy(spare[:, 0:1], spare[:, 1:2]).then_inc(sem("spacer"), 1)
            dve.bn_aggr(mv[i][:, t, :], stats[i][:, t, :]).then_inc(sem(f"aggr_made{i}"), 1)

        def stats_before(which):
            return (0, NW, 1, NW + 1, 2)[LN.index(which)]

        def end_stats(dve, which):
            n, i = ln_place(which)
            dve.wait_ge(sem(f"aggr_made{i}"), T * (stats_before(which) + 1))
            dve.tensor_scalar(veps[i][:, :], mv[i][:, :, 1], 1e-5, None, ALU.add).then_inc(sem("var_made"), 1)
            shift_of(dve, n, i)

        def normalized_scales(act, which):
            act.wait_ge(sem("nmr_made"), NW + LN.index(which) + 1)

        def normalize(act, dst, src, t, i=0):
            return act.activation(dst, src, ACT.Identity, scale=rstd[i][:, t:t + 1], bias=nmr[i][:, t:t + 1])

        def affine(act, dst, src, v, name):
            for c in range(CH):
                act.activation(dst[:, c * P:(c + 1) * P], src[:, c * P:(c + 1) * P], ACT.Identity,
                               scale=vecs[:, v + c:v + c + 1], bias=vecs[:, v + 2 + c:v + 3 + c]).then_inc(sem(name), 1)

        def load_x(sp, n, g):
            if n > 0:
                sp.wait_ge(sem("x_lo_made"), NP * (n - 1) + GRP * g + GRP)
            a, b = GRP * g, GRP * g + GRP
            sp.dma_start(xraw[:, a:b, 0:4, :], d["x_main"][bass.ds(n * P, P), a * 512:b * 512]
                         .rearrange("p (k c b) -> p k c b", k=GRP, c=4)).then_inc(sem(f"x_loaded{g}"), 16)
            sp.dma_start(xraw[0:KREST, a:b, 4, :], d["x_rest"][bass.ds(n * KREST, KREST), a * P:b * P]
                         .rearrange("p (k b) -> p k b", k=GRP)).then_inc(sem(f"x_loaded{g}"), 16)

        def split_x_hi(act, n, k):
            act.wait_ge(sem(f"x_loaded{k // GRP}"), 32 * (n + 1))
            if n > 0:
                act.wait_ge(sem("conv_done"), NP * (n - 1) + k + 1)
            act.activation(x_hi[:, k, :], xraw[:, k].rearrange("p c b -> p (c b)"), ACT.Copy)\
               .then_inc(sem("x_hi_made"), 1)

        def split_x_lo(pool, n, k):
            pool.wait_ge(sem("x_hi_made"), NP * n + k + 1)
            pool.tensor_tensor(x_lo[:, k, :], xraw[:, k].rearrange("p c b -> p (c b)"), x_hi[:, k, :],
                               ALU.subtract).then_inc(sem("x_lo_made"), 1)

        def conv(pe, n, k):
            if n > 0 or k >= 2:
                pe.wait_ge(sem("pe_copied"), NP * n + k + 1 - earlier(k, NP))
            pe.wait_ge(sem("x_lo_made"), NP * n + k + 1)
            for c in range(KC):
                a = [x[:, k, c * P:(c + 1) * P] for x in (x_hi, x_lo)]
                last = mm3(pe, bank(k % 2), a, (wc_hi[:, c, :], wc_lo[:, c, :]), c == 0, c == KC - 1)
            last.then_inc(sem("conv_done"), 1)

        def copy_pe(act, n, k):
            if n > 0:
                act.wait_ge(sem("xn_made"), NP * (n - 1) + k + 1)
                act.wait_ge(sem("summed"), (NP - 1) * n)
            act.wait_ge(sem("conv_done"), NP * n + k + 1)
            act.activation(pe_sb[:, k * C:(k + 1) * C], bank(k % 2), ACT.Copy).then_inc(sem("pe_copied"), 1)

        def measure(dve, n, k):
            dve.wait_ge(sem("pe_copied"), NP * n + k + 1)
            dve.bn_stats(stats[0][:, k, :], pe_sb[:, k * C:(k + 1) * C]).then_inc(sem("stats_made0"), 1)
            if k:
                dve.bn_aggr(mv[0][:, k - 1, :], stats[0][:, k - 1, :]).then_inc(sem("aggr_made0"), 1)
            if k > 1:
                dve.wait_ge(sem("summed"), (NP - 1) * n + k - 1)
            if k:
                dve.tensor_tensor(red_sum[:, :], pe_sb[:, 0:C] if k == 1 else red_sum[:, :],
                                  pe_sb[:, k * C:(k + 1) * C], ALU.add).then_inc(sem("summed"), 1)
            dve.wait_ge(sem("stats_made0"), T * n + k + 1)

        def reduce_window(dve, n):
            if n > 0:
                dve.wait_ge(sem("redn_made"), n)
            dve.wait_ge(sem("summed"), (NP - 1) * (n + 1))
            dve.tensor_scalar(red[:, :], red_sum[:, :], 1.0 / NP, None, ALU.mult).then_inc(sem("red_made"), 1)
            dve.bn_aggr(mv[0][:, NP - 1, :], stats[0][:, NP - 1, :]).then_inc(sem("aggr_made0"), 1)
            dve.wait_ge(sem("red_made"), n + 1)
            dve.bn_stats(stats[0][:, NP, :], red[:, :]).then_inc(sem("stats_made0"), 1)
            dve.wait_ge(sem("stats_made0"), T * (n + 1))
            dve.tensor_tensor(local[:, bass.ds(n * C, C)], red[:, :], rows[:, 0:C], ALU.add).then_inc(sem("residual_made"), 1)
            dve.bn_aggr(mv[0][:, NP, :], stats[0][:, NP, :]).then_inc(sem("aggr_made0"), 1)
            dve.wait_ge(sem("aggr_made0"), T * (n + 1))
            dve.tensor_scalar(veps[0][:, :], mv[0][:, :, 1], 1e-5, None, ALU.add).then_inc(sem("var_made"), 1)

        def normalize_patch(act, n, k):
            act.wait_ge(sem("nmr_made"), n + 1)
            if n > 0:
                act.wait_ge(sem("xT_done"), NP * (n - 1) + k + 1)
            normalize(act, xn[:, k * C:(k + 1) * C], pe_sb[:, k * C:(k + 1) * C], k).then_inc(sem("xn_made"), 1)

        def turn_patch(pe, n, k):
            pe.wait_ge(sem("xn_made"), NP * n + k + 1)
            if n > 0 or k >= 2:
                pe.wait_ge(sem("xg_lo_made"), NP * n + k + 1 - earlier(k, NP))
            turn(pe, bank(2 + k % 2), xn[:, k * C:(k + 1) * C]).then_inc(sem("xT_done"), 1)

        def split_xT_hi(act, n, k):
            if n > 0 or k >= 2:
                act.wait_ge(sem("kv_done"), NP * n + k + 1 - earlier(k, NP))
            act.wait_ge(sem("xT_done"), NP * n + k + 1)
            act.activation(xg_hi[:, k % 2, :], bank(2 + k % 2), ACT.Copy).then_inc(sem("xg_hi_made"), 1)

        def split_xT_lo(dve, n, k):
            dve.wait_ge(sem("xg_hi_made"), NP * n + k + 1)
            dve.tensor_tensor(xg_lo[:, k % 2, :], bank(2 + k % 2), xg_hi[:, k % 2, :], ALU.subtract)\
               .then_inc(sem("xg_lo_made"), 1)

        def project_kv(pe, n, k):
            pe.wait_ge(sem("xg_lo_made"), NP * n + k + 1)
            if n > 0 or k >= 2:
                pe.wait_ge(sem("kv_copied"), NP * n + k + 1 - earlier(k, NP))
            dst = bank(4 + k % 2, 0, 512)
            for c in range(CH):
                a = [x[:, k % 2, c * P:(c + 1) * P] for x in (xg_hi, xg_lo)]
                last = mm3(pe, dst, a, (wkv_hi[:, c, :], wkv_lo[:, c, :]), c == 0, c == CH - 1)
            last.then_inc(sem("kv_done"), 1)

        def copy_kv(act, n, k):
            if n > 0:
                act.wait_ge(sem("vprod_made"), n)
            act.wait_ge(sem("kv_done"), NP * n + k + 1)
            act.activation(kv_sb[:, k, :], bank(4 + k % 2, 0, 512), ACT.Copy).then_inc(sem("kv_copied"), 1)

        def normalize_red(act, n):
            act.wait_ge(sem("nmr_made"), n + 1)
            if n > 0:
                act.wait_ge(sem("redT_done"), n)
            normalize(act, redn[:, :], red[:, :], NP).then_inc(sem("redn_made"), 1)

        def turn_red(pe, n):
            pe.wait_ge(sem("redn_made"), n + 1)
            turn(pe, bank(6), redn).then_inc(sem("redT_done"), 1)

        def affine_red(act, n):
            if n > 0:
                act.wait_ge(sem("q_done"), n)
            act.wait_ge(sem("redT_done"), n + 1)
            affine(act, redT, bank(6), LAQ, "redT_made")

        def project_q(pe, n):
            pe.wait_ge(sem("redT_made"), CH * (n + 1))
            mm_rows(pe, bank(7), redT, w_q, 0, C).then_inc(sem("q_done"), 1)

        def copy_q(act, n):
            act.wait_ge(sem("q_done"), n + 1)
            if n > 0:
                act.wait_ge(sem("score_made"), n)
            act.activation(q_sb[:, :], bank(7), ACT.Copy, scale=C ** -0.5).then_inc(sem("q_made"), 1)

        def by_head(x):
            return x[:, 0:NP * H8].rearrange("p (k h) -> p h k", k=NP)

        def by_key(x, slots=NP):
            return x[:, 0:slots * H8].rearrange("p (k h) -> p k h", k=slots)

        def over_keys(x):
            return x.unsqueeze(1).broadcast_to([P, NP, H8])

        def slots_of(n):
            return NP + 1 if n < NW else NP

        def score(dve, n):
            ns = slots_of(n)
            dve.wait_ge(sem("kv_copied"), NP * (n + 1))
            dve.wait_ge(sem("q_made"), n + 1)
            dve.tensor_tensor(prod[:, 0:ns * C].rearrange("p (k c) -> p k c", k=ns), kv_sb[:, 0:ns, 0:C],
                              q_sb[:, :].unsqueeze(1).broadcast_to([P, ns, C]), ALU.mult).then_inc(sem("score_link"), 1)
            dve.wait_ge(sem("score_link"), 4 * n + 1)
            dve.tensor_reduce(sc[:, 0:ns * H8], prod[:, 0:ns * C].rearrange("p (x d) -> p x d", d=DH8), AX, ALU.add)\
               .then_inc(sem("score_link"), 1)
            dve.wait_ge(sem("score_link"), 4 * n + 2)
            links = 2
            if n < NW:
                dve.tensor_tensor(by_key(sc), by_key(sc), over_keys(sc[:, NP * H8:]), ALU.add)\
                   .then_inc(sem("score_link"), 1)
                dve.wait_ge(sem("score_link"), 4 * n + 3)
                links = 3
            dve.tensor_reduce(smax[:, :], by_head(sc), AX, ALU.max).then_inc(sem("score_link"), 1)
            dve.wait_ge(sem("score_link"), 4 * n + links + 1)
            dve.tensor_tensor(by_key(sc), by_key(sc), over_keys(smax[:, :]), ALU.subtract).then_inc(sem("score_made"), 1)

        def weigh(dve, n):
            dve.wait_ge(sem("exp_made"), n + 1)
            dve.tensor_reduce(den[:, :], by_head(pr), AX, ALU.add).then_inc(sem("weigh_link"), 1)
            dve.wait_ge(sem("weigh_link"), 2 * n + 1)
            dve.reciprocal(rden[:, :], den[:, :]).then_inc(sem("weigh_link"), 1)
            dve.wait_ge(sem("weigh_link"), 2 * n + 2)
            dve.tensor_tensor(by_key(attn), by_key(pr), over_keys(rden[:, :]), ALU.mult).then_inc(sem("attn_made"), 1)

        def value_prod(pool, n):
            ns = slots_of(n)
            pool.wait_ge(sem("attn_made"), n + 1)
            pool.tensor_tensor(vprod[:, 0:ns * C].rearrange("p (k h d) -> p k h d", k=ns, d=DH8),
                               kv_sb[:, 0:ns, C:2 * C].rearrange("p k (h d) -> p k h d", d=DH8),
                               by_key(attn, ns).unsqueeze(3).broadcast_to([P, ns, H8, DH8]), ALU.mult)\
                .then_inc(sem("vprod_made"), 1)

        def aggregate(dve, n):
            ns = slots_of(n)
            dve.wait_ge(sem("vprod_made"), n + 1)
            if n > 0:
                dve.wait_ge(sem("aggT_done"), n)
            dve.tensor_reduce(agg[:, :], vprod[:, 0:ns * C].rearrange("p (k c) -> p c k", k=ns), AX, ALU.add)\
               .then_inc(sem("agg_made"), 1)

        def exponent(act, n):
            act.wait_ge(sem("score_made"), n + 1)
            act.activation(pr[:, :], sc[:, 0:NP * H8], ACT.Exp).then_inc(sem("exp_made"), 1)

        def turn_agg(pe, n):
            pe.wait_ge(sem("agg_made"), n + 1)
            if n < NW - 1:
                pe.wait_ge(sem("redT_made"), CH * (n + 2))
            else:
                pe.wait_ge(sem("aggT_copied"), n)
            turn(pe, bank(6), agg).then_inc(sem("aggT_done"), 1)

        def copy_aggT(act, n):
            act.wait_ge(sem("aggT_done"), n + 1)
            if n > 0:
                act.wait_ge(sem("proj_done"), n)
            act.activation(aggT[:, :], bank(6), ACT.Copy).then_inc(sem("aggT_copied"), 1)

        def project_agg(pe, n):
            pe.wait_ge(sem("aggT_copied"), n + 1)
            if n < NW - 1:
                pe.wait_ge(sem("q_made"), n + 2)
            else:
                pe.wait_ge(sem("local_made"), n)
            mm_rows(pe, bank(7), aggT, w_proj, 0, C).then_inc(sem("proj_done"), 1)

        def add_local(dve, n):
            dve.wait_ge(sem("residual_made"), n + 1)
            dve.wait_ge(sem("proj_done"), n + 1)
            dve.tensor_tensor(local[:, bass.ds(n * C, C)], bank(7), local[:, bass.ds(n * C, C)], ALU.add)\
               .then_inc(sem("local_made"), 1)

        def round_pe(pe, n, first, last):
            if not last:
                for k in range(NP):
                    conv(pe, n + 1, k)
            for k in range(NP):
                turn_patch(pe, n, k)
                if k:
                    project_kv(pe, n, k - 1)
                if k == 1:
                    turn_red(pe, n)
                if k == 3:
                    project_q(pe, n)
                if not first and k == 5:
                    turn_agg(pe, n - 1)
                if not first and k == 7:
                    project_agg(pe, n - 1)
            project_kv(pe, n, NP - 1)

        EARLY = 5

        def round_act(act, n, first, last, second_last):
            normalize_red(act, n)
            for k in range(NP):
                normalize_patch(act, n, k)
                if not last:
                    if k < NP - EARLY:
                        split_x_hi(act, n + 1, EARLY + k)
                    if k:
                        copy_pe(act, n + 1, k - 1)
                if not first and k == 5:
                    exponent(act, n - 1)
            if not last:
                copy_pe(act, n + 1, NP - 1)
            for k in range(NP):
                split_xT_hi(act, n, k)
                if k == 1:
                    affine_red(act, n)
                if k == 3:
                    copy_q(act, n)
                if not first and k == 5:
                    copy_aggT(act, n - 1)
                if k:
                    copy_kv(act, n, k - 1)
                if not (last or second_last) and k < EARLY:
                    split_x_hi(act, n + 2, k)
            copy_kv(act, n, NP - 1)

        def round_pool(pool, n, first, last, second_last):
            if not last:
                for k in range(EARLY, NP):
                    split_x_lo(pool, n + 1, k)
            if not first:
                value_prod(pool, n - 1)
            if not (last or second_last):
                split_x_lo(pool, n + 2, 0)
            if not last:
                pool.wait_ge(sem("xn_made"), NP * (n + 1))
                pool.wait_ge(sem("redn_made"), n + 1)
                inverse_std(pool, n + 1)
            if not (last or second_last):
                for k in range(1, EARLY):
                    split_x_lo(pool, n + 2, k)

        def round_dve(dve, n, first, last):
            if not first:
                score(dve, n - 1)
            for k in range(NP):
                if not last:
                    measure(dve, n + 1, k)
                if not first and k == 3:
                    weigh(dve, n - 1)
            for k in range(NP):
                split_xT_lo(dve, n, k)
                if not last and k == 0:
                    reduce_window(dve, n + 1)
                if not last and k == 5:
                    shift_of(dve, n + 1)
                if not first and k == 2:
                    aggregate(dve, n - 1)
                if not first and k == 7:
                    add_local(dve, n - 1)
                if not first and k == 8:
                    local_stats(dve, n - 1)

        def pe_global(pe):
            def turns(s):
                pe.wait_ge(sem("ga_xn_made"), s + 1)
                if s >= 2:
                    pe.wait_ge(sem("gnT_made"), CH * (s - 1))
                turn(pe, bank(2 + s % 2), redn[:, :] if s == 0 else xn[:, (s - 1) * C:s * C]).then_inc(sem("ga_turned"), 1)
                if s:
                    pe.wait_ge(sem("local_made"), NW)
                    if s >= 3:
                        pe.wait_ge(sem("localT_made"), s - 2)
                    turn(pe, bank(s % 2), local[:, (s - 1) * C:s * C]).then_inc(sem("local_turned"), 1)

            turns(0)
            for s in range(1 + NW):
                if s < NW:
                    turns(s + 1)
                pe.wait_ge(sem("gnT_made"), CH * (s + 1))
                if s == 0:
                    mm_rows(pe, bank(4), gnT[:, 0, :], w_gq, 0, C).then_inc(sem("q_done"), 1)
                    continue
                if s == 2:
                    pe.wait_ge(sem("q_made"), NW + 1)
                elif s >= 3:
                    pe.wait_ge(sem("kv_copied"), NP * NW + s - 2)
                mm_rows(pe, bank(4 + s % 2, 0, 2 * C), gnT[:, s % 2, :], w_gkv, 0, 2 * C).then_inc(sem("kv_done"), 1)
                pe.wait_ge(sem("localT_made"), s)
                if s >= 3:
                    pe.wait_ge(sem("patch_made"), s - 2)
                mm_rows(pe, bank(6 + s % 2), localT[:, s % 2, :], w_mod, 0, C).then_inc(sem("mod_done"), 1)
            pe.wait_ge(sem("agg_made"), NW + 1)
            pe.wait_ge(sem("patch_made"), NW)
            turn(pe, bank(6), agg).then_inc(sem("aggT_done"), 1)
            pe.wait_ge(sem("aggT_copied"), NW + 1)
            mm_rows(pe, bank(7), aggT, w_gproj, 0, C).then_inc(sem("proj_done"), 1)

        def act_global(act):
            normalized_scales(act, "class")
            act.wait_ge(sem("redT_done"), NW)
            normalize(act, redn[:, :], rows[:, 3 * C:4 * C], NW, 1).then_inc(sem("ga_xn_made"), 1)

            def norm(s):
                normalize(act, xn[:, (s - 1) * C:s * C], local[:, (s - 1) * C:s * C], s - 1, 1).then_inc(sem("ga_xn_made"), 1)

            norm(1)
            for s in range(1 + NW):
                act.wait_ge(sem("ga_turned"), s + 1)
                if s == 2:
                    act.wait_ge(sem("q_done"), NW + 1)
                elif s >= 3:
                    act.wait_ge(sem("kv_done"), NP * NW + s - 2)
                affine(act, gnT[:, s % 2, :], bank(2 + s % 2), GAQ if s == 0 else GAKV, "gnT_made")
                if s + 2 <= NW:
                    norm(s + 2)
                if s == 1:
                    copy_q_global(act)
                if s >= 2:
                    copy_gkv(act, s - 1)
            copy_gkv(act, NW)
            exponent(act, NW)
            copy_aggT(act, NW)

        def copy_q_global(act):
            act.wait_ge(sem("q_done"), NW + 1)
            act.wait_ge(sem("vprod_made"), NW)
            act.activation(q_sb[:, :], bank(4), ACT.Copy, scale=C ** -0.5).then_inc(sem("q_made"), 1)

        def copy_gkv(act, s):
            act.wait_ge(sem("kv_done"), NP * NW + s)
            act.activation(kv_sb[:, s - 1, :], bank(4 + s % 2, 0, 2 * C), ACT.Copy).then_inc(sem("kv_copied"), 1)

        def local_stats(dve, n):
            dve.wait_ge(sem("local_made"), n + 1)
            tile_stats(dve, "class", n, local[:, n * C:(n + 1) * C])

        def dve_global(dve):
            local_stats(dve, NW - 1)
            tile_stats(dve, "class", NW, rows[:, 3 * C:4 * C])
            end_stats(dve, "class")
            for s in range(1, 1 + NW):
                dve.wait_ge(sem("local_turned"), s)
                if s >= 3:
                    dve.wait_ge(sem("mod_done"), s - 2)
                dve.tensor_copy(localT[:, s % 2, :], bank(s % 2)).then_inc(sem("localT_made"), 1)
                if s >= 2:
                    patch_out(dve, s - 1)
            patch_out(dve, NW)
            score(dve, NW)
            weigh(dve, NW)
            aggregate(dve, NW)
            dve.tensor_tensor(redT[:, :], rows[:, 2 * C:3 * C], rows[:, 3 * C:4 * C], ALU.add).then_inc(sem("cls_bias"), 1)
            dve.wait_ge(sem("cls_bias"), 1)
            dve.wait_ge(sem("proj_done"), NW + 1)
            dve.tensor_tensor(h_at(NW), bank(7), redT[:, :], ALU.add).then_inc(sem("patch_made"), 1)
            dve.wait_ge(sem("patch_made"), NW + 1)
            tile_stats(dve, "attention 0", NW, h_at(NW))

        def patch_out(dve, s):
            dve.wait_ge(sem("mod_done"), s)
            dve.tensor_tensor(h_at(s - 1), bank(6 + s % 2), rows[:, C:2 * C], ALU.add).then_inc(sem("patch_made"), 1)
            dve.wait_ge(sem("patch_made"), s)
            tile_stats(dve, "attention 0", s - 1, h_at(s - 1))

        ENDS = {"w_loaded": 48, "qkv_made": 2 * T, "pool_prod_made": 12, "pool_prod_used": 12,
                "s_made": 1, "exp_made": 1, "p_made": 1}

        def seen(layer, name, count):
            return count + layer * ENDS.get(name, T)

        def keys(layer, t):
            return T if layer == 0 else t + 1

        def on_pool(layer, t):
            return t % 2 == 1 or t == 4

        def of_query(x, t, layer, ns):
            return x[:, t * T * H16:(t * T + ns) * H16]

        def score_products(eng, layer, t, dst):
            ns = keys(layer, t)
            return eng.tensor_tensor(dst[:, 0:ns * C].rearrange("p (s c) -> p s c", s=ns), a_qkv[:, 0:ns, C:2 * C],
                                     a_qkv[:, t, 0:C].unsqueeze(1).broadcast_to([P, ns, C]), ALU.mult)

        def value_products(eng, layer, t, dst):
            ns = keys(layer, t)
            return eng.tensor_tensor(dst[:, 0:ns * C].rearrange("p (s h d) -> p s h d", s=ns, d=D16),
                                     a_qkv[:, 0:ns, 2 * C:3 * C].rearrange("p s (h d) -> p s h d", d=D16),
                                     of_query(a_p, t, layer, ns).rearrange("p (s h) -> p s h", s=ns).unsqueeze(3)
                                     .broadcast_to([P, ns, H16, D16]), ALU.mult)

        def pool_attention(pool, layer):
            inverse_std(pool, *ln_place(f"attention {layer}"))
            n = 0
            for make, ready in ((score_products, False), (value_products, True)):
                if ready:
                    pool.wait_ge(sem("a_p_made"), seen(layer, "p_made", 1))
                for t in range(T):
                    if on_pool(layer, t):
                        if not ready:
                            pool.wait_ge(sem("a_qkv_made"), seen(layer, "qkv_made", 2 * keys(layer, t)))
                        if n:
                            pool.wait_ge(sem("a_pool_prod_used"), seen(layer, "pool_prod_used", n))
                        make(pool, layer, t, a_prod[:, 1, :]).then_inc(sem("a_pool_prod_made"), 1)
                        n += 1

        def pe_attention(pe, layer):
            w, wo = a_w[layer], a_wo[layer]
            pe.wait_ge(sem("a_w_loaded"), seen(layer, "w_loaded", 48 if layer == 0 else 32))
            def turn_x(t):
                pe.wait_ge(sem("a_xn_made"), seen(layer, "xn_made", t + 1))
                if t >= 2:
                    pe.wait_ge(sem("a_xT_made"), seen(layer, "xT_made", t - 1))
                turn(pe, bank(t % 2), a_xn[:, t % 2, :]).then_inc(sem("a_turned"), 1)

            def turn_o(t):
                pe.wait_ge(sem("a_o_made"), seen(layer, "o_made", t + 1))
                if t >= 2:
                    pe.wait_ge(sem("a_oT_made"), seen(layer, "oT_made", t - 1))
                turn(pe, bank(t % 2), a_o[:, t * C:(t + 1) * C]).then_inc(sem("a_o_turned"), 1)

            turn_x(0)
            for t in range(T):
                if t + 1 < T:
                    turn_x(t + 1)
                pe.wait_ge(sem("a_xT_made"), seen(layer, "xT_made", t + 1))
                if t >= 2:
                    pe.wait_ge(sem("a_qkv_made"), seen(layer, "qkv_made", 2 * (t - 1)))
                mm_rows(pe, bank(2 + t % 2, 0, 2 * C), a_xT[:, t % 2, :], w, 0, 2 * C)
                mm_rows(pe, bank(4 + t % 2), a_xT[:, t % 2, :], w, 2 * C, 3 * C).then_inc(sem("a_qkv_done"), 1)
            for t in range(T):
                turn_o(t)
                pe.wait_ge(sem("a_oT_made"), seen(layer, "oT_made", t + 1))
                if t >= 2:
                    pe.wait_ge(sem("a_h_made"), seen(layer, "h_made", t - 1))
                mm_rows(pe, bank(6 + t % 2), a_oT[:, t % 2, :], wo, 0, C).then_inc(sem("a_o_done"), 1)

        def act_attention(act, layer):
            normalized_scales(act, f"attention {layer}")

            def norm(t):
                if t >= 2:
                    act.wait_ge(sem("a_turned"), seen(layer, "turned", t - 1))
                normalize(act, a_xn[:, t % 2, :], h_at(t), t).then_inc(sem("a_xn_made"), 1)

            norm(0)
            norm(1)
            for t in range(T):
                act.wait_ge(sem("a_turned"), seen(layer, "turned", t + 1))
                if t >= 2:
                    act.wait_ge(sem("a_qkv_done"), seen(layer, "qkv_done", t - 1))
                act.activation(a_xT[:, t % 2, :], bank(t % 2), ACT.Copy).then_inc(sem("a_xT_made"), 1)
                if t + 2 < T:
                    norm(t + 2)
                if layer == 1 and t:
                    copy_qkv(act, t - 1)
            if layer == 1:
                copy_qkv(act, T - 1)
            act.wait_ge(sem("a_s_made"), seen(layer, "s_made", 1))
            act.activation(a_p[:, :], a_s[:, :], ACT.Exp, scale=D16 ** -0.5).then_inc(sem("a_exp_made"), 1)
            for t in range(T):
                act.wait_ge(sem("a_o_turned"), seen(layer, "o_turned", t + 1))
                if t >= 2:
                    act.wait_ge(sem("a_o_done"), seen(layer, "o_done", t - 1))
                act.activation(a_oT[:, t % 2, :], bank(t % 2), ACT.Copy).then_inc(sem("a_oT_made"), 1)

        def copy_qkv(act, t):
            act.wait_ge(sem("a_qkv_done"), seen(1, "qkv_done", t + 1))
            act.activation(a_qkv[:, t, 0:2 * C], bank(2 + t % 2, 0, 2 * C), ACT.Copy).then_inc(sem("a_qkv_made"), 1)
            act.activation(a_qkv[:, t, 2 * C:3 * C], bank(4 + t % 2), ACT.Copy).then_inc(sem("a_qkv_made"), 1)

        def dve_attention(dve, layer):
            link = Chain(dve, f"a{layer}_link")
            end_stats(dve, f"attention {layer}")
            if layer == 0:
                dve.wait_ge(sem("a_w_loaded"), seen(layer, "w_loaded", 48))
                for t in range(T):
                    dve.wait_ge(sem("a_qkv_done"), seen(layer, "qkv_done", t + 1))
                    dve.tensor_tensor(a_qkv[:, t, 0:2 * C], bank(2 + t % 2, 0, 2 * C), a_bias[:, 0:2 * C], ALU.add)\
                       .then_inc(sem("a_qkv_made"), 1)
                    dve.tensor_tensor(a_qkv[:, t, 2 * C:3 * C], bank(4 + t % 2), a_bias[:, 2 * C:3 * C], ALU.add)\
                       .then_inc(sem("a_qkv_made"), 1)
            else:
                link(dve.memset(a_s[:, :], NEG4))
            pooled = 0
            for t in range(T):
                dve.wait_ge(sem("a_qkv_made"), seen(layer, "qkv_made", 2 * keys(layer, t)))
                ns = keys(layer, t)
                slot = a_prod[:, int(on_pool(layer, t)), 0:ns * C]
                if on_pool(layer, t):
                    pooled += 1
                    dve.wait_ge(sem("a_pool_prod_made"), seen(layer, "pool_prod_made", pooled))
                else:
                    link(score_products(dve, layer, t, a_prod[:, 0, :]))
                st = of_query(a_s, t, layer, ns)
                ins = dve.tensor_reduce(st, slot.rearrange("p (x d) -> p x d", d=D16), AX, ALU.add)
                if on_pool(layer, t):
                    ins.then_inc(sem("a_pool_prod_used"), 1)
                    dve.wait_ge(sem("a_pool_prod_used"), seen(layer, "pool_prod_used", pooled))
                else:
                    link(ins)
                if layer == 1:
                    link(dve.tensor_scalar(st, st, -40.0, 40.0, ALU.max, ALU.min))
            s4 = a_s[:, :].rearrange("p (t s h) -> p t s h", t=T, s=T)
            p4 = a_p[:, :].rearrange("p (t s h) -> p t s h", t=T, s=T)
            if layer == 0:
                link(dve.memset(s4[:, 0, T - 1, :], NEG4))
                link(dve.memset(s4[:, T - 1, 0, :], NEG4))
            th = lambda x: x[:, :].rearrange("p (t h) -> p t h", t=T)
            over_s = lambda x: th(x).unsqueeze(2).broadcast_to([P, T, T, H16])
            link(dve.tensor_reduce(th(a_max), s4.rearrange("p t s h -> p t h s"), AX, ALU.max))
            dve.tensor_tensor(s4, s4, over_s(a_max), ALU.subtract).then_inc(sem("a_s_made"), 1)
            dve.wait_ge(sem("a_exp_made"), seen(layer, "exp_made", 1))
            link(dve.tensor_reduce(th(a_den), p4.rearrange("p t s h -> p t h s"), AX, ALU.add))
            link(dve.reciprocal(a_rden[:, :], a_den[:, :]))
            dve.tensor_tensor(p4, p4, over_s(a_rden), ALU.mult).then_inc(sem("a_p_made"), 1)
            dve.wait_ge(sem("a_p_made"), seen(layer, "p_made", 1))
            for t in range(T):
                ns = keys(layer, t)
                slot = a_prod[:, int(on_pool(layer, t)), 0:ns * C]
                if on_pool(layer, t):
                    pooled += 1
                    dve.wait_ge(sem("a_pool_prod_made"), seen(layer, "pool_prod_made", pooled))
                else:
                    link(value_products(dve, layer, t, a_prod[:, 0, :]))
                dve.tensor_reduce(a_o[:, t * C:(t + 1) * C], slot.rearrange("p (s c) -> p c s", s=ns), AX, ALU.add)\
                   .then_inc(sem("a_o_made"), 1)
                dve.wait_ge(sem("a_o_made"), seen(layer, "o_made", t + 1))
                if on_pool(layer, t):
                    dve.sem_inc(sem("a_pool_prod_used"), 1)
                if t >= 2:
                    add_o(dve, layer, t - 2)
            add_o(dve, layer, T - 2)
            add_o(dve, layer, T - 1)

        def add_o(dve, layer, t):
            dve.wait_ge(sem("a_o_done"), seen(layer, "o_done", t + 1))
            dve.tensor_tensor(h_at(t), bank(6 + t % 2), h_at(t), ALU.add).then_inc(sem("a_h_made"), 1)
            dve.wait_ge(sem("a_h_made"), seen(layer, "h_made", t + 1))
            tile_stats(dve, "experts" if layer == 0 else "low rank", t, h_at(t))

        def top_two(dve, link, x, t8, ti, tf, count):
            for t in range(count):
                dve.max(t8[:, t, :], x[:, t, :])
            link(dve.memset(spare[:, :], 0.0))
            for t in range(count):
                dve.max_index(ti[:, t, :], t8[:, t, :], x[:, t, :])
            link(dve.memset(spare[:, :], 0.0))
            link(dve.tensor_copy(tf[:, :, :], ti[:, :, 0:2]))

        def spread(dve, link, tf, w, hots, dst, n):
            for j in range(2):
                link(dve.tensor_tensor(hots[:, j], iota[:, 0:n].unsqueeze(1).broadcast_to([P, T, n]),
                                       tf[:, :, j:j + 1].broadcast_to([P, T, n]), ALU.is_equal))
                link(dve.tensor_tensor(hots[:, j], hots[:, j], w[:, :, j:j + 1].broadcast_to([P, T, n]), ALU.mult))
            link(dve.tensor_tensor(dst[:, :, :], hots[:, 0], hots[:, 1], ALU.add))

        STEPS = 2 * NB * FC
        LAG = 2
        START = {"gelu_made": 2, "hid_made": 2, "down_made": FC, "res_made": 2, "gm_made": 2}

        def made(name, count):
            return count + START.get(name, 0)

        def where(j):
            par, r = divmod(j, NB * FC)
            b, fc = divmod(r, FC)
            return par, b, fc, par * NB + b

        def pe_experts(pe):
            pe.wait_ge(sem("moe_small_loaded"), 32)
            def turn_x2(t):
                pe.wait_ge(sem("x2_made"), t + 1)
                if t >= 2:
                    pe.wait_ge(sem("x2T_made"), t - 1)
                turn(pe, bank(t % 2), x2[:, t * C:(t + 1) * C]).then_inc(sem("x2_turned"), 1)

            turn_x2(0)
            for t in range(T):
                if t + 1 < T:
                    turn_x2(t + 1)
                pe.wait_ge(sem("x2T_made"), t + 1)
                if t >= 2:
                    pe.wait_ge(sem("lg_made"), t - 1)
                mm_rows(pe, bank(2 + t % 2, 0, E), x2T[:, t, :], w_rt, 0, E).then_inc(sem("lg_done"), 1)
            pe.wait_ge(sem("lg_made"), T)
            pe.wait_ge(sem("xT_split"), 2 * T)

            def turn_gates(t):
                pe.wait_ge(sem("gates_made"), 1)
                if t:
                    pe.wait_ge(sem("gT_made"), t)
                pe.transpose(bank(6, 0, P)[0:E, :], gates[:, t, :], ident[:, :]).then_inc(sem("g_turned"), 1)

            def times_beta(t):
                pe.wait_ge(sem("gT_made"), t + 1)
                if t:
                    pe.wait_ge(sem("beta_added"), t)
                pe.matmul(bank(7), gT[:, t, :], beta[:, :], start=True, stop=True).then_inc(sem("beta_done"), 1)

            def up(ep, j):
                par, b, fc, blk = where(j)
                if b == 0 and fc == 0:
                    pe.wait_ge(sem("w_lo_made"), PIECES * (2 * ep + par + 1))
                pe.wait_ge(sem("gelu_made"), made("gelu_made", STEPS * ep + j - 1))
                for c in range(CH):
                    at = c * FF + fc * P
                    last = mm3(pe, bank(fc % 2), (w1_hi[par][:, at:at + P], w1_lo[par][:, at:at + P]),
                               (xT_hi[:, c, b * BW:(b + 1) * BW], xT_lo[:, c, b * BW:(b + 1) * BW]), c == 0, c == CH - 1)
                last.then_inc(sem("up_done"), 1)

            def down(ep, j):
                par, b, fc, blk = where(j)
                pe.wait_ge(sem("hid_made"), made("hid_made", STEPS * ep + j + 1))
                if fc == 0:
                    pe.wait_ge(sem("res_made"), made("res_made", 2 * NB * ep + blk - 1))
                for u in range(BT):
                    last = mm3(pe, pair[1 + blk % 2][:, u, 0:C],
                               (hid_hi[:, fc, u * P:(u + 1) * P], hid_lo[:, fc, u * P:(u + 1) * P]),
                               (w2_hi[par][:, fc * C:(fc + 1) * C], w2_lo[par][:, fc * C:(fc + 1) * C]),
                               fc == 0, fc == FC - 1)
                last.then_inc(sem("down_made"), 1)

            def experts(ep):
                for j in range(STEPS):
                    par, b, fc, blk = where(j)
                    up(ep, j)
                    if j >= LAG:
                        down(ep, j - LAG)
                    if ep == 0 and par == 0 and 3 <= fc < 3 + 2 * BT:
                        (turn_gates if fc % 2 else times_beta)(BT * b + (fc - 3) // 2)
                for j in range(STEPS - LAG, STEPS):
                    down(ep, j)

            for ep in range(E // 2):
                experts(ep)

        def load_expert(sp, e):
            rows_of = slice(e * P, (e + 1) * P)
            sp.dma_start(w1raw[e % 2][:, :], d["w1"][rows_of, :]).then_inc(sem(f"w_loaded{e % 2}"), 16)
            sp.dma_start(w2raw[e % 2][:, :], d["w2"][rows_of, :]).then_inc(sem(f"w_loaded{e % 2}"), 16)

        def load_vectors(sp, e):
            par = e % 2
            sp.dma_start(b1[par][:, :], d["b1"][:, e * FC:(e + 1) * FC]).then_inc(sem(f"v_loaded{par}"), 16)
            for dst, name in ((b2, "b2"), (gam, "gamma")):
                sp.dma_start(dst[par][:, :], d[name][:, e * C:(e + 1) * C].broadcast_to([P, C]))\
                  .then_inc(sem(f"v_loaded{par}"), 16)

        def piece(j):
            r = j % (NB * FC)
            return r // 4 if r % 4 == 2 and r // 4 < PIECES else None

        def weight_piece(par, i):
            n = CH * FF * 2 // PIECES
            a = (i % 4) * n
            return [x[par][:, a:a + n] for x in ((w1raw, w1_hi, w1_lo) if i < 4 else (w2raw, w2_hi, w2_lo))]

        def split_w_hi(act, ep, par, i):
            raw, hi, _ = weight_piece(par, i)
            if i == 0:
                act.wait_ge(sem(f"w_loaded{par}"), 32 * (ep + 1))
                act.wait_ge(sem("down_made"), made("down_made", NB * FC * (2 * ep + par - 1) if not isinstance(ep, int) or 2 * ep + par > 1 else 0))
            act.activation(hi, raw, ACT.Copy).then_inc(sem("w_hi_made"), 1)

        def split_w_lo(pool, ep, par, i):
            raw, hi, lo = weight_piece(par, i)
            if i == 0:
                pool.wait_ge(sem("down_made"), made("down_made", NB * FC * (2 * ep + par - 1) if not isinstance(ep, int) or 2 * ep + par > 1 else 0))
            pool.wait_ge(sem("w_hi_made"), PIECES * (2 * ep + par) + i + 1)
            pool.tensor_tensor(lo, raw, hi, ALU.subtract).then_inc(sem("w_lo_made"), 1)

        def act_experts(act):
            act.sem_inc(sem("gelu_made"), START["gelu_made"])
            normalized_scales(act, "experts")

            def norm(t):
                normalize(act, x2[:, t * C:(t + 1) * C], h_at(t), t, 1).then_inc(sem("x2_made"), 1)

            norm(0)
            norm(1)
            for t in range(T):
                if t + 2 < T:
                    norm(t + 2)
                act.wait_ge(sem("x2_turned"), t + 1)
                act.activation(x2T[:, t, :], bank(t % 2), ACT.Copy).then_inc(sem("x2T_made"), 1)
            for i in range(PIECES):
                split_w_hi(act, 0, 0, i)
            act.wait_ge(sem("tw_made"), 1)
            act.activation(te[:, :, :], tw[:, :, :], ACT.Exp).then_inc(sem("te_made"), 1)
            def copy_gT(t):
                act.wait_ge(sem("g_turned"), t + 1)
                act.activation(gT[:, t, :], bank(6, 0, P)[0:E, :], ACT.Copy).then_inc(sem("gT_made"), 1)

            def experts(ep, end):
                for j in range(STEPS):
                    par, b, fc, blk = where(j)
                    g = STEPS * ep + j
                    if b == 0 and fc == 0:
                        act.wait_ge(sem(f"v_loaded{par}"), 48 * (ep + 1))
                    act.wait_ge(sem("hid_made"), made("hid_made", g - 1))
                    act.wait_ge(sem("up_done"), g + 1)
                    act.activation(gel[:, fc % 2, :], bank(fc % 2), ACT.Gelu,
                                   bias=b1[par][:, fc:fc + 1]).then_inc(sem("gelu_made"), 1)
                    if ep == 0 and par == 0 and fc in (3, 5):
                        copy_gT(BT * b + (fc - 3) // 2)
                    if piece(j) is not None and not (end and par == 1):
                        split_w_hi(act, ep + par, 1 - par, piece(j))

            for ep in range(E // 2):
                experts(ep, ep == E // 2 - 1)

        def pool_experts(pool):
            inverse_std(pool, *ln_place("experts"))
            pool.sem_inc(sem("gm_made"), START["gm_made"])
            for i in range(PIECES):
                split_w_lo(pool, 0, 0, i)
            pool.wait_ge(sem("x2_made"), T)

            def block_input(ep, blk):
                par, b = divmod(blk, NB)
                if b == 0:
                    pool.wait_ge(sem(f"v_loaded{par}"), 48 * (ep + 1))
                pool.wait_ge(sem("res_made"), made("res_made", 2 * NB * ep + blk))
                pool.tensor_tensor(xb[:, :].rearrange("p (u c) -> p u c", u=BT),
                                   x2[:, b * BT * C:(b + 1) * BT * C].rearrange("p (u c) -> p u c", u=BT),
                                   b2[par][:, :].unsqueeze(1).broadcast_to([P, BT, C]), ALU.add)\
                    .then_inc(sem("xb_made"), 1)

            def block_scale(ep, blk):
                pool.wait_ge(sem("bvar_made"), 2 * NB * ep + blk + 1)
                pool.tensor_tensor(brs[:, :], bve[:, :], mhalf[:, 0:BT], ALU.pow).then_inc(sem("brstd_made"), 1)

            def block_output(ep, blk):
                par, b = divmod(blk, NB)
                n = 2 * NB * ep + blk
                pool.wait_ge(sem("nr_made"), BT * (n + 1))
                pool.tensor_tensor(gm[:, :].rearrange("p (u c) -> p u c", u=BT),
                                   nr[:, blk % 2, :].rearrange("p (u c) -> p u c", u=BT),
                                   gam[par][:, :].unsqueeze(1).broadcast_to([P, BT, C]), ALU.mult)\
                    .then_inc(sem("gm_made"), 1)
                pool.wait_ge(sem("gm_made"), made("gm_made", n + 1))
                if ep == 0 and par == 0:
                    pool.wait_ge(sem("beta_added"), BT * (b + 1))
                pool.tensor_tensor(h_at(BT * b, BT), h_at(BT * b, BT), gm[:, :], ALU.add).then_inc(sem("y_added"), 1)
                pool.wait_ge(sem("y_added"), n + 1)

            def experts(ep, end):
                for blk in range(2 * NB):
                    par = blk // NB
                    todo = [piece(j) for j in range(blk * FC, (blk + 1) * FC) if piece(j) is not None]
                    if end and par == 1:
                        todo = []
                    if blk == 0:
                        block_input(ep, 0)
                    else:
                        block_scale(ep, blk - 1)
                        block_input(ep, blk)
                        block_output(ep, blk - 1)
                    for i in todo:
                        split_w_lo(pool, ep + par, 1 - par, i)
                block_scale(ep, 2 * NB - 1)
                block_output(ep, 2 * NB - 1)

            for ep in range(E // 2):
                experts(ep, ep == E // 2 - 1)

        def dve_experts(dve):
            link = Chain(dve, "moe_link")
            end_stats(dve, "experts")
            for name in ("hid_made", "res_made", "down_made"):
                dve.sem_inc(sem(name), START[name])
            for t in range(T):
                dve.wait_ge(sem("x2T_made"), t + 1)
                src = x2T[:, t, :].rearrange("p (c b) -> p c b", c=CH)
                at = slice(t * P, (t + 1) * P)
                dve.tensor_copy(xT_hi[:, :, at], src).then_inc(sem("xT_split"), 1)
                dve.wait_ge(sem("xT_split"), 2 * t + 1)
                dve.tensor_tensor(xT_lo[:, :, at], src, xT_hi[:, :, at], ALU.subtract).then_inc(sem("xT_split"), 1)
                dve.wait_ge(sem("lg_done"), t + 1)
                dve.tensor_copy(lg[:, t, :], bank(2 + t % 2, 0, E)).then_inc(sem("lg_made"), 1)
            dve.wait_ge(sem("lg_made"), T)
            top_two(dve, link, lg, top, topi, topf, T)
            dve.tensor_tensor(tw[:, :, :], top[:, :, 0:2], top[:, :, 0:1].broadcast_to([P, T, 2]), ALU.subtract)\
               .then_inc(sem("tw_made"), 1)
            dve.wait_ge(sem("te_made"), 1)
            link(dve.tensor_reduce(tsum[:, :], te[:, :, :], AX, ALU.add))
            link(dve.reciprocal(trec[:, :], tsum[:, :]))
            link(dve.tensor_tensor(tw[:, :, :], te[:, :, :], trec[:, :].unsqueeze(2).broadcast_to([P, T, 2]), ALU.mult))
            spread(dve, link, topf, tw, hot, gates, E)
            dve.tensor_copy(gat_e[:, :].rearrange("p (e t) -> p t e", e=E), gates[:, :, :]).then_inc(sem("gates_made"), 1)
            dve.wait_ge(sem("gates_made"), 1)
            def split_hidden(ep, j):
                par, b, fc, blk = where(j)
                g = STEPS * ep + j
                dve.wait_ge(sem("down_made"), made("down_made", g + 1 - FC))
                dve.wait_ge(sem("gelu_made"), made("gelu_made", g + 1))
                dve.tensor_copy(hid_hi[:, fc, :], gel[:, fc % 2, :]).then_inc(sem("hid_hi_made"), 1)
                dve.wait_ge(sem("hid_hi_made"), g + 1)
                dve.tensor_tensor(hid_lo[:, fc, :], gel[:, fc % 2, :], hid_hi[:, fc, :], ALU.subtract)\
                   .then_inc(sem("hid_made"), 1)

            def block_stats(ep, blk):
                n = 2 * NB * ep + blk
                dve.wait_ge(sem("xb_made"), n + 1)
                dve.wait_ge(sem("down_made"), made("down_made", FC * (n + 1)))
                dve.tensor_tensor(res[:, :].rearrange("p (u c) -> p u c", u=BT), pair[1 + blk % 2][:, :, 0:C],
                                  xb[:, :].rearrange("p (u c) -> p u c", u=BT), ALU.add).then_inc(sem("res_made"), 1)
                dve.wait_ge(sem("res_made"), made("res_made", n + 1))
                for u in range(BT):
                    dve.bn_stats(bst[:, u, :], res[:, u * C:(u + 1) * C]).then_inc(sem("bstats_made"), 1)
                dve.wait_ge(sem("bstats_made"), BT * (n + 1))
                dve.tensor_copy(spare[:, 0:1], spare[:, 1:2]).then_inc(sem("spacer"), 1)
                for u in range(BT):
                    dve.bn_aggr(bmv[:, u, :], bst[:, u, :]).then_inc(sem("baggr_made"), 1)
                dve.wait_ge(sem("baggr_made"), BT * (n + 1))
                dve.tensor_scalar(bve[:, :], bmv[:, :, 1], 1e-6, None, ALU.add).then_inc(sem("bvar_made"), 1)

            def block_normalize(ep, blk):
                par, b = divmod(blk, NB)
                n = 2 * NB * ep + blk
                dve.wait_ge(sem("brstd_made"), n + 1)
                dve.tensor_tensor(bsc[:, :], brs[:, :], gat_e[:, bass.ds((2 * ep + par) * T + BT * b, BT)], ALU.mult)\
                   .then_inc(sem("bscale_made"), 1)
                dve.wait_ge(sem("bscale_made"), n + 1)
                dve.wait_ge(sem("gm_made"), made("gm_made", n - 1))
                for u in range(BT):
                    dve.tensor_scalar(nr[:, blk % 2, u * C:(u + 1) * C], res[:, u * C:(u + 1) * C], bmv[:, u, 0:1],
                                      bsc[:, u:u + 1], ALU.subtract, ALU.mult).then_inc(sem("nr_made"), 1)
                dve.wait_ge(sem("nr_made"), BT * (n + 1))

            def add_beta(b):
                for t in range(BT * b, BT * b + BT):
                    dve.wait_ge(sem("beta_done"), t + 1)
                    dve.tensor_tensor(h_at(t), bank(7), h_at(t), ALU.add).then_inc(sem("beta_added"), 1)

            def finished(b):
                dve.wait_ge(sem("y_added"), NB * (E - 1) + b + 1)
                for t in range(BT * b, BT * b + BT):
                    tile_stats(dve, "attention 1", t, h_at(t))

            def experts(ep):
                for j in range(STEPS):
                    par, b, fc, blk = where(j)
                    split_hidden(ep, j)
                    if blk and fc == 2:
                        block_stats(ep, blk - 1)
                    if blk and fc == 4:
                        block_normalize(ep, blk - 1)
                    if ep == 0 and par == 0 and fc == 6:
                        add_beta(b)
                    if ep == E // 2 - 1 and par == 1 and b >= 2 and fc == 6:
                        finished(b - 2)
                block_stats(ep, 2 * NB - 1)
                block_normalize(ep, 2 * NB - 1)
                if ep == E // 2 - 1:
                    for b in (NB - 2, NB - 1):
                        finished(b)

            for ep in range(E // 2):
                experts(ep)

        def pe_lora(pe):
            pe.wait_ge(sem("z_loaded"), 64)
            def turn_z(t):
                pe.wait_ge(sem("z_xn_made"), t + 1)
                if t >= 2:
                    pe.wait_ge(sem("z_xT_made"), t - 1)
                turn(pe, bank(t % 2), z_xn[:, t % 2, :]).then_inc(sem("z_turned"), 1)

            turn_z(0)
            for t in range(T):
                if t + 1 < T:
                    turn_z(t + 1)
                pe.wait_ge(sem("z_xT_made"), t + 1)
                if t >= 2:
                    pe.wait_ge(sem("z_made"), t - 1)
                mm_rows(pe, bank(2 + t % 2, 0, ZW), z_xT[:, t, :], z_w, 0, ZW).then_inc(sem("z_done"), 1)
            for t in range(T):
                pe.wait_ge(sem("z_s_made"), t + 1)
                if t >= 2:
                    pe.wait_ge(sem("z_sT_made"), t - 1)
                pe.transpose(bank(4 + t % 2, 0, P)[0:LOW, :], z_s[:, t, :], ident[:, :]).then_inc(sem("z_s_turned"), 1)
                if t >= 2:
                    pe.wait_ge(sem("z_out_made"), t - 1)
                for c in range(CH):
                    pe.matmul(bank(6 + t % 2), z_xT[:, t, c * P:(c + 1) * P], z_base[:, c, :], start=(c == 0), stop=False)
                pe.wait_ge(sem("z_sT_made"), t + 1)
                pe.matmul(bank(6 + t % 2), z_sT[0:LOW, t % 2, :], z_b[:, :], start=False, stop=True)\
                  .then_inc(sem("z_out_done"), 1)

        def act_lora(act):
            normalized_scales(act, "low rank")
            def norm(t):
                if t >= 2:
                    act.wait_ge(sem("z_turned"), t - 1)
                normalize(act, z_xn[:, t % 2, :], h_at(t), t, 1).then_inc(sem("z_xn_made"), 1)

            norm(0)
            norm(1)
            for t in range(T):
                if t + 2 < T:
                    norm(t + 2)
                act.wait_ge(sem("z_turned"), t + 1)
                act.activation(z_xT[:, t, :], bank(t % 2), ACT.Copy).then_inc(sem("z_xT_made"), 1)
            act.wait_ge(sem("z_l_made"), 1)
            act.activation(z_p[:, :, :], z_l[:, :, :], ACT.Exp).then_inc(sem("z_exp_made"), 1)
            for t in range(T):
                act.wait_ge(sem("z_s_turned"), t + 1)
                if t >= 2:
                    act.wait_ge(sem("z_out_done"), t - 1)
                act.activation(z_sT[0:LOW, t % 2, :], bank(4 + t % 2, 0, P)[0:LOW, :], ACT.Copy).then_inc(sem("z_sT_made"), 1)

        def dve_lora(dve):
            link = Chain(dve, "z_link")
            end_stats(dve, "low rank")
            dve.wait_ge(sem("z_loaded"), 64)
            link(dve.memset(z_g[:, :, :], -1.0))
            for t in range(T):
                dve.wait_ge(sem("z_done"), t + 1)
                dve.tensor_copy(z[:, t, :], bank(2 + t % 2, 0, ZW)).then_inc(sem("z_made"), 1)
            dve.wait_ge(sem("z_made"), T)
            over = lambda x, n: x[:, :].unsqueeze(2).broadcast_to([P, T, n])
            link(dve.tensor_tensor(z_l[:, :, :], z[:, :, LOW:ZW],
                                   z_rows[:, C:C + E6].unsqueeze(1).broadcast_to([P, T, E6]), ALU.add))
            link(dve.tensor_reduce(z_max[:, :], z_l[:, :, :], AX, ALU.max))
            dve.tensor_tensor(z_l[:, :, :], z_l[:, :, :], over(z_max, E6), ALU.subtract).then_inc(sem("z_l_made"), 1)
            dve.wait_ge(sem("z_exp_made"), 1)
            link(dve.tensor_reduce(z_sum[:, :], z_p[:, :, :], AX, ALU.add))
            link(dve.reciprocal(z_rec[:, :], z_sum[:, :]))
            link(dve.tensor_tensor(z_g[:, :, 0:E6], z_p[:, :, :], over(z_rec, E6), ALU.mult))
            top_two(dve, link, z_g, z_top, z_topi, z_topf, T)
            link(dve.tensor_reduce(z_sum[:, :], z_top[:, :, 0:2], AX, ALU.add))
            link(dve.tensor_scalar(z_sum[:, :], z_sum[:, :], 1e-6, None, ALU.add))
            link(dve.reciprocal(z_rec[:, :], z_sum[:, :]))
            link(dve.tensor_tensor(z_tw[:, :, :], z_top[:, :, 0:2], over(z_rec, 2), ALU.mult))
            spread(dve, link, z_topf, z_tw, z_hot, z_sw, E6)
            for t in range(T):
                link(dve.tensor_copy(z_s[:, t, 0:R16], z[:, t, 0:R16]))
                dve.tensor_tensor(z_s[:, t, R16:LOW].rearrange("p (e r) -> p e r", e=E6),
                                  z[:, t, R16:LOW].rearrange("p (e r) -> p e r", e=E6),
                                  z_sw[:, t, :].unsqueeze(2).broadcast_to([P, E6, R16]), ALU.mult)\
                   .then_inc(sem("z_s_made"), 1)
                link(dve.tensor_tensor(h_at(t), h_at(t), z_rows[:, 0:C], ALU.add))
            for t in range(T):
                dve.wait_ge(sem("z_out_done"), t + 1)
                dve.tensor_tensor(z_o[:, t, :], bank(6 + t % 2), h_at(t), ALU.add).then_inc(sem("z_out_made"), 1)

        @block.sync
        def _(sp):
            sp.dma_start(wc_raw[:, 0:4, :], d["conv_main"].rearrange("p (c n) -> p c n", c=4)).then_inc(sem("wc_loaded"), 16)
            sp.wait_ge(sem("pads_zeroed"), 2)
            sp.dma_start(wc_raw[0:KREST, 4, :], d["conv_rest"]).then_inc(sem("wc_loaded"), 16)
            for g in range(NP // GRP):
                load_x(sp, 0, g)
            two = lambda name: d[name].rearrange("(c p) n -> p c n", p=P)
            sp.dma_start(wkv_raw[:, :, :], two("la_wkv")).then_inc(sem("wkv_loaded"), 16)
            sp.dma_start(vecs[:, :], d["vecs"]).then_inc(sem("wkv_loaded"), 16)
            sp.dma_start(rows[:, :], d["rows"].broadcast_to([P, len(ROWS) * C])).then_inc(sem("wkv_loaded"), 16)
            for dst, name in ((w_q, "la_wq"), (w_proj, "la_proj_w"), (w_mod, "mod_w"), (w_gq, "ga_wq"),
                              (w_gkv, "ga_wkv"), (w_gproj, "ga_proj_w")):
                sp.dma_start(dst[:, :, :], two(name)).then_inc(sem("tok_w_loaded"), 16)
            with sp.Fori(1, NW) as n:
                for g in range(NP // GRP):
                    load_x(sp, n, g)
            phase(sp, 1)
            for layer in range(2):
                sp.dma_start(a_w[layer][:, :, :], two(f"qkv_w{layer}")).then_inc(sem("a_w_loaded"), 16)
                sp.dma_start(a_wo[layer][:, :, :], two(f"o_w{layer}")).then_inc(sem("a_w_loaded"), 16)
                if layer == 0:
                    for e in range(2):
                        load_expert(sp, e)
                    sp.dma_start(a_bias[:, :], d["qkv_b"].broadcast_to([P, QKV])).then_inc(sem("a_w_loaded"), 16)
                    phase(sp, 2)
                    sp.dma_start(w_rt[:, :, :], two("router_w")).then_inc(sem("moe_small_loaded"), 16)
                    sp.dma_start(beta[:, :], d["beta"]).then_inc(sem("moe_small_loaded"), 16)
                    for e in range(2):
                        load_vectors(sp, e)
                    for e in range(2, E):
                        sp.wait_ge(sem("w_lo_made"), PIECES * (e - 1))
                        load_expert(sp, e)
                        sp.wait_ge(sem("y_added"), NB * (e - 1))
                        load_vectors(sp, e)
                    phase(sp, 3)
            phase(sp, 4)
            sp.dma_start(z_w[:, :, :], two("z_w")).then_inc(sem("z_loaded"), 16)
            sp.dma_start(z_b[:, :], d["z_b"]).then_inc(sem("z_loaded"), 16)
            sp.dma_start(z_base[:, :, :], two("base_w")).then_inc(sem("z_loaded"), 16)
            sp.dma_start(z_rows[:, :], d["z_rows"].broadcast_to([P, C + E6])).then_inc(sem("z_loaded"), 16)
            for t in range(T):
                sp.wait_ge(sem("z_out_made"), t + 1)
                sp.dma_start(out[:, t, :], z_o[:, t, :]).then_inc(sem("stored"), 16)
            sp.wait_ge(sem("stored"), 16 * T)

        @block.gpsimd
        def _(pool):
            pool.memset(ident[:, :], 0.0).then_inc(sem("ident_zeroed"), 1)
            pool.memset(mhalf[:, :], -0.5).then_inc(sem("consts_made"), 1)
            pool.memset(xraw[:, :, 4, :], 0.0).then_inc(sem("pads_zeroed"), 1)
            pool.wait_ge(sem("ident_zeroed"), 1)
            pool.affine_select(out=ident[:, :], in_=ident[:, :], compare_op=ALU.not_equal, fill=1.0,
                               base=0, pattern=[[-1, P]], channel_multiplier=1).then_inc(sem("consts_made"), 1)
            pool.iota(iota[:, :], pattern=[[1, 8]], base=0, channel_multiplier=0,
                      allow_small_or_imprecise_dtypes=True).then_inc(sem("consts_made"), 1)
            for k in range(NP):
                split_x_lo(pool, 0, k)
            pool.wait_ge(sem("consts_made"), 1)
            inverse_std(pool, 0)
            for k in range(EARLY):
                split_x_lo(pool, 1, k)
            round_pool(pool, 0, True, False, False)
            for n in range(1, NW - 2):
                round_pool(pool, n, False, False, False)
            round_pool(pool, NW - 2, False, False, True)
            round_pool(pool, NW - 1, False, True, False)
            value_prod(pool, NW - 1)
            inverse_std(pool, *ln_place("class"))
            value_prod(pool, NW)
            phase(pool, 1)
            pool_attention(pool, 0)
            phase(pool, 2)
            pool_experts(pool)
            phase(pool, 3)
            pool_attention(pool, 1)
            phase(pool, 4)
            inverse_std(pool, *ln_place("low rank"))

        @block.tensor
        def _(pe):
            pe.wait_ge(sem("consts_made"), 3)
            pe.wait_ge(sem("wc_made"), 2)
            for k in range(NP):
                conv(pe, 0, k)
            pe.wait_ge(sem("bias_columns"), CH)
            mm_rows(pe, bank(4, 0, 2 * C), aggT, wkv_raw, 0, 2 * C).then_inc(sem("kvb_done"), 1)
            pe.wait_ge(sem("wkv_lo_made"), CH)
            pe.wait_ge(sem("kvb_made"), 1)
            pe.wait_ge(sem("tok_w_loaded"), 96)
            round_pe(pe, 0, True, False)
            for n in range(1, NW - 1):
                round_pe(pe, n, False, False)
            round_pe(pe, NW - 1, False, True)
            turn_agg(pe, NW - 1)
            project_agg(pe, NW - 1)
            pe_global(pe)
            phase(pe, 1)
            pe_attention(pe, 0)
            phase(pe, 2)
            pe_experts(pe)
            phase(pe, 3)
            pe_attention(pe, 1)
            phase(pe, 4)
            pe_lora(pe)

        @block.scalar
        def _(act):
            act.wait_ge(sem("wc_loaded"), 32)
            act.activation(wc_hi[:, :, :], wc_raw[:, :, :], ACT.Copy).then_inc(sem("wc_made"), 1)
            for k in range(NP):
                split_x_hi(act, 0, k)
                if k >= 2:
                    copy_pe(act, 0, k - 2)
            for k in (NP - 2, NP - 1):
                copy_pe(act, 0, k)
            for k in range(EARLY):
                split_x_hi(act, 1, k)
            act.wait_ge(sem("wkv_scaled"), 2)
            for c in range(CH):
                act.activation(wkv_hi[:, c, :], wkv_raw[:, c, :], ACT.Copy).then_inc(sem("wkv_hi_made"), 1)
            round_act(act, 0, True, False, False)
            for n in range(1, NW - 2):
                round_act(act, n, False, False, False)
            round_act(act, NW - 2, False, False, True)
            round_act(act, NW - 1, False, True, False)
            exponent(act, NW - 1)
            copy_aggT(act, NW - 1)
            act_global(act)
            phase(act, 1)
            act_attention(act, 0)
            phase(act, 2)
            act_experts(act)
            phase(act, 3)
            act_attention(act, 1)
            phase(act, 4)
            act_lora(act)

        @block.vector
        def _(dve):
            dve.memset(wc_raw[:, 4, :], 0.0).then_inc(sem("pads_zeroed"), 1)
            dve.memset(spare[:, :], 0.0).then_inc(sem("ones_made"), 1)
            dve.memset(attn[:, NP * H8:], 1.0).then_inc(sem("ones_made"), 1)
            dve.wait_ge(sem("wc_made"), 1)
            dve.tensor_tensor(wc_lo[:, :, :], wc_raw[:, :, :], wc_hi[:, :, :], ALU.subtract).then_inc(sem("wc_made"), 1)
            dve.wait_ge(sem("ones_made"), 2)
            dve.wait_ge(sem("wkv_loaded"), 48)
            for c in range(CH):
                dve.tensor_copy(aggT[:, c * P:(c + 1) * P], vecs[:, LAKV + 2 + c:LAKV + 3 + c].broadcast_to([P, P]))\
                   .then_inc(sem("bias_columns"), 1)
            for k in range(NP):
                measure(dve, 0, k)
            reduce_window(dve, 0)
            dve.wait_ge(sem("kvb_done"), 1)
            dve.tensor_copy(kv_sb[:, NP, :], bank(4, 0, 2 * C)).then_inc(sem("kvb_made"), 1)
            dve.wait_ge(sem("kvb_made"), 1)
            for c in range(CH):
                dve.tensor_scalar(wkv_raw[:, c, :], wkv_raw[:, c, :], vecs[:, LAKV + c:LAKV + c + 1], None, ALU.mult)\
                   .then_inc(sem("wkv_scaled"), 1)
            shift_of(dve, 0)
            dve.wait_ge(sem("wkv_hi_made"), CH)
            for c in range(CH):
                dve.tensor_tensor(wkv_lo[:, c, :], wkv_raw[:, c, :], wkv_hi[:, c, :], ALU.subtract)\
                   .then_inc(sem("wkv_lo_made"), 1)
            round_dve(dve, 0, True, False)
            for n in range(1, NW - 1):
                round_dve(dve, n, False, False)
            round_dve(dve, NW - 1, False, True)
            score(dve, NW - 1)
            weigh(dve, NW - 1)
            aggregate(dve, NW - 1)
            add_local(dve, NW - 1)
            dve_global(dve)
            phase(dve, 1)
            dve_attention(dve, 0)
            phase(dve, 2)
            dve_experts(dve)
            phase(dve, 3)
            dve_attention(dve, 1)
            phase(dve, 4)
            dve_lora(dve)


def kernel(**inputs):
    import numpy as np
    import concourse.bacc as bacc
    from concourse.bass_utils import run_bass_kernel_spmd

    a = {k: np.asarray(v) for k, v in inputs.items()}
    cat, tidy = np.concatenate, np.ascontiguousarray
    tok = lambda name: a["L0_tok_" + name]
    x = a["x"][:, :, :126, :126].reshape(P, 3, 3, 3, 14, 3, 3, 14).transpose(2, 5, 1, 4, 7, 3, 6, 0)
    x = x.reshape(NW, 588, NP, P)
    conv = tok("conv_w").reshape(C, 588).T
    arrays = {
        "x_main": x[:, :512].reshape(NW, 4, P, NP, P).transpose(0, 2, 3, 1, 4).reshape(NW * P, NP * 512),
        "x_rest": x[:, 512:].reshape(NW * KREST, NP * P),
        "conv_main": conv[:512].reshape(4, P, C).transpose(1, 0, 2).reshape(P, 4 * C),
        "conv_rest": conv[512:],
        "vecs": np.stack([tok(n) for n in VECS]).reshape(len(VECS), CH, P).transpose(2, 0, 1).reshape(P, -1),
        "rows": cat([tok(n) for n in ROWS])[None],
        "la_wq": tok("la_wq"), "la_wkv": tok("la_wkv"), "la_proj_w": tok("la_proj_w"),
        "ga_wq": tok("ga_wq"), "ga_wkv": tok("ga_wkv"), "ga_proj_w": tok("ga_proj_w"), "mod_w": tok("mod_w"),
        "qkv_w0": cat([a["L0_attn_" + n].T for n in ("Wq", "Wk", "Wv")], axis=1),
        "qkv_b": cat([a["L0_attn_" + n] for n in ("bq", "bk", "bv")])[None],
        "o_w0": a["L0_attn_Wo"].T,
        "qkv_w1": a["L1_attn_Wqkv"].T, "o_w1": a["L1_attn_Wout"].T,
        "router_w": a["L0_ffn_router_w"],
        "w1": a["L0_ffn_w1"].reshape(E, CH, P, FF).transpose(0, 2, 1, 3).reshape(E * P, CH * FF),
        "w2": a["L0_ffn_w2"].reshape(E, FC, P, C).transpose(0, 2, 1, 3).reshape(E * P, FC * C),
        "b1": a["L0_ffn_b1"].reshape(E * FC, P).T,
        "b2": a["L0_ffn_b2"].reshape(1, E * C), "gamma": a["L0_ffn_gamma"].reshape(1, E * C),
        "beta": a["L0_ffn_beta"],
        "z_w": cat([a["L1_ffn_shared_A"], a["L1_ffn_routed_A"].reshape(E6 * R16, C), a["L1_ffn_router_W"]]).T,
        "z_b": cat([a["L1_ffn_shared_B"].T, a["L1_ffn_routed_B"].transpose(0, 2, 1).reshape(E6 * R16, C)]),
        "z_rows": cat([a["L1_ffn_base_b"], a["L1_ffn_router_b"]])[None],
        "base_w": a["L1_ffn_base_W"].T,
    }
    nc = bacc.Bacc("TRN2", target_bir_lowering=False, num_devices=1)
    feed, d = {}, {}
    for name, value in arrays.items():
        feed[f"in_{name}"] = tidy(value)
        d[name] = nc.dram_tensor(f"in_{name}", value.shape, F32, kind="ExternalInput").ap()
    out = nc.dram_tensor("out_h", (P, T, C), F32, kind="ExternalOutput").ap()
    vision_tower(nc, d, out)
    return run_bass_kernel_spmd(nc, [feed], core_ids=[0]).results[0]["out_h"]
```

```python
from contextlib import ExitStack

import concourse.bass as bass
from concourse import mybir

ALU = mybir.AluOpType
ACT = mybir.ActivationFunctionType
AX = mybir.AxisListType.X
F32 = mybir.dt.float32
F32R = mybir.dt.float32r
U32 = mybir.dt.uint32

P = 128
C = 256
CH = C // P
NW = 9
NP = 9
KC = 5
KREST = 588 - 4 * P
GRP = 3
H8, DH8 = 8, 32
H16, D16 = 16, 16
T = NW + 1
QKV = 3 * C
E, FF = 8, 1024
FC = FF // P
BT = 2
NB = T // BT
BW = BT * P
PIECES = 8
E6, R16 = 6, 16
LOW = (E6 + 1) * R16
ZW = LOW + E6
NEG4 = -4.0e9
VECS = ["la_ln_q_g", "la_ln_q_b", "la_ln_kv_g", "la_ln_kv_b", "ga_ln_q_g", "ga_ln_q_b", "ga_ln_kv_g", "ga_ln_kv_b"]
LAQ, LAKV, GAQ, GAKV = 0, 4, 8, 12
ROWS = ["la_proj_b", "mod_b", "ga_proj_b", "class_emb"]


def earlier(k, cycle, slots=2):
    return slots if k >= slots else k + cycle - (k + ((cycle - 1 - k) // slots) * slots)


def vision_tower(nc, d, out):
    ctx = ExitStack()
    with ctx:
        def sb(name, shape, dt=F32, scope=None):
            return (scope or ctx).enter_context(nc.sbuf_tensor(name, shape, dt))

        sems = {}

        def sem(name):
            if name not in sems:
                sems[name] = ctx.enter_context(nc.semaphore(name))
            return sems[name]

        pair = [ctx.enter_context(nc.psum_tensor(f"banks{2 * i}", [P, 2, 512], F32)) for i in range(4)]

        def bank(i, a=0, b=C):
            return pair[i // 2][:, i % 2, a:b]

        h = sb("h", [P, T * C])
        ident = sb("ident", [P, P])
        iota = sb("iota", [P, 8])
        pick = sb("pick", [64, P], F32R)
        stats = [sb(f"stats{i}", [P, T, 6]) for i in range(3)]
        mv = [sb(f"mv{i}", [P, T, 2]) for i in range(3)]
        veps = [sb(f"veps{i}", [P, T]) for i in range(3)]
        mhalf = sb("mhalf", [P, 10])
        spare = sb("spare", [P, 2])
        rstd = [sb(f"rstd{i}", [P, T]) for i in range(3)]
        nmr = [sb(f"nmr{i}", [P, T]) for i in range(3)]

        def h_at(t, n=1):
            return h[:, t * C:(t + n) * C]

        tok = ExitStack()
        wc_raw = sb("wc_raw", [P, KC, C], F32, tok)
        wc_hi = sb("wc_hi", [P, KC, C], F32R, tok)
        wc_lo = sb("wc_lo", [P, KC, C], F32R, tok)
        wkv_raw = sb("wkv_raw", [P, CH, 2 * C], F32, tok)
        wkv_hi = sb("wkv_hi", [P, CH, 2 * C], F32R, tok)
        wkv_lo = sb("wkv_lo", [P, CH, 2 * C], F32R, tok)
        xraw = sb("xraw", [P, NP, KC, P], F32, tok)
        x_hi = sb("x_hi", [P, NP, KC * P], F32R, tok)
        x_lo = sb("x_lo", [P, NP, KC * P], F32R, tok)
        pe_sb = sb("pe_sb", [P, NP * C], F32, tok)
        xn = sb("xn", [P, NP * C], F32, tok)
        xg_hi = sb("xg_hi", [P, 2, C], F32R, tok)
        xg_lo = sb("xg_lo", [P, 2, C], F32R, tok)
        kv_sb = sb("kv_sb", [P, NP + 1, 2 * C], F32, tok)
        prod = sb("prod", [P, (NP + 1) * C], F32, tok)
        vprod = sb("vprod", [P, (NP + 1) * C], F32, tok)
        red = sb("red", [P, C], F32, tok)
        redn = sb("redn", [P, C], F32, tok)
        red_sum = sb("red_sum", [P, C], F32, tok)
        redT = sb("redT", [P, C], F32, tok)
        q_sb = sb("q_sb", [P, C], F32, tok)
        g_q = red_sum
        sc = sb("sc", [P, (NP + 1) * H8], F32, tok)
        smax = sb("smax", [P, H8], F32, tok)
        pr = sb("pr", [P, NP * H8], F32, tok)
        den = sb("den", [P, H8], F32, tok)
        rden = sb("rden", [P, H8], F32, tok)
        attn = sb("attn", [P, (NP + 1) * H8], F32, tok)
        agg = sb("agg", [P, C], F32, tok)
        aggT = sb("aggT", [P, C], F32, tok)
        local = sb("local", [P, NW * C], F32, tok)
        w_q = sb("w_q", [P, CH, C], F32, tok)
        w_proj = sb("w_proj", [P, CH, C], F32, tok)
        w_mod = sb("w_mod", [P, CH, C], F32, tok)
        w_gq = sb("w_gq", [P, CH, C], F32, tok)
        w_gkv = sb("w_gkv", [P, CH, 2 * C], F32, tok)
        w_gproj = sb("w_gproj", [P, CH, C], F32, tok)
        vecs = sb("vecs", [P, 2 * len(VECS)], F32, tok)
        rows = sb("rows", [P, len(ROWS) * C], F32, tok)
        localT = sb("localT", [P, 2, C], F32, tok)
        gnT = wc_raw[:, 0:2, :]
        tok.close()

        w_raw = sb("w_raw", [P, 4 * CH * FF])
        w1raw = [w_raw[:, i * CH * FF:(i + 1) * CH * FF] for i in range(2)]
        w2raw = [w_raw[:, (2 + i) * CH * FF:(3 + i) * CH * FF] for i in range(2)]
        s_slot = [w_raw[:, 2 * C + i * T * C:2 * C + (i + 1) * T * C] for i in range(3)]

        a_w = [sb(f"a_w{i}", [P, CH, QKV]) for i in range(2)]
        a_wo = [sb(f"a_wo{i}", [P, CH, C]) for i in range(2)]
        att = ExitStack()
        a_bias = sb("a_bias", [64, QKV], F32, att)
        bias_r = sb("bias_r", [64, QKV], F32R, att)
        a_xn = sb("a_xn", [P, 2, C], F32, att)
        a_xT = sb("a_xT", [P, 2, C], F32, att)
        a_qkv = sb("a_qkv", [P, T, QKV], F32, att)
        a_s = sb("a_s", [P, T * T * H16], F32, att)
        a_prod = sb("a_prod", [P, 4, T * C], F32, att)
        g_kv = a_prod[:, 0:2, :].rearrange("p a b -> p (a b)")[:, 0:NW * 2 * C]\
            .rearrange("p (n c) -> p n c", n=NW)
        a_p = sb("a_p", [P, T * T * H16], F32, att)
        a_max = sb("a_max", [P, T * H16], F32, att)
        a_den = sb("a_den", [P, T * H16], F32, att)
        a_rden = sb("a_rden", [P, T * H16], F32, att)
        a_o = sb("a_o", [P, T * C], F32, att)
        a_oT = sb("a_oT", [P, 2, C], F32, att)
        z_w = sb("z_w", [P, CH, ZW], F32, att)
        z_b = sb("z_b", [LOW, C], F32, att)
        z_base = sb("z_base", [P, CH, C], F32, att)
        z_rows = sb("z_rows", [P, C + E6], F32, att)
        att.close()

        moe = ExitStack()
        split_w = [sb("split_w1", [P, 4, CH * FF], F32R, moe)]
        x2 = sb("x2", [P, T * C], F32, moe)
        x2T = sb("x2T", [P, T, C], F32, moe)
        xT_hi = sb("xT_hi", [P, CH, T * P], F32R, moe)
        xT_lo = sb("xT_lo", [P, CH, T * P], F32R, moe)
        gel = sb("gel", [P, 2, BW], F32, moe)
        hid_hi = sb("hid_hi", [P, FC, BW], F32R, moe)
        hid_lo = sb("hid_lo", [P, FC, BW], F32R, moe)
        lg = sb("lg", [P, T, E], F32, moe)
        top = sb("top", [P, T, 8], F32, moe)
        topi = sb("topi", [P, T, 8], U32, moe)
        topf = sb("topf", [P, T, 2], F32, moe)
        tw = sb("tw", [P, T, 2], F32, moe)
        te = sb("te", [P, T, 2], F32, moe)
        warm = sb("warm", [P, 2], F32, moe)
        tsum = sb("tsum", [P, T], F32, moe)
        trec = sb("trec", [P, T], F32, moe)
        hot = sb("hot", [P, 2, T, E], F32, moe)
        gates = sb("gates", [P, T, E], F32, moe)
        gat_e = sb("gat_e", [P, E * T], F32, moe)
        gT = sb("gT", [E, T, P], F32, moe)
        xb = sb("xb", [P, BT * C], F32, moe)
        res = sb("res", [P, BT * C], F32, moe)
        nr = sb("nr", [P, 2, BT * C], F32, moe)
        gm = sb("gm", [P, BT * C], F32, moe)
        bst = sb("bst", [P, BT, 6], F32, moe)
        bmv = sb("bmv", [P, BT, 2], F32, moe)
        bve = sb("bve", [P, BT], F32, moe)
        brs = sb("brs", [P, BT], F32, moe)
        bsc = sb("bsc", [P, BT], F32, moe)
        split_w.insert(0, sb("split_w0", [P, 4, CH * FF], F32R, moe))
        b1 = [sb(f"b1_{i}", [P, FC], F32, moe) for i in range(2)]
        b2 = [sb(f"b2_{i}", [P, C], F32, moe) for i in range(2)]
        gam = [sb(f"gam{i}", [P, C], F32, moe) for i in range(2)]
        beta = sb("beta", [E, C], F32, moe)
        w_rt = sb("w_rt", [P, CH, E], F32, moe)
        w1_hi, w1_lo, w2_hi, w2_lo = ([split_w[i][:, j, :] for i in range(2)] for j in range(4))
        moe.close()

        lora = ExitStack()
        z_xn = sb("z_xn", [P, 4, C], F32, lora)
        z_xT = sb("z_xT", [P, T, C], F32, lora)
        z = sb("z", [P, T, ZW], F32, lora)
        z_s = sb("z_s", [P, T, LOW], F32, lora)
        z_l = sb("z_l", [P, T, E6], F32, lora)
        z_max = sb("z_max", [P, T], F32, lora)
        z_p = sb("z_p", [P, T, E6], F32, lora)
        z_g = sb("z_g", [P, T, 8], F32, lora)
        z_top = sb("z_top", [P, T, 8], F32, lora)
        z_topi = sb("z_topi", [P, T, 8], U32, lora)
        z_topf = sb("z_topf", [P, T, 2], F32, lora)
        z_tw = sb("z_tw", [P, T, 2], F32, lora)
        z_sum = sb("z_sum", [P, T], F32, lora)
        z_rec = sb("z_rec", [P, T], F32, lora)
        z_hot = sb("z_hot", [P, 2, T, E6], F32, lora)
        z_sw = sb("z_sw", [P, T, E6], F32, lora)
        z_sT = sb("z_sT", [P, 2, P], F32, lora)
        z_o = sb("z_o", [P, T, C], F32, lora)
        lora.close()

        block = ctx.enter_context(nc.Block())

        def phase(eng, n):
            eng.drain().then_inc(sem("phase_ended"), 1)
            eng.wait_ge(sem("phase_ended"), 5 * n)

        def mm3(pe, dst, a, b, start, stop):
            pe.matmul(dst, a[0], b[0], start=start, stop=False)
            pe.matmul(dst, a[0], b[1], start=False, stop=False)
            return pe.matmul(dst, a[1], b[0], start=False, stop=stop)

        def mm_rows(pe, dst, aT, w, a, b):
            for c in range(CH):
                last = pe.matmul(dst, aT[:, c * P:(c + 1) * P], w[:, c, a:b], start=(c == 0), stop=(c == CH - 1))
            return last

        def turn(pe, dst, src):
            for c in range(CH):
                last = pe.transpose(dst[:, c * P:(c + 1) * P], src[:, c * P:(c + 1) * P], ident[:, :])
            return last

        class Chain:

            def __init__(self, eng, name):
                self.eng, self.sem, self.n = eng, sem(name), 0

            def __call__(self, ins):
                ins.then_inc(self.sem, 1)
                self.n += 1
                self.eng.wait_ge(self.sem, self.n)

        SET = {"class": 1, "attention 0": 2, "experts": 1, "attention 1": 0, "low rank": 1}
        BEFORE = {"class": 0, "attention 0": 0, "experts": 1, "attention 1": NW, "low rank": 2}
        BATCHES = [("class", 0, NW - 1), ("attention 0", 0, NW - 2), ("class", NW - 1, NW), ("attention 0", NW - 2, NW - 1),
                   ("class", NW, T), ("attention 0", NW - 1, NW), ("attention 0", NW, T),
                   ("experts", 0, T - BT), ("experts", T - BT, T), ("attention 1", 0, T - BT), ("attention 1", T - BT, T),
                   ("low rank", 0, T - BT), ("low rank", T - BT, T)]

        def batch_of(which, part):
            n = [i for i, b in enumerate(BATCHES) if b[0] == which][part]
            return (NW + n,) + BATCHES[n][1:] + (SET[which],)

        def inverse_std(pool, n, a=0, b=T, i=0):
            pool.wait_ge(sem("var_made"), n + 1)
            pool.tensor_tensor(rstd[i][:, a:b], veps[i][:, a:b], mhalf[:, a:b], ALU.pow).then_inc(sem("rstd_made"), 1)

        def shift_of(dve, n, a=0, b=T, i=0):
            dve.wait_ge(sem("rstd_made"), n + 1)
            dve.scalar_tensor_tensor(out=nmr[i][:, a:b], in0=mv[i][:, a:b, 0], scalar=-1.0, in1=rstd[i][:, a:b],
                                     op0=ALU.mult, op1=ALU.mult).then_inc(sem("nmr_made"), 1)

        def tile_stats(dve, which, t, src):
            i = SET[which]
            dve.bn_stats(stats[i][:, t, :], src).then_inc(sem(f"stats_made{i}"), 1)
            dve.wait_ge(sem(f"stats_made{i}"), T * BEFORE[which] + t + 1)
            dve.tensor_copy(spare[:, 0:1], spare[:, 1:2]).then_inc(sem("spacer"), 1)
            dve.bn_aggr(mv[i][:, t, :], stats[i][:, t, :]).then_inc(sem(f"aggr_made{i}"), 1)

        def add_eps(dve, which, part):
            n, a, b, i = batch_of(which, part)
            dve.wait_ge(sem(f"aggr_made{i}"), T * BEFORE[which] + b)
            dve.tensor_scalar(veps[i][:, a:b], mv[i][:, a:b, 1], 1e-5, None, ALU.add).then_inc(sem("var_made"), 1)

        def end_stats(dve, which, part=0):
            add_eps(dve, which, part)
            shift_of(dve, *batch_of(which, part))

        def normalized_scales(act, which, part=0):
            act.wait_ge(sem("nmr_made"), batch_of(which, part)[0] + 1)

        def normalize(act, dst, src, t, i=0):
            return act.activation(dst, src, ACT.Identity, scale=rstd[i][:, t:t + 1], bias=nmr[i][:, t:t + 1])

        def affine(act, dst, src, v, name):
            for c in range(CH):
                act.activation(dst[:, c * P:(c + 1) * P], src[:, c * P:(c + 1) * P], ACT.Identity,
                               scale=vecs[:, v + c:v + c + 1], bias=vecs[:, v + 2 + c:v + 3 + c]).then_inc(sem(name), 1)

        def load_x(sp, n, g, first=False):
            if not first:
                sp.wait_ge(sem("x_lo_made"), NP * (n - 1) + GRP * g + GRP)
            a, b = GRP * g, GRP * g + GRP
            sp.dma_start(xraw[:, a:b, 0:4, :], d["x_main"][bass.ds(n * P, P), a * 512:b * 512]
                         .rearrange("p (k c b) -> p k c b", k=GRP, c=4)).then_inc(sem(f"x_loaded{g}"), 16)
            sp.dma_start(xraw[0:KREST, a:b, 4, :], d["x_rest"][bass.ds(n * KREST, KREST), a * P:b * P]
                         .rearrange("p (k b) -> p k b", k=GRP)).then_inc(sem(f"x_loaded{g}"), 16)

        def split_x_hi(act, n, k):
            act.wait_ge(sem(f"x_loaded{k // GRP}"), 32 * (n + 1))
            if n > 0:
                act.wait_ge(sem("conv_done"), NP * (n - 1) + k + 1)
            act.activation(x_hi[:, k, :], xraw[:, k].rearrange("p c b -> p (c b)"), ACT.Copy)\
               .then_inc(sem("x_hi_made"), 1)

        def split_x_lo(pool, n, k):
            pool.wait_ge(sem("x_hi_made"), NP * n + k + 1)
            pool.tensor_tensor(x_lo[:, k, :], xraw[:, k].rearrange("p c b -> p (c b)"), x_hi[:, k, :],
                               ALU.subtract).then_inc(sem("x_lo_made"), 1)

        def conv(pe, n, k):
            if n > 0 or k >= 2:
                pe.wait_ge(sem("pe_copied"), NP * n + k + 1 - earlier(k, NP))
            if k < 2 and n >= 4:
                pe.wait_ge(sem("localT_made" if k == 0 else "patch_made"), n - 3)
            pe.wait_ge(sem("x_lo_made"), NP * n + k + 1)
            for c in range(KC):
                a = [x[:, k, c * P:(c + 1) * P] for x in (x_hi, x_lo)]
                last = mm3(pe, bank(k % 2), a, (wc_hi[:, c, :], wc_lo[:, c, :]), c == 0, c == KC - 1)
            last.then_inc(sem("conv_done"), 1)

        def copy_pe(act, n, k):
            if n > 0:
                act.wait_ge(sem("xn_made"), NP * (n - 1) + k + 1)
                act.wait_ge(sem("summed"), (NP - 1) * n)
            act.wait_ge(sem("conv_done"), NP * n + k + 1)
            act.activation(pe_sb[:, k * C:(k + 1) * C], bank(k % 2), ACT.Copy).then_inc(sem("pe_copied"), 1)

        def measure(dve, n, k):
            dve.wait_ge(sem("pe_copied"), NP * n + k + 1)
            dve.bn_stats(stats[0][:, k, :], pe_sb[:, k * C:(k + 1) * C]).then_inc(sem("stats_made0"), 1)
            if k:
                dve.bn_aggr(mv[0][:, k - 1, :], stats[0][:, k - 1, :]).then_inc(sem("aggr_made0"), 1)
            if k > 1:
                dve.wait_ge(sem("summed"), (NP - 1) * n + k - 1)
            if k:
                dve.tensor_tensor(red_sum[:, :], pe_sb[:, 0:C] if k == 1 else red_sum[:, :],
                                  pe_sb[:, k * C:(k + 1) * C], ALU.add).then_inc(sem("summed"), 1)
            dve.wait_ge(sem("stats_made0"), T * n + k + 1)

        def reduce_window(dve, n):
            if n > 0:
                dve.wait_ge(sem("redn_made"), n)
            dve.wait_ge(sem("summed"), (NP - 1) * (n + 1))
            dve.tensor_scalar(red[:, :], red_sum[:, :], 1.0 / NP, None, ALU.mult).then_inc(sem("red_made"), 1)
            dve.bn_aggr(mv[0][:, NP - 1, :], stats[0][:, NP - 1, :]).then_inc(sem("aggr_made0"), 1)
            dve.wait_ge(sem("red_made"), n + 1)
            dve.bn_stats(stats[0][:, NP, :], red[:, :]).then_inc(sem("stats_made0"), 1)
            dve.wait_ge(sem("stats_made0"), T * (n + 1))
            dve.tensor_tensor(local[:, bass.ds(n * C, C)], red[:, :], rows[:, 0:C], ALU.add).then_inc(sem("residual_made"), 1)
            dve.bn_aggr(mv[0][:, NP, :], stats[0][:, NP, :]).then_inc(sem("aggr_made0"), 1)
            dve.wait_ge(sem("aggr_made0"), T * (n + 1))
            dve.tensor_scalar(veps[0][:, :], mv[0][:, :, 1], 1e-5, None, ALU.add).then_inc(sem("var_made"), 1)

        def normalize_patch(act, n, k):
            act.wait_ge(sem("nmr_made"), n + 1)
            if n > 0:
                act.wait_ge(sem("xT_done"), NP * (n - 1) + k + 1)
            normalize(act, xn[:, k * C:(k + 1) * C], pe_sb[:, k * C:(k + 1) * C], k).then_inc(sem("xn_made"), 1)

        def turn_patch(pe, n, k):
            pe.wait_ge(sem("xn_made"), NP * n + k + 1)
            if n > 0 or k >= 2:
                pe.wait_ge(sem("xg_lo_made"), NP * n + k + 1 - earlier(k, NP))
            turn(pe, bank(2 + k % 2), xn[:, k * C:(k + 1) * C]).then_inc(sem("xT_done"), 1)

        def split_xT_hi(act, n, k):
            if n > 0 or k >= 2:
                act.wait_ge(sem("kv_done"), NP * n + k + 1 - earlier(k, NP))
            act.wait_ge(sem("xT_done"), NP * n + k + 1)
            act.activation(xg_hi[:, k % 2, :], bank(2 + k % 2), ACT.Copy).then_inc(sem("xg_hi_made"), 1)

        def split_xT_lo(dve, n, k):
            dve.wait_ge(sem("xg_hi_made"), NP * n + k + 1)
            dve.tensor_tensor(xg_lo[:, k % 2, :], bank(2 + k % 2), xg_hi[:, k % 2, :], ALU.subtract)\
               .then_inc(sem("xg_lo_made"), 1)

        def project_kv(pe, n, k):
            pe.wait_ge(sem("xg_lo_made"), NP * n + k + 1)
            if n > 0 or k >= 2:
                pe.wait_ge(sem("kv_copied"), NP * n + k + 1 - earlier(k, NP))
            dst = bank(4 + k % 2, 0, 512)
            for c in range(CH):
                a = [x[:, k % 2, c * P:(c + 1) * P] for x in (xg_hi, xg_lo)]
                last = mm3(pe, dst, a, (wkv_hi[:, c, :], wkv_lo[:, c, :]), c == 0, c == CH - 1)
            last.then_inc(sem("kv_done"), 1)

        def copy_kv(act, n, k):
            if 0 < n < NW - 1:
                act.wait_ge(sem("vprod_made"), n)
            act.wait_ge(sem("kv_done"), NP * n + k + 1)
            act.activation(kv_of(n)[:, k, :], bank(4 + k % 2, 0, 512), ACT.Copy).then_inc(sem("kv_copied"), 1)

        def normalize_red(act, n):
            act.wait_ge(sem("nmr_made"), n + 1)
            if n > 0:
                act.wait_ge(sem("redT_done"), n)
            normalize(act, redn[:, :], red[:, :], NP).then_inc(sem("redn_made"), 1)

        def turn_red(pe, n):
            pe.wait_ge(sem("redn_made"), n + 1)
            turn(pe, bank(6), redn).then_inc(sem("redT_done"), 1)

        def affine_red(act, n):
            if n > 0:
                act.wait_ge(sem("q_done"), n)
            act.wait_ge(sem("redT_done"), n + 1)
            affine(act, redT, bank(6), LAQ, "redT_made")

        def project_q(pe, n):
            pe.wait_ge(sem("redT_made"), CH * (n + 1))
            mm_rows(pe, bank(7), redT, w_q, 0, C).then_inc(sem("q_done"), 1)

        def copy_q(act, n):
            act.wait_ge(sem("q_done"), n + 1)
            if n > 0:
                act.wait_ge(sem("score_made"), n)
            act.activation(q_sb[:, :], bank(7), ACT.Copy, scale=C ** -0.5).then_inc(sem("q_made"), 1)

        def by_head(x):
            return x[:, 0:NP * H8].rearrange("p (k h) -> p h k", k=NP)

        def by_key(x, slots=NP):
            return x[:, 0:slots * H8].rearrange("p (k h) -> p k h", k=slots)

        def over_keys(x):
            return x.unsqueeze(1).broadcast_to([P, NP, H8])

        def kv_of(n):
            return a_qkv[:, :, 0:2 * C] if n == NW - 1 else kv_sb if n < NW else g_kv

        def slots_of(n):
            return NP + 1 if n < NW else NP

        def score(dve, n, parts=(0, 1, 2)):
            ns = slots_of(n)
            q, kv = (q_sb if n < NW else g_q), kv_of(n)
            if 0 in parts:
                dve.wait_ge(sem("kv_copied"), NP * (n + 1))
                dve.wait_ge(sem("q_made"), n + 1)
                if n == NW - 1:
                    dve.wait_ge(sem("kvb_made"), 2)
                dve.tensor_tensor(prod[:, 0:ns * C].rearrange("p (k c) -> p k c", k=ns), kv[:, 0:ns, 0:C],
                                  q[:, :].unsqueeze(1).broadcast_to([P, ns, C]), ALU.mult).then_inc(sem("score_link"), 1)
            if 1 in parts:
                dve.wait_ge(sem("score_link"), 4 * n + 1)
                dve.tensor_reduce(sc[:, 0:ns * H8], prod[:, 0:ns * C].rearrange("p (x d) -> p x d", d=DH8), AX, ALU.add)\
                   .then_inc(sem("score_link"), 1)
            if 2 in parts:
                dve.wait_ge(sem("score_link"), 4 * n + 2)
                links = 2
                if n < NW:
                    dve.tensor_tensor(by_key(sc), by_key(sc), over_keys(sc[:, NP * H8:]), ALU.add)\
                       .then_inc(sem("score_link"), 1)
                    dve.wait_ge(sem("score_link"), 4 * n + 3)
                    links = 3
                dve.tensor_reduce(smax[:, :], by_head(sc), AX, ALU.max).then_inc(sem("score_link"), 1)
                dve.wait_ge(sem("score_link"), 4 * n + links + 1)
                dve.tensor_tensor(by_key(sc), by_key(sc), over_keys(smax[:, :]), ALU.subtract).then_inc(sem("score_made"), 1)

        def weigh(dve, n):
            dve.wait_ge(sem("exp_made"), n + 1)
            dve.tensor_reduce(den[:, :], by_head(pr), AX, ALU.add).then_inc(sem("weigh_link"), 1)
            dve.wait_ge(sem("weigh_link"), 2 * n + 1)
            dve.reciprocal(rden[:, :], den[:, :]).then_inc(sem("weigh_link"), 1)
            dve.wait_ge(sem("weigh_link"), 2 * n + 2)
            dve.tensor_tensor(by_key(attn), by_key(pr), over_keys(rden[:, :]), ALU.mult).then_inc(sem("attn_made"), 1)

        def value_prod(pool, n):
            ns = slots_of(n)
            pool.wait_ge(sem("attn_made"), n + 1)
            kv = kv_of(n)
            pool.tensor_tensor(vprod[:, 0:ns * C].rearrange("p (k h d) -> p k h d", k=ns, d=DH8),
                               kv[:, 0:ns, C:2 * C].rearrange("p k (h d) -> p k h d", d=DH8),
                               by_key(attn, ns).unsqueeze(3).broadcast_to([P, ns, H8, DH8]), ALU.mult)\
                .then_inc(sem("vprod_made"), 1)

        def aggregate(dve, n, half):
            ns = slots_of(n)
            at = slice(half * P, (half + 1) * P)
            if half == 0:
                dve.wait_ge(sem("vprod_made"), n + 1)
                if n > 0:
                    dve.wait_ge(sem("aggT_done"), n)
            dve.tensor_reduce(agg[:, at], vprod[:, 0:ns * C].rearrange("p (k c) -> p c k", k=ns)[:, at], AX, ALU.add)\
               .then_inc(sem("agg_made"), 1)

        def exponent(act, n):
            act.wait_ge(sem("score_made"), n + 1)
            act.activation(pr[:, :], sc[:, 0:NP * H8], ACT.Exp).then_inc(sem("exp_made"), 1)

        def turn_agg(pe, n):
            pe.wait_ge(sem("agg_made"), 2 * (n + 1))
            if n < NW - 1:
                pe.wait_ge(sem("redT_made"), CH * (n + 2))
            else:
                pe.wait_ge(sem("aggT_copied"), n)
            turn(pe, bank(6), agg).then_inc(sem("aggT_done"), 1)

        def copy_aggT(act, n):
            act.wait_ge(sem("aggT_done"), n + 1)
            if n > 0:
                act.wait_ge(sem("proj_done"), n)
            act.activation(aggT[:, :], bank(6), ACT.Copy).then_inc(sem("aggT_copied"), 1)

        def project_agg(pe, n):
            pe.wait_ge(sem("aggT_copied"), n + 1)
            if n < NW - 1:
                pe.wait_ge(sem("q_made"), n + 2)
            else:
                pe.wait_ge(sem("local_made"), n)
            mm_rows(pe, bank(7), aggT, w_proj, 0, C).then_inc(sem("proj_done"), 1)

        def add_local(dve, n):
            dve.wait_ge(sem("residual_made"), n + 1)
            dve.wait_ge(sem("proj_done"), n + 1)
            dve.tensor_tensor(local[:, bass.ds(n * C, C)], bank(7), local[:, bass.ds(n * C, C)], ALU.add)\
               .then_inc(sem("local_made"), 1)

        def turn_local(pe, n, b=0):
            pe.wait_ge(sem("local_made"), n + 1)
            if b == 0:
                pe.wait_ge(sem("pe_copied"), NP * min(n + 4, NW))
            else:
                pe.wait_ge(sem("aggT_copied"), n + 1)
            turn(pe, bank(b), local[:, n * C:(n + 1) * C]).then_inc(sem("local_turned"), 1)

        def copy_localT(dve, n, b=0):
            dve.wait_ge(sem("local_turned"), n + 1)
            if n >= 2:
                dve.wait_ge(sem("mod_done"), n - 1)
            dve.tensor_copy(localT[:, n % 2, :], bank(b)).then_inc(sem("localT_made"), 1)

        def project_mod(pe, n, b=1):
            pe.wait_ge(sem("localT_made"), n + 1)
            mm_rows(pe, bank(b), localT[:, n % 2, :], w_mod, 0, C).then_inc(sem("mod_done"), 1)

        def token_out(dve, n, b=1):
            dve.wait_ge(sem("mod_done"), n + 1)
            dve.tensor_tensor(h_at(n), bank(b), rows[:, C:2 * C], ALU.add).then_inc(sem("patch_made"), 1)
            dve.wait_ge(sem("patch_made"), n + 1)
            tile_stats(dve, "attention 0", n, h_at(n))

        def round_pe(pe, n, first, last):
            if not last:
                for k in range(NP - 1):
                    conv(pe, n + 1, k)
            turn_patch(pe, n, 0)
            turn_red(pe, n)
            if not last:
                conv(pe, n + 1, NP - 1)
            for k in range(NP):
                if k + 1 < NP:
                    turn_patch(pe, n, k + 1)
                project_kv(pe, n, k)
                if k == 2:
                    project_q(pe, n)
                if not first and k == (7 if last else 4):
                    turn_agg(pe, n - 1)
                if not first and k == (8 if last else 6):
                    project_agg(pe, n - 1)
                if n >= 2 and k == 2:
                    turn_local(pe, n - 2)
                if n >= 2 and k == 6:
                    project_mod(pe, n - 2)

        EARLY = 6

        def round_act(act, n, first, last, second_last):
            normalize_red(act, n)
            for k in range(2 if last else NP):
                normalize_patch(act, n, k)
                if not last:
                    if k < NP - EARLY:
                        split_x_hi(act, n + 1, EARLY + k)
                    if k:
                        copy_pe(act, n + 1, k - 1)
                if not (first or last) and k == 5:
                    exponent(act, n - 1)
            split_xT_hi(act, n, 0)
            if not last:
                copy_pe(act, n + 1, NP - 1)
            affine_red(act, n)
            for k in range(NP):
                if last and k + 2 < NP:
                    normalize_patch(act, n, k + 2)
                if k + 1 < NP:
                    split_xT_hi(act, n, k + 1)
                if k == 3:
                    copy_q(act, n)
                if last and k == 3:
                    exponent(act, n - 1)
                if not first and k == (NP - 1 if last else 5):
                    copy_aggT(act, n - 1)
                copy_kv(act, n, k)
                if not (last or second_last) and k < EARLY:
                    split_x_hi(act, n + 2, k)

        def round_pool(pool, n, first, last, second_last):
            if not last:
                for k in range(EARLY, NP):
                    split_x_lo(pool, n + 1, k)
            if last:
                inverse_std(pool, *batch_of("class", 0))
            if not first:
                value_prod(pool, n - 1)
            if not (last or second_last):
                for k in range(3):
                    split_x_lo(pool, n + 2, k)
            if not last:
                pool.wait_ge(sem("xn_made"), NP * (n + 1))
                pool.wait_ge(sem("redn_made"), n + 1)
                inverse_std(pool, n + 1)
            if not (last or second_last):
                for k in range(3, EARLY):
                    split_x_lo(pool, n + 2, k)

        def last_round_dve(dve):
            n = NW - 1
            add_eps(dve, "class", 0)
            dve.wait_ge(sem("conv_done"), NP * NW)
            dve.tensor_copy(kv_of(n)[:, NP, :], kv_sb[:, NP, :]).then_inc(sem("kvb_made"), 1)
            split_xT_lo(dve, n, 0)
            shift_of(dve, *batch_of("class", 0))
            split_xT_lo(dve, n, 1)
            score(dve, n - 1, (0,))
            split_xT_lo(dve, n, 2)
            score(dve, n - 1, (1,))
            split_xT_lo(dve, n, 3)
            score(dve, n - 1, (2,))
            split_xT_lo(dve, n, 4)
            weigh(dve, n - 1)
            split_xT_lo(dve, n, 5)
            copy_localT(dve, n - 2)
            split_xT_lo(dve, n, 6)
            split_xT_lo(dve, n, 7)
            aggregate(dve, n - 1, 0)
            aggregate(dve, n - 1, 1)
            split_xT_lo(dve, n, 8)
            token_out(dve, n - 2)
            add_eps(dve, "attention 0", 0)

        def round_dve(dve, n, first):
            if not first:
                score(dve, n - 1)
            for k in range(NP - 1):
                measure(dve, n + 1, k)
                if not first and k == 3:
                    weigh(dve, n - 1)
            split_xT_lo(dve, n, 0)
            measure(dve, n + 1, NP - 1)
            for k in range(1, NP):
                split_xT_lo(dve, n, k)
                if not first and k in (2, 3):
                    aggregate(dve, n - 1, k - 2)
                if k == 4:
                    reduce_window(dve, n + 1)
                if n >= 2 and k == 5:
                    copy_localT(dve, n - 2)
                if k == 7:
                    shift_of(dve, n + 1)
                if not first and k == 7:
                    add_local(dve, n - 1)
                if not first and k == 8:
                    local_stats(dve, n - 1)
            if n >= 2:
                token_out(dve, n - 2)

        def local_stats(dve, n):
            dve.wait_ge(sem("local_made"), n + 1)
            tile_stats(dve, "class", n + 1, local[:, n * C:(n + 1) * C])

        def turn_g(pe, s):
            pe.wait_ge(sem("ga_xn_made"), s + 1)
            if s >= 2:
                pe.wait_ge(sem("gnT_made"), CH * (s - 1))
            if s == NW:
                pe.wait_ge(sem("localT_made"), NW)
            dst = bank(6) if s == NW else bank(2 + s % 2)
            turn(pe, dst, redn[:, :] if s == 0 else xn[:, (s - 1) * C:s * C]).then_inc(sem("ga_turned"), 1)

        def project_g(pe, s):
            pe.wait_ge(sem("gnT_made"), CH * (s + 1))
            if s == 0:
                pe.wait_ge(sem("kv_copied"), NP * NW)
                mm_rows(pe, bank(4), gnT[:, 0, :], w_gq, 0, C).then_inc(sem("q_done"), 1)
                return
            if s == 2:
                pe.wait_ge(sem("q_made"), NW + 1)
            elif s == NW:
                pe.wait_ge(sem("patch_made"), NW)
            elif s >= 3:
                pe.wait_ge(sem("kv_copied"), NP * NW + s - 2)
            dst = bank(7, 0, 2 * C) if s == NW else bank(4 + s % 2, 0, 2 * C)
            mm_rows(pe, dst, gnT[:, s % 2, :], w_gkv, 0, 2 * C).then_inc(sem("kv_done"), 1)

        def pe_end(pe):
            turn_g(pe, 0)
            for s in range(NW):
                if s + 1 < NW:
                    turn_g(pe, s + 1)
                project_g(pe, s)
                if s == 2:
                    turn_local(pe, NW - 2)
                if s == 4:
                    project_mod(pe, NW - 2)
            pe.wait_ge(sem("patch_made"), NW - 1)
            pe.wait_ge(sem("kv_copied"), NP * NW + NW - 1)
            pe_start_attention(pe, 0)

            def meanwhile(half_tile):
                if half_tile == 0:
                    turn_agg(pe, NW - 1)
                if half_tile == 1:
                    project_agg(pe, NW - 1)
                if half_tile == 2:
                    turn_local(pe, NW - 1, 6)
                if half_tile == 3:
                    turn_g(pe, NW)
                if half_tile == 4:
                    pe.wait_ge(sem("local_made"), NW)
                    project_mod(pe, NW - 1, 7)
                if half_tile == 5:
                    project_g(pe, NW)
                if half_tile == 13:
                    pe.wait_ge(sem("agg_made"), 2 * (NW + 1))
                    turn(pe, bank(6), agg).then_inc(sem("aggT_done"), 1)
                if half_tile == 14:
                    pe.wait_ge(sem("aggT_copied"), NW + 1)
                    pe.wait_ge(sem("kv_copied"), NP * NW + NW)
                    mm_rows(pe, bank(7), aggT, w_gproj, 0, C).then_inc(sem("proj_done"), 1)

            for t in range(NW):
                project_tile(pe, 0, t, t + 1 < NW, meanwhile)
            turn_x(pe, 0, NW)
            project_tile(pe, 0, NW, False)
            for t, kind in SUMS_ON_PE:
                pe_sum_scores(pe, t, kind)

        def norm_g(act, s):
            normalize(act, xn[:, (s - 1) * C:s * C], local[:, (s - 1) * C:s * C], s, 1).then_inc(sem("ga_xn_made"), 1)

        def affine_g(act, s):
            act.wait_ge(sem("ga_turned"), s + 1)
            if s == 2:
                act.wait_ge(sem("q_done"), NW + 1)
            elif s >= 3:
                act.wait_ge(sem("kv_done"), NP * NW + s - 2)
            affine(act, gnT[:, s % 2, :], bank(6) if s == NW else bank(2 + s % 2), GAQ if s == 0 else GAKV, "gnT_made")

        def copy_gkv(act, s):
            act.wait_ge(sem("kv_done"), NP * NW + s)
            act.activation(g_kv[:, s - 1, :], bank(7, 0, 2 * C) if s == NW else bank(4 + s % 2, 0, 2 * C), ACT.Copy)\
               .then_inc(sem("kv_copied"), 1)

        def act_end(act):
            normalized_scales(act, "class", 0)
            act.wait_ge(sem("redT_done"), NW)
            normalize(act, redn[:, :], rows[:, 3 * C:4 * C], 0, 1).then_inc(sem("ga_xn_made"), 1)
            norm_g(act, 1)
            for s in range(NW):
                affine_g(act, s)
                if s + 2 == NW - 1:
                    normalized_scales(act, "class", 1)
                if s + 2 < NW:
                    norm_g(act, s + 2)
                if s == 1:
                    act.wait_ge(sem("q_done"), NW + 1)
                    act.activation(g_q[:, :], bank(4), ACT.Copy, scale=C ** -0.5).then_inc(sem("q_made"), 1)
                if s >= 2:
                    copy_gkv(act, s - 1)
                if s == 5:
                    exponent(act, NW - 1)
            copy_gkv(act, NW - 1)
            normalized_scales(act, "attention 0", 0)
            norm_x(act, 0, 0)
            norm_x(act, 0, 1)
            for t in range(NW):
                copy_xT(act, 0, t)
                if t + 2 in (NW - 2, NW - 1):
                    normalized_scales(act, "attention 0", t + 2 - (NW - 3))
                if t + 2 < NW:
                    norm_x(act, 0, t + 2)
                if t == 0:
                    copy_aggT(act, NW - 1)
                if t == 1:
                    act.wait_ge(sem("vprod_made"), NW)
                if t:
                    copy_qkv(act, 0, t - 1)
                if t == 1:
                    normalized_scales(act, "class", 2)
                    norm_g(act, NW)
                if t == 2:
                    affine_g(act, NW)
                if t == 3:
                    copy_gkv(act, NW)
                if t == 5:
                    exponent(act, NW)
                if t == 7:
                    copy_aggT(act, NW)
            copy_qkv(act, 0, NW - 1)
            normalized_scales(act, "attention 0", 3)
            norm_x(act, 0, NW)
            copy_xT(act, 0, NW)
            copy_qkv(act, 0, NW)
            copy_sums(act)

        def pool_end(pool):
            inverse_std(pool, *batch_of("attention 0", 0))
            inverse_std(pool, *batch_of("class", 1))
            inverse_std(pool, *batch_of("attention 0", 1))
            value_prod(pool, NW - 1)
            inverse_std(pool, *batch_of("class", 2))
            pool_scores(pool, 0, 0, 2)
            inverse_std(pool, *batch_of("attention 0", 2))
            value_prod(pool, NW)
            pool_scores(pool, 0, 2, 5)
            inverse_std(pool, *batch_of("attention 0", 3))
            pool_scores(pool, 0, 5, T)

        def dve_end(dve, link):
            add_local(dve, NW - 2)
            local_stats(dve, NW - 2)
            shift_of(dve, *batch_of("attention 0", 0))
            add_eps(dve, "class", 1)
            score(dve, NW - 1, (0,))
            shift_of(dve, *batch_of("class", 1))
            copy_localT(dve, NW - 2)
            score(dve, NW - 1, (1, 2))
            token_out(dve, NW - 2)
            add_eps(dve, "attention 0", 1)
            weigh(dve, NW - 1)
            shift_of(dve, *batch_of("attention 0", 1))
            split_bias(dve)
            for half in range(2):
                aggregate(dve, NW - 1, half)
            add_local(dve, NW - 1)
            local_stats(dve, NW - 1)
            add_eps(dve, "class", 2)
            shift_of(dve, *batch_of("class", 2))
            copy_localT(dve, NW - 1, 6)
            dve_scores(dve, link, 0, 0)
            token_out(dve, NW - 1, 7)
            add_eps(dve, "attention 0", 2)
            dve.tensor_tensor(redT[:, :], rows[:, 2 * C:3 * C], rows[:, 3 * C:4 * C], ALU.add).then_inc(sem("cls_bias"), 1)
            dve_scores(dve, link, 0, 1)
            shift_of(dve, *batch_of("attention 0", 2))
            score(dve, NW)
            weigh(dve, NW)
            dve_scores(dve, link, 0, 2)
            for half in range(2):
                aggregate(dve, NW, half)
            dve_scores(dve, link, 0, 3)
            dve.wait_ge(sem("cls_bias"), 1)
            dve.wait_ge(sem("proj_done"), NW + 1)
            dve.tensor_tensor(h_at(NW), bank(7), redT[:, :], ALU.add).then_inc(sem("patch_made"), 1)
            dve.wait_ge(sem("patch_made"), NW + 1)
            tile_stats(dve, "attention 0", NW, h_at(NW))
            add_eps(dve, "attention 0", 3)
            dve_scores(dve, link, 0, 4)
            shift_of(dve, *batch_of("attention 0", 3))
            for t in range(5, T + 1):
                dve_scores(dve, link, 0, t)

        ENDS = {"qkv_made": 2 * T, "s_made": 2, "exp_made": 2, "p_made": 2}
        HALF = T // 2
        VALUES_ON_POOL = (0, 2, 4, 6, 8)
        SUMS_ON_DVE = (1, 3, 5, 9)

        def seen(layer, name, count):
            return count + layer * ENDS.get(name, T)

        def keys(layer, t):
            return T if layer == 0 else t + 1

        def score_jobs(layer, t):
            jobs = [("row", t + 1, t in (2, 5) if layer == 0 else t % 2 == 1)]
            if layer == 0 and t:
                jobs.append(("column", t, True))
            return jobs

        SUMS_ON_PE = {(T - 3, "column"): 6, (T - 2, "column"): 0}

        def summed_on_pe(layer, t, kind):
            return layer == 0 and (t, kind) in SUMS_ON_PE

        def pool_jobs(layer):
            return [(t, kind, n) for t in range(T) for kind, n, pooled in score_jobs(layer, t) if pooled]

        def used_count(layer, i):
            done = pool_jobs(0) * layer + pool_jobs(layer)[:i + 1]
            return len(done) - sum(summed_on_pe(0, t, kind) for t, kind, _ in (pool_jobs(0) if layer else done))

        def of_query(x, t, n):
            return x[:, t * T * H16:(t * T + n) * H16]

        def score_products(eng, kind, t, n, slot):
            first, second = (C, 0) if kind == "row" else (0, C)
            return eng.tensor_tensor(slot[:, 0:n * C].rearrange("p (s c) -> p s c", s=n), a_qkv[:, 0:n, first:first + C],
                                     a_qkv[:, t, second:second + C].unsqueeze(1).broadcast_to([P, n, C]), ALU.mult)

        def score_place(kind, t, n):
            s4 = a_s[:, :].rearrange("p (t s h) -> p t s h", t=T, s=T)
            return s4[:, t, 0:n, :] if kind == "row" else s4[:, 0:n, t, :]

        def value_products(eng, layer, t, slot):
            n = keys(layer, t)
            return eng.tensor_tensor(slot[:, 0:n * C].rearrange("p (s h d) -> p s h d", s=n, d=D16),
                                     a_qkv[:, 0:n, 2 * C:3 * C].rearrange("p s (h d) -> p s h d", d=D16),
                                     of_query(a_p, t, n).rearrange("p (s h) -> p s h", s=n).unsqueeze(3)
                                     .broadcast_to([P, n, H16, D16]), ALU.mult)

        def half_scores(x, layer, g):
            nk = HALF if layer == 1 and g == 0 else T
            return x[:, :].rearrange("p (t s h) -> p t s h", t=T, s=T)[:, g * HALF:(g + 1) * HALF, 0:nk, :]

        VALUES_ON_DVE = [t for t in range(T) if t not in VALUES_ON_POOL]

        def value_slot(t):
            if t in VALUES_ON_POOL:
                return a_prod[:, 2 + VALUES_ON_POOL.index(t) % 2, :]
            return a_prod[:, VALUES_ON_DVE.index(t) % 2, :]

        def wait_value_slot(eng, layer, t):
            mine = VALUES_ON_POOL if t in VALUES_ON_POOL else VALUES_ON_DVE
            i = mine.index(t)
            if i >= 2:
                eng.wait_ge(sem("a_o_turned"), seen(layer, "o_turned", mine[i - 2] + 1))

        def pool_scores(pool, layer, first, last):
            jobs = pool_jobs(layer)
            for i, (t, kind, n) in enumerate(jobs):
                if first <= t < last:
                    pool.wait_ge(sem("a_qkv_made"), seen(layer, "qkv_made", 2 * t + 1))
                    if i >= 2 and summed_on_pe(layer, *jobs[i - 2][:2]):
                        pool.wait_ge(sem("a_summed"), list(SUMS_ON_PE).index(jobs[i - 2][:2]) + 1)
                    elif i >= 2:
                        pool.wait_ge(sem("a_pool_prod_used"), used_count(layer, i - 2))
                    score_products(pool, kind, t, n, s_slot[1 + i % 2]).then_inc(sem("a_pool_prod_made"), 1)

        def pool_attention(pool, layer):
            if layer == 1:
                pool_scores(pool, layer, 0, T)
            for t in VALUES_ON_POOL:
                pool.wait_ge(sem("a_p_made"), seen(layer, "p_made", 1 + t // HALF))
                wait_value_slot(pool, layer, t)
                value_products(pool, layer, t, value_slot(t)).then_inc(sem("a_pool_values_made"), 1)
            if layer == 0:
                for i in range(PIECES):
                    split_w_lo(pool, 0, 0, i)
            for part in range(2):
                inverse_std(pool, *batch_of("experts" if layer == 0 else "low rank", part))

        def pe_sum_scores(pe, t, kind):
            b = SUMS_ON_PE[t, kind]
            i = pool_jobs(0).index((t, kind, t))
            n, slot = t, s_slot[1 + i % 2]
            pe.wait_ge(sem("a_pool_prod_made"), i + 1)
            pe.wait_ge(sem("aggT_copied"), NW + 1)
            by_channel = slot[:, 0:n * C].rearrange("p (x d) -> p x d", d=D16)
            for ch in range(D16):
                last = pe.matmul(bank(b, 0, n * H16), ident[:, :], by_channel[:, :, ch], start=(ch == 0), stop=(ch == D16 - 1))
            last.then_inc(sem("a_summed"), 1)

        def copy_sums(act):
            for i, (t, kind) in enumerate(SUMS_ON_PE):
                act.wait_ge(sem("a_summed"), i + 1)
                act.activation(score_place(kind, t, t), bank(SUMS_ON_PE[t, kind], 0, t * H16)
                               .rearrange("p (s h) -> p s h", s=t), ACT.Copy).then_inc(sem("a_sums_copied"), 1)

        def pe_start_attention(pe, layer):
            if layer == 0:
                pe.wait_ge(sem("a_w_loaded"), 80)
                pe.wait_ge(sem("ones_made"), 5)
                pe.wait_ge(sem("bias_split"), 2)
            turn_x(pe, layer, 0)

        def turn_x(pe, layer, t):
            pe.wait_ge(sem("a_xn_made"), seen(layer, "xn_made", t + 1))
            if t >= 2:
                pe.wait_ge(sem("a_xT_made"), seen(layer, "xT_made", t - 1))
            turn(pe, bank(t % 2), a_xn[:, t % 2, :]).then_inc(sem("a_turned"), 1)

        def project_tile(pe, layer, t, turn_next, meanwhile=lambda half_tile: None):
            if turn_next:
                turn_x(pe, layer, t + 1)
            pe.wait_ge(sem("a_xT_made"), seen(layer, "xT_made", t + 1))
            if t >= 2:
                pe.wait_ge(sem("a_qkv_made"), seen(layer, "qkv_made", 2 * (t - 1)))
            for half, (dst, a, b) in enumerate(((bank(2 + t % 2, 0, 2 * C), 0, 2 * C), (bank(4 + t % 2), 2 * C, 3 * C))):
                if layer == 0:
                    pe.matmul(dst, pick[:, :], bias_r[:, a:b], start=True, stop=False)
                for c in range(CH):
                    last = pe.matmul(dst, a_xT[:, t % 2, c * P:(c + 1) * P], a_w[layer][:, c, a:b],
                                     start=(layer == 1 and c == 0), stop=(c == CH - 1))
                if half == 1:
                    last.then_inc(sem("a_qkv_done"), 1)
                meanwhile(2 * t + half)

        def pe_attention(pe, layer):
            wo = a_wo[layer]

            def turn_o(t):
                if t >= 2:
                    pe.wait_ge(sem("a_oT_made"), seen(layer, "oT_made", t - 1))
                if t in SUMS_ON_DVE:
                    pe.wait_ge(sem("a_o_made"), len(SUMS_ON_DVE) * layer + SUMS_ON_DVE.index(t) + 1)
                    turn(pe, bank(t % 2), a_o[:, t * C:(t + 1) * C]).then_inc(sem("a_o_turned"), 1)
                    return
                if t in VALUES_ON_POOL:
                    pe.wait_ge(sem("a_pool_values_made"), len(VALUES_ON_POOL) * layer + VALUES_ON_POOL.index(t) + 1)
                else:
                    summed = [q for q in VALUES_ON_DVE if q not in SUMS_ON_DVE]
                    pe.wait_ge(sem("a_dve_values_made"), len(summed) * layer + summed.index(t) + 1)
                ns = keys(layer, t)
                for c in range(CH):
                    for k in range(ns):
                        last = pe.matmul(bank(t % 2, c * P, (c + 1) * P), value_slot(t)[:, k * C + c * P:k * C + (c + 1) * P],
                                         ident[:, :], start=(k == 0), stop=(k == ns - 1))
                last.then_inc(sem("a_o_turned"), 1)

            if layer == 1:
                pe_start_attention(pe, layer)
                for t in range(T):
                    project_tile(pe, layer, t, t + 1 < T)

            def project_o(t):
                pe.wait_ge(sem("a_oT_made"), seen(layer, "oT_made", t + 1))
                if t >= 2:
                    pe.wait_ge(sem("a_h_made"), seen(layer, "h_made", t - 1))
                mm_rows(pe, bank(6 + t % 2), a_oT[:, t % 2, :], wo, 0, C).then_inc(sem("a_o_done"), 1)

            for t in range(T):
                turn_o(t)
                if t:
                    project_o(t - 1)
            project_o(T - 1)

        def norm_x(act, layer, t):
            if t >= 2:
                act.wait_ge(sem("a_turned"), seen(layer, "turned", t - 1))
            normalize(act, a_xn[:, t % 2, :], h_at(t), t, SET[f"attention {layer}"]).then_inc(sem("a_xn_made"), 1)

        def copy_xT(act, layer, t):
            act.wait_ge(sem("a_turned"), seen(layer, "turned", t + 1))
            if t >= 2:
                act.wait_ge(sem("a_qkv_done"), seen(layer, "qkv_done", t - 1))
            act.activation(a_xT[:, t % 2, :], bank(t % 2), ACT.Copy).then_inc(sem("a_xT_made"), 1)

        def copy_qkv(act, layer, t):
            act.wait_ge(sem("a_qkv_done"), seen(layer, "qkv_done", t + 1))
            act.activation(a_qkv[:, t, 0:2 * C], bank(2 + t % 2, 0, 2 * C), ACT.Copy).then_inc(sem("a_qkv_made"), 1)
            act.activation(a_qkv[:, t, 2 * C:3 * C], bank(4 + t % 2), ACT.Copy).then_inc(sem("a_qkv_made"), 1)

        def act_attention(act, layer):
            if layer == 1:
                normalized_scales(act, "attention 1", 1)
                norm_x(act, 1, 0)
                norm_x(act, 1, 1)
                for t in range(T):
                    copy_xT(act, 1, t)
                    if t + 2 < T:
                        norm_x(act, 1, t + 2)
                    if t:
                        copy_qkv(act, 1, t - 1)
                copy_qkv(act, 1, T - 1)
            for g in range(2):
                act.wait_ge(sem("a_s_made"), seen(layer, "s_made", g + 1))
                act.activation(half_scores(a_p, layer, g), half_scores(a_s, layer, g), ACT.Exp, scale=D16 ** -0.5)\
                   .then_inc(sem("a_exp_made"), 1)
            for t in range(T):
                act.wait_ge(sem("a_o_turned"), seen(layer, "o_turned", t + 1))
                if t >= 2:
                    act.wait_ge(sem("a_o_done"), seen(layer, "o_done", t - 1))
                act.activation(a_oT[:, t % 2, :], bank(t % 2), ACT.Copy).then_inc(sem("a_oT_made"), 1)
                if layer == 0 and t < PIECES:
                    split_w_hi(act, 0, 0, t)

        def split_bias(dve):
            dve.wait_ge(sem("a_w_loaded"), 80)
            dve.tensor_copy(bias_r[:, :], a_bias[:, :]).then_inc(sem("bias_split"), 1)
            dve.wait_ge(sem("bias_split"), 1)
            dve.tensor_tensor(bias_r[32:64, :], a_bias[32:64, :], bias_r[32:64, :], ALU.subtract)\
               .then_inc(sem("bias_split"), 1)

        def clip(dve, link, layer, kind, t, n):
            if layer == 1:
                st = score_place(kind, t, n)
                link(dve.tensor_scalar(st, st, -40.0, 40.0, ALU.max, ALU.min))

        def add_up(dve, kind, t, n, slot):
            return dve.tensor_reduce(score_place(kind, t, n), slot[:, 0:n * C].rearrange(
                "p (s h d) -> p s h d", s=n, d=D16), AX, ALU.add)

        def dve_scores(dve, link, layer, t):
            if t < T:
                dve.wait_ge(sem("a_qkv_made"), seen(layer, "qkv_made", 2 * t + 1))
                for kind, n, on_pool in score_jobs(layer, t):
                    if not on_pool:
                        link(score_products(dve, kind, t, n, s_slot[0]))
                        link(add_up(dve, kind, t, n, s_slot[0]))
                        clip(dve, link, layer, kind, t, n)
            before = len(pool_jobs(0)) * layer
            for i, (at, kind, n) in enumerate(pool_jobs(layer)):
                if at == t - 1 and not summed_on_pe(layer, at, kind):
                    dve.wait_ge(sem("a_pool_prod_made"), before + i + 1)
                    add_up(dve, kind, at, n, s_slot[1 + i % 2]).then_inc(sem("a_pool_prod_used"), 1)
                    dve.wait_ge(sem("a_pool_prod_used"), used_count(layer, i))
                    clip(dve, link, layer, kind, at, n)

        def dve_attention(dve, layer, link):
            if layer == 1:
                link(dve.memset(a_s[:, :], NEG4))
                for t in range(T + 1):
                    dve_scores(dve, link, 1, t)
            s4 = a_s[:, :].rearrange("p (t s h) -> p t s h", t=T, s=T)
            if layer == 0:
                dve.wait_ge(sem("a_sums_copied"), len(SUMS_ON_PE))
                link(dve.memset(s4[:, 0, T - 1, :], NEG4))
                link(dve.memset(s4[:, T - 1, 0, :], NEG4))

            def half(x, g):
                return x[:, g * HALF * H16:(g + 1) * HALF * H16].rearrange("p (t h) -> p t h", t=HALF)

            def over_s(x, g, nk):
                return half(x, g).unsqueeze(2).broadcast_to([P, HALF, nk, H16])

            for g in range(2):
                s_g = half_scores(a_s, layer, g)
                link(dve.tensor_reduce(half(a_max, g), s_g.rearrange("p t s h -> p t h s"), AX, ALU.max))
                dve.tensor_tensor(s_g, s_g, over_s(a_max, g, s_g.shape[2]), ALU.subtract).then_inc(sem("a_s_made"), 1)
            for g in range(2):
                p_g = half_scores(a_p, layer, g)
                dve.wait_ge(sem("a_exp_made"), seen(layer, "exp_made", g + 1))
                link(dve.tensor_reduce(half(a_den, g), p_g.rearrange("p t s h -> p t h s"), AX, ALU.add))
                link(dve.reciprocal(half(a_rden, g), half(a_den, g)))
                dve.tensor_tensor(p_g, p_g, over_s(a_rden, g, p_g.shape[2]), ALU.mult).then_inc(sem("a_p_made"), 1)
            dve.wait_ge(sem("a_p_made"), seen(layer, "p_made", 2))
            added = 0
            for t in VALUES_ON_DVE:
                wait_value_slot(dve, layer, t)
                ins = value_products(dve, layer, t, value_slot(t))
                if t in SUMS_ON_DVE:
                    link(ins)
                    dve.tensor_reduce(a_o[:, t * C:(t + 1) * C],
                                      value_slot(t)[:, 0:keys(layer, t) * C].rearrange("p (s c) -> p c s", c=C), AX, ALU.add)\
                       .then_inc(sem("a_o_made"), 1)
                else:
                    ins.then_inc(sem("a_dve_values_made"), 1)
                while added < t - 3:
                    add_o(dve, layer, added)
                    added += 1
            following = "experts" if layer == 0 else "low rank"
            for t in range(added, T):
                add_o(dve, layer, t)
                if t == T - BT - 1:
                    add_eps(dve, following, 0)
                if t == T - BT:
                    shift_of(dve, *batch_of(following, 0))
            end_stats(dve, following, 1)

        def add_o(dve, layer, t):
            dve.wait_ge(sem("a_o_done"), seen(layer, "o_done", t + 1))
            dve.tensor_tensor(h_at(t), bank(6 + t % 2), h_at(t), ALU.add).then_inc(sem("a_h_made"), 1)
            dve.wait_ge(sem("a_h_made"), seen(layer, "h_made", t + 1))
            tile_stats(dve, "experts" if layer == 0 else "low rank", t, h_at(t))

        def top_two(dve, link, x, t8, ti, tf, count):
            for t in range(count):
                dve.max(t8[:, t, :], x[:, t, :])
            link(dve.memset(spare[:, :], 0.0))
            for t in range(count):
                dve.max_index(ti[:, t, :], t8[:, t, :], x[:, t, :])
            link(dve.memset(spare[:, :], 0.0))
            link(dve.tensor_copy(tf[:, :, :], ti[:, :, 0:2]))

        def spread(dve, link, tf, w, hots, dst, n):
            for j in range(2):
                link(dve.tensor_tensor(hots[:, j], iota[:, 0:n].unsqueeze(1).broadcast_to([P, T, n]),
                                       tf[:, :, j:j + 1].broadcast_to([P, T, n]), ALU.is_equal))
                link(dve.tensor_tensor(hots[:, j], hots[:, j], w[:, :, j:j + 1].broadcast_to([P, T, n]), ALU.mult))
            link(dve.tensor_tensor(dst[:, :, :], hots[:, 0], hots[:, 1], ALU.add))

        STEPS = 2 * NB * FC
        LAG = 3
        START = {"gelu_made": 2, "hid_made": 2, "down_made": FC, "res_made": 2, "gm_made": 2}

        def made(name, count):
            return count + START.get(name, 0)

        def where(j):
            par, r = divmod(j, NB * FC)
            b, fc = divmod(r, FC)
            return par, b, fc, par * NB + b

        def turn_bank(t):
            return bank((0, 1, 4, 5)[t % 4])

        def pe_experts(pe):
            pe.wait_ge(sem("moe_small_loaded"), 32)
            def turn_x2(t):
                pe.wait_ge(sem("x2_made"), t + 1)
                if t >= 4:
                    pe.wait_ge(sem("x2T_made"), t - 3)
                turn(pe, turn_bank(t), x2[:, t * C:(t + 1) * C]).then_inc(sem("x2_turned"), 1)

            turn_x2(0)
            turn_x2(1)
            for t in range(T):
                if t + 2 < T:
                    turn_x2(t + 2)
                pe.wait_ge(sem("x2T_made"), t + 1)
                if t >= 2:
                    pe.wait_ge(sem("lg_made"), t - 1)
                mm_rows(pe, bank(2 + t % 2, 0, E), x2T[:, t, :], w_rt, 0, E).then_inc(sem("lg_done"), 1)
            pe.wait_ge(sem("lg_made"), T)
            pe.wait_ge(sem("xT_split"), 2 * T)

            def turn_gates(b):
                pe.wait_ge(sem("gates_made"), 1)
                if b:
                    pe.wait_ge(sem("gT_made"), b)
                for u in range(BT):
                    last = pe.transpose(bank(6, u * C, u * C + P)[0:E, :], gates[:, BT * b + u, :], ident[:, :])
                last.then_inc(sem("g_turned"), 1)

            def times_beta(b):
                pe.wait_ge(sem("gT_made"), b + 1)
                if b:
                    pe.wait_ge(sem("beta_added"), b)
                for u in range(BT):
                    last = pe.matmul(bank(7, u * C, (u + 1) * C), gT[:, BT * b + u, :], beta[:, :], start=True, stop=True)
                last.then_inc(sem("beta_done"), 1)

            def up(ep, j):
                par, b, fc, blk = where(j)
                if b == 0 and fc == 0:
                    pe.wait_ge(sem("w_lo_made"), PIECES * (2 * ep + par + 1))
                pe.wait_ge(sem("gelu_made"), made("gelu_made", STEPS * ep + j - 1))
                for c in range(CH):
                    at = c * FF + fc * P
                    last = mm3(pe, bank(fc % 2), (w1_hi[par][:, at:at + P], w1_lo[par][:, at:at + P]),
                               (xT_hi[:, c, b * BW:(b + 1) * BW], xT_lo[:, c, b * BW:(b + 1) * BW]), c == 0, c == CH - 1)
                last.then_inc(sem("up_done"), 1)

            def down(ep, j):
                par, b, fc, blk = where(j)
                pe.wait_ge(sem("hid_made"), made("hid_made", STEPS * ep + j + 1))
                if fc == 0:
                    pe.wait_ge(sem("res_made"), made("res_made", 2 * NB * ep + blk - 1))
                for u in range(BT):
                    last = mm3(pe, pair[1 + blk % 2][:, u, 0:C],
                               (hid_hi[:, fc, u * P:(u + 1) * P], hid_lo[:, fc, u * P:(u + 1) * P]),
                               (w2_hi[par][:, fc * C:(fc + 1) * C], w2_lo[par][:, fc * C:(fc + 1) * C]),
                               fc == 0, fc == FC - 1)
                last.then_inc(sem("down_made"), 1)

            for g in range(E // 2 * STEPS + LAG):
                if g < E // 2 * STEPS:
                    up(*divmod(g, STEPS))
                if g >= LAG:
                    down(*divmod(g - LAG, STEPS))
                if g < NB * FC:
                    b, fc = divmod(g, FC)
                    if fc == 2:
                        turn_gates(b)
                    if fc == 6:
                        times_beta(b)

        def load_expert(sp, e):
            rows_of = slice(e * P, (e + 1) * P)
            sp.dma_start(w1raw[e % 2][:, :], d["w1"][rows_of, :]).then_inc(sem(f"w_loaded{e % 2}"), 16)
            sp.dma_start(w2raw[e % 2][:, :], d["w2"][rows_of, :]).then_inc(sem(f"w_loaded{e % 2}"), 16)

        def load_vectors(sp, e):
            par = e % 2
            sp.dma_start(b1[par][:, :], d["b1"][:, e * FC:(e + 1) * FC]).then_inc(sem(f"v_loaded{par}"), 16)
            for dst, name in ((b2, "b2"), (gam, "gamma")):
                sp.dma_start(dst[par][:, :], d[name][:, e * C:(e + 1) * C].broadcast_to([P, C]))\
                  .then_inc(sem(f"v_loaded{par}"), 16)

        def piece(j):
            r = j % (NB * FC)
            return r // 4 if r % 4 == 2 and r // 4 < PIECES else None

        def weight_piece(par, i):
            n = CH * FF * 2 // PIECES
            a = (i % 4) * n
            return [x[par][:, a:a + n] for x in ((w1raw, w1_hi, w1_lo) if i < 4 else (w2raw, w2_hi, w2_lo))]

        def split_w_hi(act, ep, par, i):
            raw, hi, _ = weight_piece(par, i)
            if i == 0:
                act.wait_ge(sem(f"w_loaded{par}"), 32 * (ep + 1))
                if 2 * ep + par > 1:
                    act.wait_ge(sem("down_made"), made("down_made", NB * FC * (2 * ep + par - 1)))
            act.activation(hi, raw, ACT.Copy).then_inc(sem("w_hi_made"), 1)

        def split_w_lo(pool, ep, par, i):
            raw, hi, lo = weight_piece(par, i)
            if i == 0 and 2 * ep + par > 1:
                pool.wait_ge(sem("down_made"), made("down_made", NB * FC * (2 * ep + par - 1)))
            pool.wait_ge(sem("w_hi_made"), PIECES * (2 * ep + par) + i + 1)
            pool.tensor_tensor(lo, raw, hi, ALU.subtract).then_inc(sem("w_lo_made"), 1)

        def act_experts(act):
            act.sem_inc(sem("gelu_made"), START["gelu_made"])
            normalized_scales(act, "experts", 0)

            def norm(t):
                if t == T - BT:
                    normalized_scales(act, "experts", 1)
                normalize(act, x2[:, t * C:(t + 1) * C], h_at(t), t, 1).then_inc(sem("x2_made"), 1)

            for t in range(3):
                norm(t)
            for t in range(T):
                if t + 3 < T:
                    norm(t + 3)
                act.wait_ge(sem("x2_turned"), t + 1)
                act.activation(x2T[:, t, :], turn_bank(t), ACT.Copy).then_inc(sem("x2T_made"), 1)
            act.wait_ge(sem("tw_made"), 1)
            act.activation(te[:, :, :], tw[:, :, :], ACT.Exp).then_inc(sem("te_made"), 1)
            act.activation(warm[:, :], iota[:, 0:2], ACT.Gelu).then_inc(sem("table_loaded"), 1)
            def copy_gT(b):
                act.wait_ge(sem("g_turned"), b + 1)
                act.activation(gT[:, BT * b:BT * b + BT, :], bank(6, 0, 2 * C)[0:E, :]
                               .rearrange("e (u c) -> e u c", u=BT)[:, :, 0:P], ACT.Copy).then_inc(sem("gT_made"), 1)

            def experts(ep, end):
                for j in range(STEPS):
                    par, b, fc, blk = where(j)
                    g = STEPS * ep + j
                    if b == 0 and fc == 0:
                        act.wait_ge(sem(f"v_loaded{par}"), 48 * (ep + 1))
                    act.wait_ge(sem("hid_made"), made("hid_made", g - 1))
                    act.wait_ge(sem("up_done"), g + 1)
                    act.activation(gel[:, fc % 2, :], bank(fc % 2), ACT.Gelu,
                                   bias=b1[par][:, fc:fc + 1]).then_inc(sem("gelu_made"), 1)
                    if ep == 0 and par == 0 and fc == 3:
                        copy_gT(b)
                    if piece(j) is not None and not (end and par == 1):
                        split_w_hi(act, ep + par, 1 - par, piece(j))

            for ep in range(E // 2):
                experts(ep, ep == E // 2 - 1)

        def pool_experts(pool):
            pool.sem_inc(sem("gm_made"), START["gm_made"])
            pool.wait_ge(sem("x2_made"), T)

            def block_input(ep, blk):
                par, b = divmod(blk, NB)
                if b == 0:
                    pool.wait_ge(sem(f"v_loaded{par}"), 48 * (ep + 1))
                pool.wait_ge(sem("res_made"), made("res_made", 2 * NB * ep + blk))
                pool.tensor_tensor(xb[:, :].rearrange("p (u c) -> p u c", u=BT),
                                   x2[:, b * BT * C:(b + 1) * BT * C].rearrange("p (u c) -> p u c", u=BT),
                                   b2[par][:, :].unsqueeze(1).broadcast_to([P, BT, C]), ALU.add)\
                    .then_inc(sem("xb_made"), 1)

            def block_scale(ep, blk):
                pool.wait_ge(sem("bvar_made"), 2 * NB * ep + blk + 1)
                pool.tensor_tensor(brs[:, :], bve[:, :], mhalf[:, 0:BT], ALU.pow).then_inc(sem("brstd_made"), 1)

            def block_output(ep, blk):
                par, b = divmod(blk, NB)
                n = 2 * NB * ep + blk
                pool.wait_ge(sem("nr_made"), BT * (n + 1))
                pool.tensor_tensor(gm[:, :].rearrange("p (u c) -> p u c", u=BT),
                                   nr[:, blk % 2, :].rearrange("p (u c) -> p u c", u=BT),
                                   gam[par][:, :].unsqueeze(1).broadcast_to([P, BT, C]), ALU.mult)\
                    .then_inc(sem("gm_made"), 1)
                pool.wait_ge(sem("gm_made"), made("gm_made", n + 1))
                if ep == 0 and par == 0:
                    pool.wait_ge(sem("beta_added"), b + 1)
                pool.tensor_tensor(h_at(BT * b, BT), h_at(BT * b, BT), gm[:, :], ALU.add).then_inc(sem("y_added"), 1)
                pool.wait_ge(sem("y_added"), n + 1)

            for n in range(E * NB):
                ep, blk = divmod(n, 2 * NB)
                if n == 0:
                    block_input(0, 0)
                else:
                    before = divmod(n - 1, 2 * NB)
                    block_scale(*before)
                    block_input(ep, blk)
                    block_output(*before)
                par = blk // NB
                for j in range(blk * FC, (blk + 1) * FC):
                    if piece(j) is not None and 2 * ep + par < E - 1:
                        split_w_lo(pool, ep + par, 1 - par, piece(j))
            last = divmod(E * NB - 1, 2 * NB)
            block_scale(*last)
            inverse_std(pool, *batch_of("attention 1", 0))
            block_output(*last)
            inverse_std(pool, *batch_of("attention 1", 1))

        def dve_experts(dve):
            link = Chain(dve, "moe_link")
            for name in ("hid_made", "res_made", "down_made"):
                dve.sem_inc(sem(name), START[name])

            def copy_logits(t):
                dve.wait_ge(sem("lg_done"), t + 1)
                dve.tensor_copy(lg[:, t, :], bank(2 + t % 2, 0, E)).then_inc(sem("lg_made"), 1)

            for t in range(T):
                dve.wait_ge(sem("x2T_made"), t + 1)
                src = x2T[:, t, :].rearrange("p (c b) -> p c b", c=CH)
                at = slice(t * P, (t + 1) * P)
                dve.tensor_copy(xT_hi[:, :, at], src).then_inc(sem("xT_split"), 1)
                dve.wait_ge(sem("xT_split"), 2 * t + 1)
                dve.tensor_tensor(xT_lo[:, :, at], src, xT_hi[:, :, at], ALU.subtract).then_inc(sem("xT_split"), 1)
                if t:
                    copy_logits(t - 1)
            copy_logits(T - 1)
            dve.wait_ge(sem("lg_made"), T)
            top_two(dve, link, lg, top, topi, topf, T)
            dve.tensor_tensor(tw[:, :, :], top[:, :, 0:2], top[:, :, 0:1].broadcast_to([P, T, 2]), ALU.subtract)\
               .then_inc(sem("tw_made"), 1)
            dve.wait_ge(sem("te_made"), 1)
            link(dve.tensor_reduce(tsum[:, :], te[:, :, :], AX, ALU.add))
            link(dve.reciprocal(trec[:, :], tsum[:, :]))
            link(dve.tensor_tensor(tw[:, :, :], te[:, :, :], trec[:, :].unsqueeze(2).broadcast_to([P, T, 2]), ALU.mult))
            spread(dve, link, topf, tw, hot, gates, E)
            dve.tensor_copy(gat_e[:, :].rearrange("p (e t) -> p t e", e=E), gates[:, :, :]).then_inc(sem("gates_made"), 1)
            dve.wait_ge(sem("gates_made"), 1)
            def split_hidden(ep, j):
                par, b, fc, blk = where(j)
                g = STEPS * ep + j
                dve.wait_ge(sem("down_made"), made("down_made", g + 1 - FC))
                dve.wait_ge(sem("gelu_made"), made("gelu_made", g + 1))
                dve.tensor_copy(hid_hi[:, fc, :], gel[:, fc % 2, :]).then_inc(sem("hid_hi_made"), 1)
                dve.wait_ge(sem("hid_hi_made"), g + 1)
                dve.tensor_tensor(hid_lo[:, fc, :], gel[:, fc % 2, :], hid_hi[:, fc, :], ALU.subtract)\
                   .then_inc(sem("hid_made"), 1)

            def block_stats(ep, blk):
                n = 2 * NB * ep + blk
                dve.wait_ge(sem("xb_made"), n + 1)
                dve.wait_ge(sem("down_made"), made("down_made", FC * (n + 1)))
                dve.tensor_tensor(res[:, :].rearrange("p (u c) -> p u c", u=BT), pair[1 + blk % 2][:, :, 0:C],
                                  xb[:, :].rearrange("p (u c) -> p u c", u=BT), ALU.add).then_inc(sem("res_made"), 1)
                dve.wait_ge(sem("res_made"), made("res_made", n + 1))
                for u in range(BT):
                    dve.bn_stats(bst[:, u, :], res[:, u * C:(u + 1) * C]).then_inc(sem("bstats_made"), 1)
                dve.wait_ge(sem("bstats_made"), BT * (n + 1))
                dve.tensor_copy(spare[:, 0:1], spare[:, 1:2]).then_inc(sem("spacer"), 1)
                for u in range(BT):
                    dve.bn_aggr(bmv[:, u, :], bst[:, u, :]).then_inc(sem("baggr_made"), 1)
                dve.wait_ge(sem("baggr_made"), BT * (n + 1))
                dve.tensor_scalar(bve[:, :], bmv[:, :, 1], 1e-6, None, ALU.add).then_inc(sem("bvar_made"), 1)

            def block_normalize(ep, blk):
                par, b = divmod(blk, NB)
                n = 2 * NB * ep + blk
                dve.wait_ge(sem("brstd_made"), n + 1)
                dve.tensor_tensor(bsc[:, :], brs[:, :], gat_e[:, bass.ds((2 * ep + par) * T + BT * b, BT)], ALU.mult)\
                   .then_inc(sem("bscale_made"), 1)
                dve.wait_ge(sem("bscale_made"), n + 1)
                dve.wait_ge(sem("gm_made"), made("gm_made", n - 1))
                for u in range(BT):
                    dve.tensor_scalar(nr[:, blk % 2, u * C:(u + 1) * C], res[:, u * C:(u + 1) * C], bmv[:, u, 0:1],
                                      bsc[:, u:u + 1], ALU.subtract, ALU.mult).then_inc(sem("nr_made"), 1)
                dve.wait_ge(sem("nr_made"), BT * (n + 1))

            def add_beta(b):
                dve.wait_ge(sem("beta_done"), b + 1)
                dve.tensor_tensor(h_at(BT * b, BT), bank(7, 0, BT * C), h_at(BT * b, BT), ALU.add).then_inc(sem("beta_added"), 1)

            def finished(b):
                dve.wait_ge(sem("y_added"), NB * (E - 1) + b + 1)
                for t in range(BT * b, BT * b + BT):
                    tile_stats(dve, "attention 1", t, h_at(t))

            for g in range(E // 2 * STEPS):
                ep, j = divmod(g, STEPS)
                par, b, fc, blk = where(j)
                split_hidden(ep, j)
                if g >= FC and fc == 3:
                    block_stats(*divmod(g // FC - 1, 2 * NB))
                if g >= FC and fc == 5:
                    block_normalize(*divmod(g // FC - 1, 2 * NB))
                if g < NB * FC and fc == 7:
                    add_beta(b)
                if 2 * ep + par == E - 1 and b >= 2 and fc == 6:
                    finished(b - 2)
            block_stats(*divmod(E * NB - 1, 2 * NB))
            finished(NB - 2)
            add_eps(dve, "attention 1", 0)
            block_normalize(*divmod(E * NB - 1, 2 * NB))
            shift_of(dve, *batch_of("attention 1", 0))
            finished(NB - 1)
            end_stats(dve, "attention 1", 1)

        def out_bank(t, n=1):
            b = (4, 5, 6, 7, 2)[t // 2]
            return bank(b, t % 2 * C, (t % 2 + n) * C)

        def pe_lora(pe):
            pe.wait_ge(sem("z_loaded"), 64)
            def turn_z(t):
                pe.wait_ge(sem("z_xn_made"), t + 1)
                if t >= 4:
                    pe.wait_ge(sem("z_xT_made"), t - 3)
                turn(pe, turn_bank(t), z_xn[:, t % 4, :]).then_inc(sem("z_turned"), 1)

            turn_z(0)
            turn_z(1)
            for t in range(T):
                if t + 2 < T:
                    turn_z(t + 2)
                pe.wait_ge(sem("z_xT_made"), t + 1)
                if t >= 2:
                    pe.wait_ge(sem("z_made"), t - 1)
                mm_rows(pe, bank(2 + t % 2, 0, ZW), z_xT[:, t, :], z_w, 0, ZW).then_inc(sem("z_done"), 1)
            pe.wait_ge(sem("z_made"), T)
            for t in range(T):
                for c in range(CH):
                    pe.matmul(out_bank(t), z_xT[:, t, c * P:(c + 1) * P], z_base[:, c, :],
                              start=(c == 0 and t % 2 == 0), stop=False)
            for t in range(T + 1):
                if t < T:
                    pe.wait_ge(sem("z_s_made"), 2 * (t + 1))
                    if t >= 2:
                        pe.wait_ge(sem("z_sT_made"), t - 1)
                    pe.transpose(bank(t % 2, 0, P)[0:LOW, :], z_s[:, t, :], ident[:, :]).then_inc(sem("z_s_turned"), 1)
                if t:
                    pe.wait_ge(sem("z_sT_made"), t)
                    pe.matmul(out_bank(t - 1), z_sT[0:LOW, (t - 1) % 2, :], z_b[:, :], start=False, stop=(t % 2 == 0))\
                      .then_inc(sem("z_out_done"), 1)

        def act_lora(act):
            normalized_scales(act, "low rank", 0)
            def norm(t):
                if t == T - BT:
                    normalized_scales(act, "low rank", 1)
                if t >= 4:
                    act.wait_ge(sem("z_turned"), t - 3)
                normalize(act, z_xn[:, t % 4, :], h_at(t), t, 1).then_inc(sem("z_xn_made"), 1)

            for t in range(3):
                norm(t)
            for t in range(T):
                if t + 3 < T:
                    norm(t + 3)
                act.wait_ge(sem("z_turned"), t + 1)
                act.activation(z_xT[:, t, :], turn_bank(t), ACT.Copy).then_inc(sem("z_xT_made"), 1)
            act.wait_ge(sem("z_l_made"), 1)
            act.activation(z_p[:, :, :], z_l[:, :, :], ACT.Exp).then_inc(sem("z_exp_made"), 1)
            for t in range(T):
                act.wait_ge(sem("z_s_turned"), t + 1)
                if t >= 2:
                    act.wait_ge(sem("z_out_done"), t - 1)
                act.activation(z_sT[0:LOW, t % 2, :], bank(t % 2, 0, P)[0:LOW, :], ACT.Copy).then_inc(sem("z_sT_made"), 1)

        def dve_lora(dve):
            link = Chain(dve, "z_link")
            dve.wait_ge(sem("z_loaded"), 64)
            link(dve.memset(z_g[:, :, :], -1.0))
            for t in range(T):
                dve.wait_ge(sem("z_done"), t + 1)
                dve.tensor_copy(z[:, t, :], bank(2 + t % 2, 0, ZW)).then_inc(sem("z_made"), 1)
                dve.tensor_tensor(h_at(t), h_at(t), z_rows[:, 0:C], ALU.add).then_inc(sem("z_h_made"), 1)
            dve.wait_ge(sem("z_made"), T)
            over = lambda x, n: x[:, :].unsqueeze(2).broadcast_to([P, T, n])
            link(dve.tensor_tensor(z_l[:, :, :], z[:, :, LOW:ZW],
                                   z_rows[:, C:C + E6].unsqueeze(1).broadcast_to([P, T, E6]), ALU.add))
            link(dve.tensor_reduce(z_max[:, :], z_l[:, :, :], AX, ALU.max))
            dve.tensor_tensor(z_l[:, :, :], z_l[:, :, :], over(z_max, E6), ALU.subtract).then_inc(sem("z_l_made"), 1)
            dve.wait_ge(sem("z_exp_made"), 1)
            link(dve.tensor_reduce(z_sum[:, :], z_p[:, :, :], AX, ALU.add))
            link(dve.reciprocal(z_rec[:, :], z_sum[:, :]))
            link(dve.tensor_tensor(z_g[:, :, 0:E6], z_p[:, :, :], over(z_rec, E6), ALU.mult))
            top_two(dve, link, z_g, z_top, z_topi, z_topf, T)
            link(dve.tensor_reduce(z_sum[:, :], z_top[:, :, 0:2], AX, ALU.add))
            link(dve.tensor_scalar(z_sum[:, :], z_sum[:, :], 1e-6, None, ALU.add))
            link(dve.reciprocal(z_rec[:, :], z_sum[:, :]))
            link(dve.tensor_tensor(z_tw[:, :, :], z_top[:, :, 0:2], over(z_rec, 2), ALU.mult))
            spread(dve, link, z_topf, z_tw, z_hot, z_sw, E6)
            for t in range(T):
                dve.tensor_copy(z_s[:, t, 0:R16], z[:, t, 0:R16]).then_inc(sem("z_s_made"), 1)
                dve.tensor_tensor(z_s[:, t, R16:LOW].rearrange("p (e r) -> p e r", e=E6),
                                  z[:, t, R16:LOW].rearrange("p (e r) -> p e r", e=E6),
                                  z_sw[:, t, :].unsqueeze(2).broadcast_to([P, E6, R16]), ALU.mult)\
                   .then_inc(sem("z_s_made"), 1)
            dve.wait_ge(sem("z_h_made"), T)
            for t in range(0, T, 2):
                dve.wait_ge(sem("z_out_done"), t + 2)
                dve.tensor_tensor(z_o[:, t:t + 2, :], out_bank(t, 2), h_at(t, 2), ALU.add).then_inc(sem("z_out_made"), 1)

        @block.sync
        def _(sp):
            sp.dma_start(wc_raw[:, 0:4, :], d["conv_main"].rearrange("p (c n) -> p c n", c=4)).then_inc(sem("wc_loaded"), 16)
            sp.wait_ge(sem("pads_zeroed"), 2)
            sp.dma_start(wc_raw[0:KREST, 4, :], d["conv_rest"]).then_inc(sem("wc_loaded"), 16)
            for g in range(NP // GRP):
                load_x(sp, 0, g, first=True)
            two = lambda name: d[name].rearrange("(c p) n -> p c n", p=P)
            sp.dma_start(wkv_raw[:, :, :], two("la_wkv")).then_inc(sem("wkv_loaded"), 16)
            sp.dma_start(vecs[:, :], d["vecs"]).then_inc(sem("wkv_loaded"), 16)
            sp.dma_start(rows[:, :], d["rows"].broadcast_to([P, len(ROWS) * C])).then_inc(sem("wkv_loaded"), 16)
            for dst, name in ((w_q, "la_wq"), (w_proj, "la_proj_w"), (w_mod, "mod_w"), (w_gq, "ga_wq"),
                              (w_gkv, "ga_wkv"), (w_gproj, "ga_proj_w")):
                sp.dma_start(dst[:, :, :], two(name)).then_inc(sem("tok_w_loaded"), 16)
            with sp.Fori(1, NW) as n:
                for g in range(NP // GRP):
                    load_x(sp, n, g)
            sp.wait_ge(sem("x_lo_made"), NP * NW)
            for layer in range(2):
                sp.dma_start(a_w[layer][:, :, :], two(f"qkv_w{layer}")).then_inc(sem("a_w_loaded"), 16)
                sp.dma_start(a_wo[layer][:, :, :], two(f"o_w{layer}")).then_inc(sem("a_w_loaded"), 16)
            sp.dma_start(a_bias[:, :], d["qkv_b"].broadcast_to([64, QKV])).then_inc(sem("a_w_loaded"), 16)
            phase(sp, 1)
            sp.wait_ge(sem("a_s_made"), 2)
            for e in range(2):
                load_expert(sp, e)
            sp.dma_start(w_rt[:, :, :], two("router_w")).then_inc(sem("moe_small_loaded"), 16)
            sp.dma_start(beta[:, :], d["beta"]).then_inc(sem("moe_small_loaded"), 16)
            for e in range(2):
                load_vectors(sp, e)
            phase(sp, 2)
            for e in range(2, E):
                sp.wait_ge(sem("w_lo_made"), PIECES * (e - 1))
                load_expert(sp, e)
                sp.wait_ge(sem("y_added"), NB * (e - 1))
                load_vectors(sp, e)
            phase(sp, 3)
            sp.dma_start(z_w[:, :, :], two("z_w")).then_inc(sem("z_loaded"), 16)
            sp.dma_start(z_b[:, :], d["z_b"]).then_inc(sem("z_loaded"), 16)
            sp.dma_start(z_base[:, :, :], two("base_w")).then_inc(sem("z_loaded"), 16)
            sp.dma_start(z_rows[:, :], d["z_rows"].broadcast_to([P, C + E6])).then_inc(sem("z_loaded"), 16)
            phase(sp, 4)
            for i in range(T // 2):
                sp.wait_ge(sem("z_out_made"), i + 1)
                sp.dma_start(out[:, 2 * i:2 * i + 2, :], z_o[:, 2 * i:2 * i + 2, :]).then_inc(sem("stored"), 16)
            sp.wait_ge(sem("stored"), 16 * (T // 2))

        @block.gpsimd
        def _(pool):
            pool.memset(ident[:, :], 0.0).then_inc(sem("ident_zeroed"), 1)
            pool.memset(mhalf[:, :], -0.5).then_inc(sem("consts_made"), 1)
            pool.memset(xraw[:, :, 4, :], 0.0).then_inc(sem("pads_zeroed"), 1)
            pool.wait_ge(sem("ident_zeroed"), 1)
            pool.affine_select(out=ident[:, :], in_=ident[:, :], compare_op=ALU.not_equal, fill=1.0,
                               base=0, pattern=[[-1, P]], channel_multiplier=1).then_inc(sem("consts_made"), 1)
            pool.iota(iota[:, :], pattern=[[1, 8]], base=0, channel_multiplier=0,
                      allow_small_or_imprecise_dtypes=True).then_inc(sem("consts_made"), 1)
            for k in range(NP):
                split_x_lo(pool, 0, k)
            pool.wait_ge(sem("consts_made"), 1)
            inverse_std(pool, 0)
            for k in range(EARLY):
                split_x_lo(pool, 1, k)
            round_pool(pool, 0, True, False, False)
            for n in range(1, NW - 2):
                round_pool(pool, n, False, False, False)
            round_pool(pool, NW - 2, False, False, True)
            round_pool(pool, NW - 1, False, True, False)
            pool_end(pool)
            phase(pool, 1)
            pool_attention(pool, 0)
            phase(pool, 2)
            pool_experts(pool)
            phase(pool, 3)
            pool_attention(pool, 1)
            phase(pool, 4)

        @block.tensor
        def _(pe):
            pe.wait_ge(sem("consts_made"), 3)
            pe.wait_ge(sem("wc_made"), 2)
            for k in range(NP):
                conv(pe, 0, k)
            pe.wait_ge(sem("bias_columns"), CH)
            mm_rows(pe, bank(4, 0, 2 * C), aggT, wkv_raw, 0, 2 * C).then_inc(sem("kvb_done"), 1)
            pe.wait_ge(sem("wkv_lo_made"), CH)
            pe.wait_ge(sem("kvb_made"), 1)
            pe.wait_ge(sem("tok_w_loaded"), 96)
            round_pe(pe, 0, True, False)
            for n in range(1, NW - 1):
                round_pe(pe, n, False, False)
            round_pe(pe, NW - 1, False, True)
            pe_end(pe)
            phase(pe, 1)
            pe_attention(pe, 0)
            phase(pe, 2)
            pe_experts(pe)
            phase(pe, 3)
            pe_attention(pe, 1)
            phase(pe, 4)
            pe_lora(pe)

        @block.scalar
        def _(act):
            act.wait_ge(sem("wc_loaded"), 32)
            act.activation(wc_hi[:, :, :], wc_raw[:, :, :], ACT.Copy).then_inc(sem("wc_made"), 1)
            for k in range(NP):
                split_x_hi(act, 0, k)
                if k >= 2:
                    copy_pe(act, 0, k - 2)
            for k in (NP - 2, NP - 1):
                copy_pe(act, 0, k)
            for k in range(EARLY):
                split_x_hi(act, 1, k)
            act.wait_ge(sem("wkv_scaled"), 2)
            for c in range(CH):
                act.activation(wkv_hi[:, c, :], wkv_raw[:, c, :], ACT.Copy).then_inc(sem("wkv_hi_made"), 1)
            round_act(act, 0, True, False, False)
            for n in range(1, NW - 2):
                round_act(act, n, False, False, False)
            round_act(act, NW - 2, False, False, True)
            round_act(act, NW - 1, False, True, False)
            act_end(act)
            phase(act, 1)
            act_attention(act, 0)
            phase(act, 2)
            act_experts(act)
            phase(act, 3)
            act_attention(act, 1)
            phase(act, 4)
            act_lora(act)

        @block.vector
        def _(dve):
            dve.memset(wc_raw[:, 4, :], 0.0).then_inc(sem("pads_zeroed"), 1)
            dve.memset(spare[:, :], 0.0).then_inc(sem("ones_made"), 1)
            dve.memset(attn[:, NP * H8:], 1.0).then_inc(sem("ones_made"), 1)
            dve.wait_ge(sem("wc_made"), 1)
            dve.tensor_tensor(wc_lo[:, :, :], wc_raw[:, :, :], wc_hi[:, :, :], ALU.subtract).then_inc(sem("wc_made"), 1)
            dve.memset(pick[:, :].bitcast(F32), 0.0).then_inc(sem("ones_made"), 1)
            dve.wait_ge(sem("ones_made"), 3)
            for row in (0, 32):
                dve.memset(pick[row:row + 1, :].bitcast(F32), 1.0).then_inc(sem("ones_made"), 1)
            dve.wait_ge(sem("wkv_loaded"), 48)
            for c in range(CH):
                dve.tensor_copy(aggT[:, c * P:(c + 1) * P], vecs[:, LAKV + 2 + c:LAKV + 3 + c].broadcast_to([P, P]))\
                   .then_inc(sem("bias_columns"), 1)
            for k in range(NP):
                measure(dve, 0, k)
            reduce_window(dve, 0)
            dve.wait_ge(sem("kvb_done"), 1)
            dve.tensor_copy(kv_sb[:, NP, :], bank(4, 0, 2 * C)).then_inc(sem("kvb_made"), 1)
            dve.wait_ge(sem("kvb_made"), 1)
            for c in range(CH):
                dve.tensor_scalar(wkv_raw[:, c, :], wkv_raw[:, c, :], vecs[:, LAKV + c:LAKV + c + 1], None, ALU.mult)\
                   .then_inc(sem("wkv_scaled"), 1)
            shift_of(dve, 0)
            dve.wait_ge(sem("wkv_hi_made"), CH)
            for c in range(CH):
                dve.tensor_tensor(wkv_lo[:, c, :], wkv_raw[:, c, :], wkv_hi[:, c, :], ALU.subtract)\
                   .then_inc(sem("wkv_lo_made"), 1)
            tile_stats(dve, "class", 0, rows[:, 3 * C:4 * C])
            round_dve(dve, 0, True)
            for n in range(1, NW - 1):
                round_dve(dve, n, False)
            last_round_dve(dve)
            link = Chain(dve, "a0_link")
            dve_end(dve, link)
            phase(dve, 1)
            dve_attention(dve, 0, link)
            phase(dve, 2)
            dve_experts(dve)
            phase(dve, 3)
            dve_attention(dve, 1, Chain(dve, "a1_link"))
            phase(dve, 4)
            dve_lora(dve)


def kernel(**inputs):
    import numpy as np
    import concourse.bacc as bacc
    from concourse.bass_utils import run_bass_kernel_spmd

    a = {k: np.asarray(v) for k, v in inputs.items()}
    cat, tidy = np.concatenate, np.ascontiguousarray
    tok = lambda name: a["L0_tok_" + name]
    x = a["x"][:, :, :126, :126].reshape(P, 3, 3, 3, 14, 3, 3, 14).transpose(2, 5, 1, 4, 7, 3, 6, 0)
    x = x.reshape(NW, 588, NP, P)
    conv = tok("conv_w").reshape(C, 588).T
    arrays = {
        "x_main": x[:, :512].reshape(NW, 4, P, NP, P).transpose(0, 2, 3, 1, 4).reshape(NW * P, NP * 512),
        "x_rest": x[:, 512:].reshape(NW * KREST, NP * P),
        "conv_main": conv[:512].reshape(4, P, C).transpose(1, 0, 2).reshape(P, 4 * C),
        "conv_rest": conv[512:],
        "vecs": np.stack([tok(n) for n in VECS]).reshape(len(VECS), CH, P).transpose(2, 0, 1).reshape(P, -1),
        "rows": cat([tok(n) for n in ROWS])[None],
        "la_wq": tok("la_wq"), "la_wkv": tok("la_wkv"), "la_proj_w": tok("la_proj_w"),
        "ga_wq": tok("ga_wq"), "ga_wkv": tok("ga_wkv"), "ga_proj_w": tok("ga_proj_w"), "mod_w": tok("mod_w"),
        "qkv_w0": cat([a["L0_attn_" + n].T for n in ("Wq", "Wk", "Wv")], axis=1),
        "qkv_b": cat([a["L0_attn_" + n] for n in ("bq", "bk", "bv")])[None],
        "o_w0": a["L0_attn_Wo"].T,
        "qkv_w1": a["L1_attn_Wqkv"].T, "o_w1": a["L1_attn_Wout"].T,
        "router_w": a["L0_ffn_router_w"],
        "w1": a["L0_ffn_w1"].reshape(E, CH, P, FF).transpose(0, 2, 1, 3).reshape(E * P, CH * FF),
        "w2": a["L0_ffn_w2"].reshape(E, FC, P, C).transpose(0, 2, 1, 3).reshape(E * P, FC * C),
        "b1": a["L0_ffn_b1"].reshape(E * FC, P).T,
        "b2": a["L0_ffn_b2"].reshape(1, E * C), "gamma": a["L0_ffn_gamma"].reshape(1, E * C),
        "beta": a["L0_ffn_beta"],
        "z_w": cat([a["L1_ffn_shared_A"], a["L1_ffn_routed_A"].reshape(E6 * R16, C), a["L1_ffn_router_W"]]).T,
        "z_b": cat([a["L1_ffn_shared_B"].T, a["L1_ffn_routed_B"].transpose(0, 2, 1).reshape(E6 * R16, C)]),
        "z_rows": cat([a["L1_ffn_base_b"], a["L1_ffn_router_b"]])[None],
        "base_w": a["L1_ffn_base_W"].T,
    }
    nc = bacc.Bacc("TRN2", target_bir_lowering=False, num_devices=1)
    feed, d = {}, {}
    for name, value in arrays.items():
        feed[f"in_{name}"] = tidy(value)
        d[name] = nc.dram_tensor(f"in_{name}", value.shape, F32, kind="ExternalInput").ap()
    out = nc.dram_tensor("out_h", (P, T, C), F32, kind="ExternalOutput").ap()
    vision_tower(nc, d, out)
    return run_bass_kernel_spmd(nc, [feed], core_ids=[0]).results[0]["out_h"]
```
